# Optimizing a Trainium2 kernel written in Bass

```python
import numpy as np
import jax
import jax.numpy as jnp

def _softmax(x, axis=-1):
    return jax.nn.softmax(x, axis=axis)

def _gelu(x):
    return jax.nn.gelu(x, approximate=True)

def _silu(x):
    return jax.nn.silu(x)

def _sigmoid(x):
    return jax.nn.sigmoid(x)

def _layernorm(x, axis=-1, eps=1e-05):
    m = jnp.mean(x, axis=axis, keepdims=True)
    v = jnp.var(x, axis=axis, keepdims=True)
    return (x - m) / jnp.sqrt(v + eps)

def _scatter_add(tgt, idx, src, axis=0):
    return tgt.at[idx].add(src)

def _segment_sum(src, seg, n):
    return jax.ops.segment_sum(src, seg, n)
kernel_name = 'mk_xattn_ffn_d2_seqx_r8_ea3016'

def setup_inputs(seed: int=0):
    np.random.seed(seed)
    _w = jnp.asarray

    def _rec_inputs():
        import jax
        import jax.numpy as jnp
        _rk = jax.random.key(seed)
        x = 7.22e-05 + 1 * jax.random.normal(jax.random.fold_in(_rk, 1), (16, 64, 256), jnp.float32)
        _lenS = 64 - jax.random.randint(jax.random.fold_in(_rk, 7), (16,), 0, max(1, 64 // 4) + 1, jnp.int32)
        _lenS2 = 64 - jax.random.randint(jax.random.fold_in(_rk, 8), (16,), 0, max(1, 64 // 4) + 1, jnp.int32)
        _ctx_512P = jax.random.normal(jax.random.fold_in(_rk, 11), (16, 16, 64), jnp.float32)
        _ctx_512c = jax.random.dirichlet(jax.random.fold_in(_rk, 511), 0.3 * jnp.ones((16,), jnp.float32), (16, 64))
        _ctx_512t = jnp.einsum('bsk,bkd->bsd', _ctx_512c, _ctx_512P)
        _ctx_512t = _ctx_512t * jax.lax.rsqrt(jnp.mean(jnp.square(_ctx_512t)) + 1e-12) * 0.953939
        ctx_512 = -0.000514642 + 1.00011 * (_ctx_512t + 0.3 * jax.random.normal(jax.random.fold_in(_rk, 611), (16, 64, 64), jnp.float32))
        return (x, ctx_512)
    x, ctx_512 = _rec_inputs()

    def _L0_xattn_setup():
        import jax, jax.numpy as jnp
        import numpy as np
        import math
        NUM_Q_HEADS = 32
        NUM_KV_HEADS = 8
        key = jax.random.key(seed)
        k1, k2, k3 = jax.random.split(key, 3)
        B, S, E = (2, 256, 256)
        kv_E = NUM_KV_HEADS * (E // NUM_Q_HEADS)
        q = jax.random.normal(k1, (B, S, E), dtype=jnp.float32)
        k = jax.random.normal(k2, (B, S, kv_E), dtype=jnp.float32)
        v = jax.random.normal(k3, (B, S, kv_E), dtype=jnp.float32)
        return {'q': q, 'k': k, 'v': v}
    _L0_xattn_all = _L0_xattn_setup()
    _L0_xattn_in = {k: v for k, v in _L0_xattn_all.items() if k in ()}
    del _L0_xattn_all

    def _L0_ffn_setup():
        import jax, jax.numpy as jnp
        import numpy as np
        DIM = 256
        HIDDEN = 1024
        NUM_EXPERTS = 2
        BATCH, SEQ = (4, 128)
        key = jax.random.key(seed)
        k1, k2, k3, k4 = jax.random.split(key, 4)
        x = jax.random.normal(k1, (BATCH, SEQ, DIM), dtype=jnp.float32)
        w_router = jax.random.normal(k2, (NUM_EXPERTS, DIM), dtype=jnp.float32) * (1.0 / np.sqrt(DIM))
        w_fc = jax.random.normal(k3, (NUM_EXPERTS, HIDDEN, DIM), dtype=jnp.float32) * (1.0 / np.sqrt(DIM))
        w_proj = jax.random.normal(k4, (NUM_EXPERTS, DIM, HIDDEN), dtype=jnp.float32) * (1.0 / np.sqrt(HIDDEN))
        return {'x': x, 'w_router': w_router, 'w_fc': w_fc, 'w_proj': w_proj}
    _L0_ffn_all = _L0_ffn_setup()
    _L0_ffn_in = {k: v for k, v in _L0_ffn_all.items() if k in ('w_router', 'w_fc', 'w_proj')}
    del _L0_ffn_all

    def _L1_xattn_setup():
        import jax, jax.numpy as jnp
        import numpy as np
        B, S, H, NH, L = (2, 256, 256, 16, 64)
        HD = H // NH
        key = jax.random.key(seed)
        k1, k2, k3, k4, k5 = jax.random.split(key, 5)
        scale = 0.02
        return {'q': jax.random.normal(k1, (B, S, H), dtype=jnp.float32), 'latent_kv': jax.random.normal(k2, (B, S, L), dtype=jnp.float32), 'Wq': jax.random.normal(k3, (H, H), dtype=jnp.float32) * scale, 'Wkv_expand': jax.random.normal(k4, (2 * H, L), dtype=jnp.float32) * scale, 'Wout': jax.random.normal(k5, (H, H), dtype=jnp.float32) * scale}
    _L1_xattn_all = _L1_xattn_setup()
    _L1_xattn_in = {k: v for k, v in _L1_xattn_all.items() if k in ('Wq', 'Wkv_expand', 'Wout')}
    del _L1_xattn_all

    def _L1_ffn_setup():
        import jax, jax.numpy as jnp
        import numpy as np
        COST_LAMBDA = 1e-07
        HID = [128, 256, 384, 512, 128, 256, 384, 512]
        TOP_K = 2

        def _gelu(v):
            return jax.nn.gelu(v, approximate=False)

        def _forward(x, down_w, down_b, up_w, up_b, router_w, router_b, shared_w1, shared_b1, shared_w2, shared_b2, core_w, core_b, expert_params):
            E = len(expert_params)
            h = x @ down_w + down_b
            cost = jnp.array([w1.shape[0] * w1.shape[1] + w2.shape[0] * w2.shape[1] for w1, _, w2, _ in expert_params], jnp.float32)
            logits = x @ router_w + router_b - COST_LAMBDA * cost
            probs = jax.nn.softmax(logits, axis=-1)
            topv, topi = jax.lax.top_k(probs, TOP_K)
            gate = jax.nn.softmax(topv, axis=-1)
            out = jnp.zeros_like(h)
            for k in range(TOP_K):
                mask = jax.nn.one_hot(topi[..., k], E, dtype=h.dtype)
                acc = jnp.zeros_like(h)
                for e, (w1, b1, w2, b2) in enumerate(expert_params):
                    hm = h * mask[..., e:e + 1]
                    acc = acc + (_gelu(_gelu(hm) @ w1 + b1) @ w2 + b2)
                out = out + acc * gate[..., k:k + 1]
            out = out + 0.1 * (_gelu(_gelu(h) @ shared_w1 + shared_b1) @ shared_w2 + shared_b2)
            out = out @ up_w + up_b
            out = out + (_gelu(x) @ core_w + core_b)
            return out
        key = jax.random.key(seed)
        ks = iter(jax.random.split(key, 80))

        def W(shape):
            return jax.random.normal(next(ks), shape, jnp.float32) * 0.02
        B, T, D, L = (4, 256, 256, 128)
        inp = {'x': jax.random.normal(next(ks), (B, T, D), jnp.float32)}
        inp['down_w'] = W((D, L))
        inp['down_b'] = jnp.zeros((L,), jnp.float32)
        inp['up_w'] = W((L, D))
        inp['up_b'] = jnp.zeros((D,), jnp.float32)
        inp['router_w'] = W((D, len(HID)))
        inp['router_b'] = jnp.zeros((len(HID),), jnp.float32)
        inp['shared_w1'] = W((L, L))
        inp['shared_b1'] = jnp.zeros((L,), jnp.float32)
        inp['shared_w2'] = W((L, L))
        inp['shared_b2'] = jnp.zeros((L,), jnp.float32)
        inp['core_w'] = W((D, D))
        inp['core_b'] = jnp.zeros((D,), jnp.float32)
        for e, h in enumerate(HID):
            inp[f'e{e}_w1'] = W((L, h))
            inp[f'e{e}_b1'] = jnp.zeros((h,), jnp.float32)
            inp[f'e{e}_w2'] = W((h, L))
            inp[f'e{e}_b2'] = jnp.zeros((L,), jnp.float32)
        return inp
    _L1_ffn_all = _L1_ffn_setup()
    _L1_ffn_in = {k: v for k, v in _L1_ffn_all.items() if k in ('down_w', 'down_b', 'up_w', 'up_b', 'router_w', 'router_b', 'shared_w1', 'shared_b1', 'shared_w2', 'shared_b2', 'core_w', 'core_b', 'e0_w1', 'e0_b1', 'e0_w2', 'e0_b2', 'e1_w1', 'e1_b1', 'e1_w2', 'e1_b2', 'e2_w1', 'e2_b1', 'e2_w2', 'e2_b2', 'e3_w1', 'e3_b1', 'e3_w2', 'e3_b2', 'e4_w1', 'e4_b1', 'e4_w2', 'e4_b2', 'e5_w1', 'e5_b1', 'e5_w2', 'e5_b2', 'e6_w1', 'e6_b1', 'e6_w2', 'e6_b2', 'e7_w1', 'e7_b1', 'e7_w2', 'e7_b2')}
    del _L1_ffn_all
    return {'x': x, 'ctx_512': ctx_512, 'L0_ffn_w_router': _L0_ffn_in['w_router'], 'L0_ffn_w_fc': _L0_ffn_in['w_fc'], 'L0_ffn_w_proj': _L0_ffn_in['w_proj'], 'L1_xattn_Wq': _L1_xattn_in['Wq'], 'L1_xattn_Wkv_expand': _L1_xattn_in['Wkv_expand'], 'L1_xattn_Wout': _L1_xattn_in['Wout'], 'L1_ffn_down_w': _L1_ffn_in['down_w'], 'L1_ffn_down_b': _L1_ffn_in['down_b'], 'L1_ffn_up_w': _L1_ffn_in['up_w'], 'L1_ffn_up_b': _L1_ffn_in['up_b'], 'L1_ffn_router_w': _L1_ffn_in['router_w'], 'L1_ffn_router_b': _L1_ffn_in['router_b'], 'L1_ffn_shared_w1': _L1_ffn_in['shared_w1'], 'L1_ffn_shared_b1': _L1_ffn_in['shared_b1'], 'L1_ffn_shared_w2': _L1_ffn_in['shared_w2'], 'L1_ffn_shared_b2': _L1_ffn_in['shared_b2'], 'L1_ffn_core_w': _L1_ffn_in['core_w'], 'L1_ffn_core_b': _L1_ffn_in['core_b'], 'L1_ffn_e0_w1': _L1_ffn_in['e0_w1'], 'L1_ffn_e0_b1': _L1_ffn_in['e0_b1'], 'L1_ffn_e0_w2': _L1_ffn_in['e0_w2'], 'L1_ffn_e0_b2': _L1_ffn_in['e0_b2'], 'L1_ffn_e1_w1': _L1_ffn_in['e1_w1'], 'L1_ffn_e1_b1': _L1_ffn_in['e1_b1'], 'L1_ffn_e1_w2': _L1_ffn_in['e1_w2'], 'L1_ffn_e1_b2': _L1_ffn_in['e1_b2'], 'L1_ffn_e2_w1': _L1_ffn_in['e2_w1'], 'L1_ffn_e2_b1': _L1_ffn_in['e2_b1'], 'L1_ffn_e2_w2': _L1_ffn_in['e2_w2'], 'L1_ffn_e2_b2': _L1_ffn_in['e2_b2'], 'L1_ffn_e3_w1': _L1_ffn_in['e3_w1'], 'L1_ffn_e3_b1': _L1_ffn_in['e3_b1'], 'L1_ffn_e3_w2': _L1_ffn_in['e3_w2'], 'L1_ffn_e3_b2': _L1_ffn_in['e3_b2'], 'L1_ffn_e4_w1': _L1_ffn_in['e4_w1'], 'L1_ffn_e4_b1': _L1_ffn_in['e4_b1'], 'L1_ffn_e4_w2': _L1_ffn_in['e4_w2'], 'L1_ffn_e4_b2': _L1_ffn_in['e4_b2'], 'L1_ffn_e5_w1': _L1_ffn_in['e5_w1'], 'L1_ffn_e5_b1': _L1_ffn_in['e5_b1'], 'L1_ffn_e5_w2': _L1_ffn_in['e5_w2'], 'L1_ffn_e5_b2': _L1_ffn_in['e5_b2'], 'L1_ffn_e6_w1': _L1_ffn_in['e6_w1'], 'L1_ffn_e6_b1': _L1_ffn_in['e6_b1'], 'L1_ffn_e6_w2': _L1_ffn_in['e6_w2'], 'L1_ffn_e6_b2': _L1_ffn_in['e6_b2'], 'L1_ffn_e7_w1': _L1_ffn_in['e7_w1'], 'L1_ffn_e7_b1': _L1_ffn_in['e7_b1'], 'L1_ffn_e7_w2': _L1_ffn_in['e7_w2'], 'L1_ffn_e7_b2': _L1_ffn_in['e7_b2']}

def reference(x, ctx_512, L0_ffn_w_router, L0_ffn_w_fc, L0_ffn_w_proj, L1_xattn_Wq, L1_xattn_Wkv_expand, L1_xattn_Wout, L1_ffn_down_w, L1_ffn_down_b, L1_ffn_up_w, L1_ffn_up_b, L1_ffn_router_w, L1_ffn_router_b, L1_ffn_shared_w1, L1_ffn_shared_b1, L1_ffn_shared_w2, L1_ffn_shared_b2, L1_ffn_core_w, L1_ffn_core_b, L1_ffn_e0_w1, L1_ffn_e0_b1, L1_ffn_e0_w2, L1_ffn_e0_b2, L1_ffn_e1_w1, L1_ffn_e1_b1, L1_ffn_e1_w2, L1_ffn_e1_b2, L1_ffn_e2_w1, L1_ffn_e2_b1, L1_ffn_e2_w2, L1_ffn_e2_b2, L1_ffn_e3_w1, L1_ffn_e3_b1, L1_ffn_e3_w2, L1_ffn_e3_b2, L1_ffn_e4_w1, L1_ffn_e4_b1, L1_ffn_e4_w2, L1_ffn_e4_b2, L1_ffn_e5_w1, L1_ffn_e5_b1, L1_ffn_e5_w2, L1_ffn_e5_b2, L1_ffn_e6_w1, L1_ffn_e6_b1, L1_ffn_e6_w2, L1_ffn_e6_b2, L1_ffn_e7_w1, L1_ffn_e7_b1, L1_ffn_e7_w2, L1_ffn_e7_b2):
    import jax
    import jax.numpy as jnp

    def _L0_xattn_ref(q, k, v):
        import jax, jax.numpy as jnp
        import numpy as np
        import math
        NUM_Q_HEADS = 32
        NUM_KV_HEADS = 8
        B, S, E = q.shape
        H, KV = (NUM_Q_HEADS, NUM_KV_HEADS)
        D = E // H
        G = H // KV
        scale = math.sqrt(D)
        qh = q.reshape(B, S, KV, G, D).transpose(0, 2, 3, 1, 4)
        kh = k.reshape(B, S, KV, D).transpose(0, 2, 1, 3)
        vh = v.reshape(B, S, KV, D).transpose(0, 2, 1, 3)
        scores = jnp.einsum('bkgsd,bktd->bkgst', qh, kh) / scale
        weights = jax.nn.softmax(scores, axis=-1)
        out = jnp.einsum('bkgst,bktd->bkgsd', weights, vh)
        return out.transpose(0, 3, 1, 2, 4).reshape(B, S, E)

    def _L0_ffn_ref(x, w_router, w_fc, w_proj):
        import jax, jax.numpy as jnp
        import numpy as np
        DIM = 256
        HIDDEN = 1024
        NUM_EXPERTS = 2
        BATCH, SEQ = (4, 128)
        bsz, seq, dim = x.shape
        num_experts = w_router.shape[0]
        x_flat = x.reshape(-1, dim)
        logits = x_flat @ w_router.T
        probs = jax.nn.softmax(logits, axis=-1)
        top_idx = jnp.argmax(probs, axis=-1)
        top_weight = jnp.take_along_axis(probs, top_idx[:, None], axis=1)[:, 0]
        h = jnp.einsum('nd,ehd->enh', x_flat, w_fc)
        a = jnp.square(jnp.where(h >= 0, h, 0.5 * h))
        expert_out = jnp.einsum('enh,edh->end', a, w_proj)
        mask = (top_idx[None, :] == jnp.arange(num_experts)[:, None]).astype(x.dtype)
        out = jnp.einsum('end,en->nd', expert_out, mask * top_weight[None, :])
        return out.reshape(bsz, seq, dim)

    def _L1_xattn_ref(q, latent_kv, Wq, Wkv_expand, Wout):
        import jax, jax.numpy as jnp
        import numpy as np
        B, S, H, NH, L = (2, 256, 256, 16, 64)
        HD = H // NH
        b, sq, _ = q.shape
        sk = latent_kv.shape[1]
        qp = q @ Wq.T
        kv = latent_kv @ Wkv_expand.T
        k, v = jnp.split(kv, 2, axis=-1)
        qh = qp.reshape(b, sq, NH, HD).transpose(0, 2, 1, 3)
        kh = k.reshape(b, sk, NH, HD).transpose(0, 2, 1, 3)
        vh = v.reshape(b, sk, NH, HD).transpose(0, 2, 1, 3)
        inv_sqrt_d = 1.0 / jnp.sqrt(jnp.float32(HD))
        scores = jnp.einsum('bhqd,bhkd->bhqk', qh, kh) * inv_sqrt_d
        causal = jnp.tril(jnp.ones((sq, sk), dtype=bool))
        scores = jnp.where(causal, scores, jnp.finfo(scores.dtype).min)
        attn = jax.nn.softmax(scores, axis=-1)
        out = jnp.einsum('bhqk,bhkd->bhqd', attn, vh)
        out = out.transpose(0, 2, 1, 3).reshape(b, sq, H)
        return out @ Wout.T

    def _L1_ffn_ref(x, down_w, down_b, up_w, up_b, router_w, router_b, shared_w1, shared_b1, shared_w2, shared_b2, core_w, core_b, e0_w1, e0_b1, e0_w2, e0_b2, e1_w1, e1_b1, e1_w2, e1_b2, e2_w1, e2_b1, e2_w2, e2_b2, e3_w1, e3_b1, e3_w2, e3_b2, e4_w1, e4_b1, e4_w2, e4_b2, e5_w1, e5_b1, e5_w2, e5_b2, e6_w1, e6_b1, e6_w2, e6_b2, e7_w1, e7_b1, e7_w2, e7_b2):
        import jax, jax.numpy as jnp
        import numpy as np
        COST_LAMBDA = 1e-07
        HID = [128, 256, 384, 512, 128, 256, 384, 512]
        TOP_K = 2

        def _gelu(v):
            return jax.nn.gelu(v, approximate=False)

        def _forward(x, down_w, down_b, up_w, up_b, router_w, router_b, shared_w1, shared_b1, shared_w2, shared_b2, core_w, core_b, expert_params):
            E = len(expert_params)
            h = x @ down_w + down_b
            cost = jnp.array([w1.shape[0] * w1.shape[1] + w2.shape[0] * w2.shape[1] for w1, _, w2, _ in expert_params], jnp.float32)
            logits = x @ router_w + router_b - COST_LAMBDA * cost
            probs = jax.nn.softmax(logits, axis=-1)
            topv, topi = jax.lax.top_k(probs, TOP_K)
            gate = jax.nn.softmax(topv, axis=-1)
            out = jnp.zeros_like(h)
            for k in range(TOP_K):
                mask = jax.nn.one_hot(topi[..., k], E, dtype=h.dtype)
                acc = jnp.zeros_like(h)
                for e, (w1, b1, w2, b2) in enumerate(expert_params):
                    hm = h * mask[..., e:e + 1]
                    acc = acc + (_gelu(_gelu(hm) @ w1 + b1) @ w2 + b2)
                out = out + acc * gate[..., k:k + 1]
            out = out + 0.1 * (_gelu(_gelu(h) @ shared_w1 + shared_b1) @ shared_w2 + shared_b2)
            out = out @ up_w + up_b
            out = out + (_gelu(x) @ core_w + core_b)
            return out
        ep = [(e0_w1, e0_b1, e0_w2, e0_b2), (e1_w1, e1_b1, e1_w2, e1_b2), (e2_w1, e2_b1, e2_w2, e2_b2), (e3_w1, e3_b1, e3_w2, e3_b2), (e4_w1, e4_b1, e4_w2, e4_b2), (e5_w1, e5_b1, e5_w2, e5_b2), (e6_w1, e6_b1, e6_w2, e6_b2), (e7_w1, e7_b1, e7_w2, e7_b2)]
        return _forward(x, down_w, down_b, up_w, up_b, router_w, router_b, shared_w1, shared_b1, shared_w2, shared_b2, core_w, core_b, ep)
    x = x + _L0_xattn_ref(_layernorm(x, axis=-1), ctx_512, ctx_512)
    x = x + _L0_ffn_ref(_layernorm(x, axis=-1), L0_ffn_w_router, L0_ffn_w_fc, L0_ffn_w_proj)
    x = x + _L1_xattn_ref(_layernorm(x, axis=-1), ctx_512, L1_xattn_Wq, L1_xattn_Wkv_expand, L1_xattn_Wout)
    x = x + _L1_ffn_ref(_layernorm(x, axis=-1), L1_ffn_down_w, L1_ffn_down_b, L1_ffn_up_w, L1_ffn_up_b, L1_ffn_router_w, L1_ffn_router_b, L1_ffn_shared_w1, L1_ffn_shared_b1, L1_ffn_shared_w2, L1_ffn_shared_b2, L1_ffn_core_w, L1_ffn_core_b, L1_ffn_e0_w1, L1_ffn_e0_b1, L1_ffn_e0_w2, L1_ffn_e0_b2, L1_ffn_e1_w1, L1_ffn_e1_b1, L1_ffn_e1_w2, L1_ffn_e1_b2, L1_ffn_e2_w1, L1_ffn_e2_b1, L1_ffn_e2_w2, L1_ffn_e2_b2, L1_ffn_e3_w1, L1_ffn_e3_b1, L1_ffn_e3_w2, L1_ffn_e3_b2, L1_ffn_e4_w1, L1_ffn_e4_b1, L1_ffn_e4_w2, L1_ffn_e4_b2, L1_ffn_e5_w1, L1_ffn_e5_b1, L1_ffn_e5_w2, L1_ffn_e5_b2, L1_ffn_e6_w1, L1_ffn_e6_b1, L1_ffn_e6_w2, L1_ffn_e6_b2, L1_ffn_e7_w1, L1_ffn_e7_b1, L1_ffn_e7_w2, L1_ffn_e7_b2)
    return x

_drawn_inputs = setup_inputs


def setup_inputs(seed=0):
    import zlib

    import numpy as np

    out = dict(_drawn_inputs(seed))
    spreads = {'L1_ffn_down_b': (0.0, 0.8),
     'L1_ffn_up_b': (0.0, 0.1),
     'L1_ffn_router_b': (0.0, 0.8),
     'L1_ffn_shared_b1': (0.0, 0.8),
     'L1_ffn_shared_b2': (0.0, 0.8),
     'L1_ffn_core_b': (0.0, 0.1),
     'L1_ffn_e0_b1': (0.0, 0.8),
     'L1_ffn_e0_b2': (0.0, 0.579),
     'L1_ffn_e1_b1': (0.0, 0.8),
     'L1_ffn_e1_b2': (0.0, 0.599),
     'L1_ffn_e2_b1': (0.0, 0.8),
     'L1_ffn_e2_b2': (0.0, 0.592),
     'L1_ffn_e3_b1': (0.0, 0.8),
     'L1_ffn_e3_b2': (0.0, 0.616),
     'L1_ffn_e4_b1': (0.0, 0.8),
     'L1_ffn_e4_b2': (0.0, 0.56),
     'L1_ffn_e5_b1': (0.0, 0.8),
     'L1_ffn_e5_b2': (0.0, 0.598),
     'L1_ffn_e6_b1': (0.0, 0.8),
     'L1_ffn_e6_b2': (0.0, 0.531),
     'L1_ffn_e7_b1': (0.0, 0.8),
     'L1_ffn_e7_b2': (0.0, 0.576)}
    factors = {'L1_xattn_Wq': 8.0,
     'L1_xattn_Wkv_expand': 3.37,
     'L1_xattn_Wout': 3.412,
     'L1_ffn_down_w': 8.0,
     'L1_ffn_router_w': 8.0,
     'L1_ffn_shared_w1': 8.0,
     'L1_ffn_shared_w2': 8.0,
     'L1_ffn_e0_w1': 8.0,
     'L1_ffn_e0_w2': 8.0,
     'L1_ffn_e1_w1': 8.0,
     'L1_ffn_e1_w2': 8.0,
     'L1_ffn_e2_w1': 8.0,
     'L1_ffn_e2_w2': 8.0,
     'L1_ffn_e3_w1': 8.0,
     'L1_ffn_e3_w2': 8.0,
     'L1_ffn_e4_w1': 8.0,
     'L1_ffn_e4_w2': 8.0,
     'L1_ffn_e5_w1': 8.0,
     'L1_ffn_e5_w2': 8.0,
     'L1_ffn_e6_w1': 8.0,
     'L1_ffn_e6_w2': 8.0,
     'L1_ffn_e7_w1': 8.0,
     'L1_ffn_e7_w2': 8.0}
    for name, (base, spread) in spreads.items():
        noise = np.random.default_rng([zlib.crc32(name.encode()), seed]).standard_normal(out[name].shape)
        drawn = base * np.exp(spread * noise) if base else spread * noise
        out[name] = jnp.asarray(drawn.astype(out[name].dtype))
    for name, factor in factors.items():
        out[name] = (out[name] * factor).astype(out[name].dtype)
    return out
```

```python
import concourse.bass as bass
from concourse import mybir
from contextlib import ExitStack

fp32 = mybir.dt.float32
bf16 = mybir.dt.bfloat16
u32 = mybir.dt.uint32
ALU = mybir.AluOpType
ACT = mybir.ActivationFunctionType
AX = mybir.AxisListType

P = 128
B, S, D = 16, 64, 256
TILES = B * S // P
GROUPS = TILES // 2
GT = 2 * P
DC = D // P
CTX = 64
NH0, NKV0, HD0 = 32, 8, 8
NH1, HD1 = 16, 16
E0, HID0 = 2, 1024
K0 = HID0 // P
L = 128
HIDS = [128, 256, 384, 512, 128, 256, 384, 512]
E1 = len(HIDS)
CH1 = [h // P for h in HIDS] + [1]
FIRST1 = [sum(CH1[:e]) for e in range(E1 + 1)]
NCH1 = sum(CH1)
EPS = 1e-5
MASKED = -3.0e38
PARTS = 3
SLOTS = 6


def mixed_network(nc: bass.Bass, x, ctx_in, ctxT, wr0, wf0, wp0, wq1, wkv1, wo1, down_w, down_b,
                  up_w, bias_rows, router_w, router_rows, core_w, w1, b1, w2, b2, out):
    ctx = ExitStack()
    with ctx:
        def sb(name, shape, dt):
            return ctx.enter_context(nc.sbuf_tensor(name, shape, dt))

        def ps(name, shape, dt):
            return ctx.enter_context(nc.psum_tensor(name, shape, dt))

        def sem(name):
            return ctx.enter_context(nc.semaphore(name))

        X = sb("X", [P, TILES, D], fp32)
        C = sb("C", [P, TILES, CTX], fp32)
        CT = sb("CT", [CTX, B * S], fp32)
        CD = sb("CD", [P, B, CTX], fp32)
        WR0 = sb("WR0", [P, DC, E0], fp32)
        WF0 = sb("WF0", [P, E0, DC, HID0], fp32)
        WP0 = sb("WP0", [P, E0, K0, D], fp32)
        WQ1 = sb("WQ1", [P, DC, D], fp32)
        WKV1 = sb("WKV1", [CTX, 2 * D], fp32)
        WO1 = sb("WO1", [P, DC, D], fp32)
        DW = sb("DW", [P, DC, L], fp32)
        DB = sb("DB", [P, 1], fp32)
        UW = sb("UW", [P, D], fp32)
        BR = sb("BR", [P, 2, D], fp32)
        RW = sb("RW", [P, DC, E1], fp32)
        RR = sb("RR", [P, 2, E1], fp32)
        CW = sb("CW", [P, DC, D], fp32)
        W1 = sb("W1", [P, NCH1, P], fp32)
        B1 = sb("B1", [P, NCH1], fp32)
        W2 = sb("W2", [P, NCH1, L], fp32)
        B2 = sb("B2", [P, E1 + 1], fp32)

        identf = sb("identf", [P, P], fp32)
        identb = sb("identb", [P, P], bf16)
        maskS = sb("maskS", [P, S], bf16)
        maskT = sb("maskT", [P, S], bf16)
        sel0 = sb("sel0", [64, NKV0, 2, S], bf16)
        sel1 = sb("sel1", [64, NH1, S], bf16)
        selG = sb("selG", [32, E1, P], bf16)
        iota8 = sb("iota8", [P, E1], fp32)
        mhalf = sb("mhalf", [P, 2], fp32)
        rbias = sb("rbias", [P, E1], fp32)
        obias = sb("obias", [P, D], fp32)
        GB1 = sb("GB1", [P, NCH1], fp32)
        Y0n = sb("Y0n", [P, E1], fp32)
        Cb = sb("Cb", [P, 1], fp32)

        stats = sb("stats", [P, 2, 6], fp32)
        mv = sb("mv", [P, 2, 2], fp32)
        vare = sb("vare", [P, 2], fp32)
        rstd = sb("rstd", [P, 2], fp32)
        Q = sb("Q", [P, D], fp32)
        QR = sb("QR", [P, D], fp32)
        QS = sb("QS", [P, NH0, 64], bf16)
        KR = sb("KR", [P, CTX], fp32)
        KS = sb("KS", [P, NKV0, 64], bf16)
        QT = sb("QT", [P, NH0 // 2, P], bf16)
        K2 = sb("K2", [P, NKV0, 2, 2, S], bf16)
        MN = sb("MN", [P, NH0], fp32)
        MR = sb("MR", [P, NH0], fp32)
        MS = sb("MS", [P, 2, 4, 2, NKV0], bf16)
        MT = sb("MT", [64, 2, P], bf16)
        PT = sb("PT", [P, NKV0, 2, P], fp32)
        V2 = sb("V2", [P, B, NKV0, 2, 16], fp32)
        OT = sb("OT", [P, 4, P], fp32)
        rec0 = sb("rec0", [P, NH0], fp32)
        O0 = sb("O0", [P, D], fp32)

        XA = sb("XA", [P, D], fp32)
        XAT = sb("XAT", [P, DC, P], fp32)
        Q1 = sb("Q1", [P, D], fp32)
        QR1 = sb("QR1", [P, D], fp32)
        QS1 = sb("QS1", [P, NH1, SLOTS, HD1], bf16)
        K1 = sb("K1", [P, D], fp32)
        KR1 = sb("KR1", [P, D], fp32)
        KS1 = sb("KS1", [P, NH1, SLOTS, HD1], bf16)
        V1 = sb("V1", [P, NH1, 32], fp32)
        QT1 = sb("QT1", [SLOTS * HD1, NH1, P], bf16)
        KT1 = sb("KT1", [SLOTS * HD1, NH1, P], bf16)
        MN1 = sb("MN1", [P, NH1], fp32)
        MR1 = sb("MR1", [P, NH1], fp32)
        MS1 = sb("MS1", [P, 4, NH1], bf16)
        MT1 = sb("MT1", [64, P], bf16)
        PT1 = sb("PT1", [P, NH1, S], fp32)
        OT1 = sb("OT1", [P, 4, P], fp32)
        rec1 = sb("rec1", [P, NH1], fp32)
        O1 = sb("O1", [P, D], fp32)
        O1T = sb("O1T", [P, DC, P], fp32)

        XN = sb("XN", [P, 2, D], fp32)
        XT = sb("XT", [P, DC, GT], fp32)
        lg = sb("lg", [P, 2, E1], fp32)
        pr = sb("pr", [P, 2, E1], fp32)
        lmax = sb("lmax", [P, 2], fp32)
        lsum = sb("lsum", [P, 2], fp32)
        G0 = sb("G0", [P, 2, E0], fp32)
        HH = sb("HH", [P, 2, 512], fp32)
        R0 = sb("R0", [P, 2, 512], fp32)
        A0 = sb("A0", [P, 2, 2, GT], fp32)
        top = sb("top", [P, 2, 8], fp32)
        topi = sb("topi", [P, 2, 8], u32)
        topf = sb("topf", [P, 2, 8], fp32)
        dlt = sb("dlt", [P, 2], fp32)
        ge = sb("ge", [P, 2], fp32)
        gk = sb("gk", [P, 2, 2], fp32)
        oh = sb("oh", [P, 2, E1], fp32)
        gate = sb("gate", [P, 2, E1], fp32)
        GR = sb("GR", [P, 2, E1], fp32)
        GS = sb("GS", [P, 2, 4, E1], bf16)
        GTT = sb("GTT", [32, GT], bf16)
        GX = sb("GX", [P, DC, GT], fp32)
        GH = sb("GH", [P, GT], fp32)
        A1 = sb("A1", [P, 2, GT], fp32)
        YS = sb("YS", [P, 2, GT], fp32)
        YG = sb("YG", [P, GT], fp32)
        ACC = sb("ACC", [P, GT], fp32)

        AB = ps("AB", [P, 1024], fp32)
        TB = ps("TB", [P, 512], fp32)
        PX = ps("PX", [P, 512], fp32)
        H = [ps(f"H{i}", [P, 512], fp32) for i in range(2)]
        Y = [ps(f"Y{i}", [P, 512], fp32) for i in range(2)]
        ABb = AB[:, :].bitcast(bf16)
        TBb = TB[:, :].bitcast(bf16)
        PXb = PX[:, :].bitcast(bf16)

        order = []
        for g in range(GROUPS):
            order += [("attn0", 2 * g), ("attn0", 2 * g + 1), ("ffn0", g),
                      ("attn1", 2 * g), ("attn1", 2 * g + 1), ("ffn1", g)]

        STAGES = {
            "attn0": [("AB", "q"), ("AB", "k"), ("AB", "s0"), ("AB", "s1"), ("TB", "m"), ("AB", "p0"), ("AB", "p1"),
                      ("TB", "o"), ("TB", "n")],
            "attn1": [("TB", "x"), ("TB", "w"), ("TB", "kv"), ("AB", "q"), ("AB", "k"), ("AB", "s"), ("TB", "m"),
                      ("AB", "p"), ("AB", "o"), ("TB", "n"), ("TB", "a"), ("TB", "r")],
            "ffn0": [("PX", "x"), ("PX", "r")] + [("H", i) for i in range(E0 * K0 // 2)] + [("Y", 0), ("Y", 1)],
            "ffn1": [("PX", "x"), ("PX", "r"), ("PX", "g"), ("PX", "d")] + [("H", i) for i in range(NCH1)]
                    + [("Y", e) for e in range(E1 + 1)] + [("Y", "u0"), ("Y", "u1")],
        }
        uses, count = {}, {"AB": 0, "TB": 0, "PX": 0, "H": 0, "Y": 0}
        for part, n in order:
            for buf, stage in STAGES[part]:
                uses[buf, part, n, stage] = count[buf]
                count[buf] += 1
        depth = {"AB": 1, "TB": 1, "PX": 1, "H": 2, "Y": 2}
        full = {b: sem(f"{b}_full") for b in depth}
        free = {b: sem(f"{b}_free") for b in depth}

        def claim(eng, buf, *key):
            u = uses[(buf, *key)]
            if u >= depth[buf]:
                eng.wait_ge(free[buf], u - depth[buf] + 1)
            return u

        def filled(eng, buf, *key):
            u = uses[(buf, *key)]
            eng.wait_ge(full[buf], u + 1)
            return u

        def read_out(eng, buf, *key):
            eng.wait_ge(free[buf], uses[(buf, *key)] + 1)

        ld_x = [sem(f"ld_x{t}") for t in range(TILES)]
        ld_c = sem("ld_c")
        ld_cd = sem("ld_cd")
        ld_ct = sem("ld_ct")
        ld_f0 = sem("ld_f0")
        ld_p0 = sem("ld_p0")
        ld_a1 = sem("ld_a1")
        ld_w1 = sem("ld_w1")
        ld_w2 = sem("ld_w2")
        ld_d = sem("ld_d")
        pool_const = sem("pool_const")
        v2_ready = sem("v2_ready")
        zeroed = sem("zeroed")
        var_ready = sem("var_ready")
        rstd_ready = sem("rstd_ready")
        qs_ready = sem("qs_ready")
        ks_ready = sem("ks_ready")
        ms_ready = sem("ms_ready")
        x1_ready = sem("x1_ready")
        xa_ready = sem("xa_ready")
        v1_ready = sem("v1_ready")
        qs1_ready = sem("qs1_ready")
        ks1_ready = sem("ks1_ready")
        ms1_ready = sem("ms1_ready")
        o1_ready = sem("o1_ready")
        xn_ready = sem("xn_ready")
        z_ready = sem("z_ready")
        e_ready = sem("e_ready")
        half_ready = sem("half_ready")
        a0_ready = sem("a0_ready")
        a0_used = sem("a0_used")
        a1_used = sem("a1_used")
        dlt_ready = sem("dlt_ready")
        ge_ready = sem("ge_ready")
        gs_ready = sem("gs_ready")
        gx_ready = sem("gx_ready")
        gb1_ready = sem("gb1_ready")
        y0_full = sem("y0_full")
        y0_ready = sem("y0_ready")
        obias_ready = sem("obias_ready")
        ys_ready = sem("ys_ready")
        acc0_ready = sem("acc0_ready")
        acc_ready = sem("acc_ready")
        stored = sem("stored")
        dve_step = sem("dve_step")
        pool_step = sem("pool_step")

        def chain(eng, step):
            done = [0]

            def link(ins):
                done[0] += 1
                ins.then_inc(step, 1)
                eng.wait_ge(step, done[0])
            return link

        EXPERTS = [E1] + list(range(E1))
        WORK = [(e, c) for e in EXPERTS for c in range(CH1[e])]
        BLOCKS0 = E0 * K0 // 2

        def expert_at(e):
            return EXPERTS.index(e)

        def block_used(eng, n):
            g, i = divmod(n, BLOCKS0)
            if i == BLOCKS0 - 1:
                filled(eng, "Y", "ffn0", g, 1)
            else:
                eng.wait_ge(a0_used, g * (BLOCKS0 - 1) + i + 1)

        def chunk_used(eng, n):
            g, i = divmod(n, NCH1)
            e, c = WORK[i]
            if c == CH1[e] - 1:
                filled(eng, "Y", "ffn1", g, expert_at(e))
            else:
                inner = [k for k, (e, c) in enumerate(WORK) if c < CH1[e] - 1]
                eng.wait_ge(a1_used, g * len(inner) + inner.index(i) + 1)

        ln_index = {}
        for part, n in order:
            ln_index[part, n] = len(ln_index)

        block = ctx.enter_context(nc.Block())

        @block.sync
        def _(sp):
            for t in range(TILES):
                sp.dma_start(X[:, t, :], x[t * P:(t + 1) * P, :]).then_inc(ld_x[t], 16)
                if t == 0:
                    sp.dma_start(C[:, :, :], ctx_in.rearrange("(t p) d -> p t d", p=P)).then_inc(ld_c, 16)
                    for half in range(2):
                        sp.dma_start(CD[half * S:(half + 1) * S, :, :],
                                     ctx_in.rearrange("(b s) d -> s b d", s=S)).then_inc(ld_cd, 16)
            sp.dma_start(WR0[:, :, :], wr0).then_inc(ld_f0, 16)
            for e in range(E0):
                sp.dma_start(WF0[:, e, :, :], wf0[:, e, :, :]).then_inc(ld_f0, 16)
                sp.dma_start(WP0[:, e, :, :], wp0[:, e, :, :]).then_inc(ld_p0, 16)
            sp.dma_start(CT[:, :], ctxT).then_inc(ld_ct, 16)
            sp.dma_start(WKV1[:, :], wkv1).then_inc(ld_a1, 16)
            sp.dma_start(WQ1[:, :, :], wq1).then_inc(ld_a1, 16)
            sp.dma_start(WO1[:, :, :], wo1).then_inc(ld_a1, 16)
            sp.dma_start(W1[:, :, :], w1).then_inc(ld_w1, 16)
            sp.dma_start(W2[:, :, :], w2).then_inc(ld_w2, 16)
            for t in range(TILES):
                read_out(sp, "Y", "ffn1", t // 2, f"u{t % 2}")
                sp.dma_start(out[t * P:(t + 1) * P, :], X[:, t, :]).then_inc(stored, 16)
            sp.wait_ge(stored, 16 * TILES)

        N_SMALL = 9

        @block.scalar
        def _(act):
            for dst, src in ((DW[:, :, :], down_w), (DB[:, :], down_b), (UW[:, :], up_w), (BR[:, :, :], bias_rows),
                             (RW[:, :, :], router_w), (RR[:, :, :], router_rows), (CW[:, :, :], core_w),
                             (B1[:, :], b1), (B2[:, :], b2)):
                act.dma_start(dst, src).then_inc(ld_d, 16)

            def attn0(t):
                key = ("attn0", t)
                filled(act, "AB", *key, "q")
                nc.scalar.copy(QT[:, :, :], ABb[:, 0:2048].rearrange("p (n c) -> p n c", c=P)).then_inc(free["AB"], 1)
                filled(act, "TB", *key, "m")
                nc.scalar.copy(MT[:, :, :], TBb[0:64, 0:256].rearrange("p (n c) -> p n c", c=P)).then_inc(free["TB"], 1)
                for c in range(2):
                    filled(act, "AB", *key, f"p{c}")
                    nc.scalar.activation(PT[:, 4 * c:4 * c + 4, :, :].rearrange("p a b c -> p (a b c)"), AB[:, :], ACT.Exp,
                                         scale=HD0 ** -0.5).then_inc(free["AB"], 1)
                filled(act, "TB", *key, "o")
                nc.scalar.copy(OT[:, :, :].rearrange("p a b -> p (a b)"), TB[:, :]).then_inc(free["TB"], 1)

            def ffn0(g):
                key = ("ffn0", g)
                filled(act, "PX", *key, "x")
                nc.scalar.copy(XT[:, :, :].rearrange("p a b -> p (a b)"), PX[:, :]).then_inc(free["PX"], 1)
                act.wait_ge(z_ready, 2 * g + 1)
                nc.scalar.activation(pr[:, :, 0:E0], lg[:, :, 0:E0], ACT.Exp).then_inc(e_ready, 1)
                for i in range(BLOCKS0):
                    n = g * BLOCKS0 + i
                    u = filled(act, "H", *key, i)
                    if n >= 2:
                        act.wait_ge(free["H"], uses["H", "ffn0", *divmod(n - 2, BLOCKS0)] + 1)
                    nc.scalar.activation(HH[:, n % 2, :], H[u % 2][:, :], ACT.Copy, scale=0.5).then_inc(half_ready, 1)

            def attn1(t):
                key = ("attn1", t)
                filled(act, "TB", *key, "x")
                nc.scalar.copy(XAT[:, :, :].rearrange("p a b -> p (a b)"), TB[:, 0:D]).then_inc(free["TB"], 1)
                filled(act, "TB", *key, "w")
                nc.scalar.copy(Q1[:, :], TB[:, 0:D]).then_inc(free["TB"], 1)
                filled(act, "TB", *key, "kv")
                nc.scalar.copy(K1[:, :], TB[:, 0:D]).then_inc(v1_ready, 1)
                nc.scalar.copy(V1[:, :, 0:HD1], TB[:, D:2 * D].rearrange("p (h d) -> p h d", d=HD1)).then_inc(free["TB"], 1)
                filled(act, "AB", *key, "q")
                nc.scalar.copy(QT1[:, :, :], ABb[0:96, 0:2048].rearrange("p (n c) -> p n c", c=P)).then_inc(free["AB"], 1)
                filled(act, "AB", *key, "k")
                nc.scalar.copy(KT1[:, :, :], ABb[0:96, 0:2048].rearrange("p (n c) -> p n c", c=P)).then_inc(free["AB"], 1)
                filled(act, "TB", *key, "m")
                nc.scalar.copy(MT1[:, :], TBb[0:64, 0:P]).then_inc(free["TB"], 1)
                filled(act, "AB", *key, "p")
                nc.scalar.activation(PT1[:, :, :].rearrange("p a b -> p (a b)"), AB[:, :], ACT.Exp,
                                     scale=HD1 ** -0.5).then_inc(free["AB"], 1)
                filled(act, "AB", *key, "o")
                nc.scalar.copy(OT1[:, :, :].rearrange("p h (b s) -> p b h s", b=2),
                               AB[:, :].rearrange("p (b x) -> p b x", b=2)[:, :, 0:256].rearrange("p b (h s) -> p b h s", s=S)
                               ).then_inc(free["AB"], 1)
                filled(act, "TB", *key, "a")
                nc.scalar.copy(O1T[:, :, :].rearrange("p a b -> p (a b)"), TB[:, 0:D]).then_inc(free["TB"], 1)

            def ffn1(g):
                key = ("ffn1", g)
                filled(act, "PX", *key, "x")
                nc.scalar.copy(XT[:, :, :].rearrange("p a b -> p (a b)"), PX[:, :]).then_inc(free["PX"], 1)
                act.wait_ge(z_ready, 2 * g + 2)
                nc.scalar.activation(pr[:, :, :], lg[:, :, :], ACT.Exp).then_inc(e_ready, 1)
                act.wait_ge(dlt_ready, g + 1)
                nc.scalar.activation(ge[:, :], dlt[:, :], ACT.Exp).then_inc(ge_ready, 1)
                filled(act, "PX", *key, "g")
                nc.scalar.copy(GTT[:, :], PXb[0:32, 0:GT]).then_inc(free["PX"], 1)
                if g == 0:
                    act.wait_ge(ld_d, 16 * N_SMALL)
                    nc.scalar.activation(GB1[:, :], B1[:, :], ACT.Gelu).then_inc(gb1_ready, 1)
                read_out(act, "PX", *key, "x")
                nc.scalar.activation(GX[:, :, :].rearrange("p a b -> p (a b)"), XT[:, :, :].rearrange("p a b -> p (a b)"),
                                     ACT.Gelu).then_inc(gx_ready, 1)
                filled(act, "PX", *key, "d")
                nc.scalar.activation(GH[:, :], PX[:, 0:GT], ACT.Gelu, bias=DB[:, :]).then_inc(free["PX"], 1)
                if g == 0:
                    act.wait_ge(y0_ready, 2)
                for e in EXPERTS:
                    for c in range(CH1[e]):
                        i = WORK.index((e, c))
                        u = filled(act, "H", *key, i)
                        n = g * NCH1 + i
                        if n >= 2:
                            chunk_used(act, n - 2)
                        nc.scalar.activation(A1[:, n % 2, :], H[u % 2][:, 0:GT], ACT.Gelu,
                                             bias=B1[:, FIRST1[e] + c:FIRST1[e] + c + 1]).then_inc(free["H"], 1)
                    at = expert_at(e)
                    u = filled(act, "Y", *key, at)
                    if e == E1:
                        if g:
                            read_out(act, "Y", "ffn1", g - 1, "u1")
                        nc.scalar.activation(ACC[:, :], Y[u % 2][:, 0:GT], ACT.Identity, bias=Cb[:, :],
                                             scale=0.1).then_inc(free["Y"], 1)
                    else:
                        if at > 2:
                            read_out(act, "Y", *key, at - 2)
                        nc.scalar.activation(YS[:, at % 2, :], Y[u % 2][:, 0:GT], ACT.Identity,
                                             bias=Y0n[:, e:e + 1]).then_inc(ys_ready, 1)

            for part, n in order:
                {"attn0": attn0, "ffn0": ffn0, "attn1": attn1, "ffn1": ffn1}[part](n)

        @block.gpsimd
        def _(pool):
            link = chain(pool, pool_step)
            nc.gpsimd.memset(mhalf[:, :], -0.5)
            nc.gpsimd.memset(KS[:, :, :], 0.0)
            nc.gpsimd.memset(identf[:, :], 0.0)
            nc.gpsimd.memset(identb[:, :], 0.0)
            nc.gpsimd.memset(maskS[:, :], 0.0)
            nc.gpsimd.memset(maskT[:, :], 0.0)
            nc.gpsimd.memset(sel0[:, :, :, :], 0.0)
            nc.gpsimd.memset(sel1[:, :, :], 0.0)
            link(nc.gpsimd.memset(selG[:, :, :], 0.0))
            for m in (identf, identb):
                link(nc.gpsimd.affine_select(out=m[:, :], in_=m[:, :], compare_op=ALU.not_equal, fill=1.0, base=0,
                                             pattern=[[-1, P]], channel_multiplier=1))
            for b in range(2):
                rows = slice(b * S, (b + 1) * S)
                link(nc.gpsimd.affine_select(out=maskS[rows, :], in_=maskS[rows, :], compare_op=ALU.is_ge,
                                             fill=MASKED, base=0, pattern=[[-1, S]], channel_multiplier=1))
                link(nc.gpsimd.affine_select(out=maskT[rows, :], in_=maskT[rows, :], compare_op=ALU.is_ge,
                                             fill=MASKED, base=0, pattern=[[1, S]], channel_multiplier=-1))
            for part in range(PARTS):
                link(nc.gpsimd.affine_select(out=sel0[:, :, :, :], in_=sel0[:, :, :, :], compare_op=ALU.not_equal,
                                             fill=1.0, base=-16 * part, pattern=[[-1, NKV0], [-NKV0, 2], [0, S]],
                                             channel_multiplier=1))
                link(nc.gpsimd.affine_select(out=sel1[:, :, :], in_=sel1[:, :, :], compare_op=ALU.not_equal,
                                             fill=1.0, base=-NH1 * part, pattern=[[-1, NH1], [0, S]],
                                             channel_multiplier=1))
                link(nc.gpsimd.affine_select(out=selG[:, :, :], in_=selG[:, :, :], compare_op=ALU.not_equal,
                                             fill=1.0, base=-E1 * part, pattern=[[-1, E1], [0, P]],
                                             channel_multiplier=1))
            nc.gpsimd.iota(iota8[:, :], pattern=[[1, E1]], base=0, channel_multiplier=0,
                           allow_small_or_imprecise_dtypes=True).then_inc(pool_const, 1)

            def norm(part, n):
                i = ln_index[part, n]
                w = 1 if part.startswith("attn") else 2
                pool.wait_ge(var_ready, i + 1)
                nc.gpsimd.tensor_tensor(rstd[:, 0:w], vare[:, 0:w], mhalf[:, 0:w], ALU.pow).then_inc(rstd_ready, 1)

            def attn0(t):
                if t == 0:
                    pool.wait_ge(ld_c, 16)
                else:
                    pool.wait_ge(full["AB"], uses["AB", "attn0", t - 1, "k"] + 1)
                key = C[:, t, :].rearrange("p (k d) -> p k d", d=HD0)
                rest = KR[:, :].rearrange("p (k d) -> p k d", d=HD0)

                def slot(s):
                    return KS[:, :, s * HD0:(s + 1) * HD0]
                link(nc.gpsimd.tensor_copy(slot(0), key))
                link(nc.gpsimd.tensor_tensor(rest, key, slot(0), ALU.subtract))
                nc.gpsimd.tensor_copy(slot(3), slot(0))
                nc.gpsimd.tensor_copy(slot(5), slot(0))
                link(nc.gpsimd.tensor_copy(slot(1), rest))
                nc.gpsimd.tensor_copy(slot(4), slot(1))
                nc.gpsimd.tensor_tensor(slot(2), rest, slot(1), ALU.subtract).then_inc(ks_ready, 1)
                norm("attn0", t)

            def ffn0(g):
                norm("ffn0", g)
                for i in range(BLOCKS0):
                    n = g * BLOCKS0 + i
                    read_out(pool, "H", "ffn0", g, i)
                    if n >= 2:
                        block_used(pool, n - 2)
                    nc.gpsimd.tensor_tensor(A0[:, n % 2, :, :].rearrange("p a b -> p (a b)"), R0[:, n % 2, :],
                                            R0[:, n % 2, :], ALU.mult).then_inc(a0_ready, 1)

            def attn1(t):
                norm("attn1", t)
                pool.wait_ge(v1_ready, t + 1)
                if t:
                    pool.wait_ge(full["AB"], uses["AB", "attn1", t - 1, "k"] + 1)
                key = K1[:, :].rearrange("p (h d) -> p h d", d=HD1)
                rest = KR1[:, :].rearrange("p (h d) -> p h d", d=HD1)
                link(nc.gpsimd.tensor_copy(KS1[:, :, 0, :], key))
                link(nc.gpsimd.tensor_tensor(rest, key, KS1[:, :, 0, :], ALU.subtract))
                nc.gpsimd.tensor_copy(KS1[:, :, 3, :], KS1[:, :, 0, :])
                nc.gpsimd.tensor_copy(KS1[:, :, 5, :], KS1[:, :, 0, :])
                link(nc.gpsimd.tensor_copy(KS1[:, :, 1, :], rest))
                nc.gpsimd.tensor_copy(KS1[:, :, 4, :], KS1[:, :, 1, :])
                nc.gpsimd.tensor_tensor(KS1[:, :, 2, :], rest, KS1[:, :, 1, :], ALU.subtract).then_inc(ks1_ready, 1)

            def ffn1(g):
                norm("ffn1", g)

            for part, n in order:
                {"attn0": attn0, "ffn0": ffn0, "attn1": attn1, "ffn1": ffn1}[part](n)

        @block.vector
        def _(dve):
            link = chain(dve, dve_step)
            nc.vector.memset(QS[:, :, :], 0.0)
            nc.vector.memset(K2[:, :, :, :, :], 0.0)
            nc.vector.memset(MS[:, :, :, :, :], 0.0)
            nc.vector.memset(MS1[:, :, :], 0.0)
            nc.vector.memset(GS[:, :, :, :], 0.0)
            nc.vector.memset(V2[:, :, :, :, :].rearrange("p a b c d -> p (a b c d)"), 0.0)
            nc.vector.memset(V1[:, :, HD1 + 1:32], 0.0)
            link(nc.vector.memset(V1[:, :, HD1:HD1 + 1], 1.0))
            dve.wait_ge(ld_cd, 32)
            for half in range(2):
                rows = slice(half * S, (half + 1) * S)
                nc.vector.tensor_copy(V2[rows, :, :, half, 0:HD0],
                                      CD[rows, :, :].rearrange("p b (k d) -> p b k d", d=HD0))
                nc.vector.memset(V2[rows, :, :, half, HD0:HD0 + 1], 1.0).then_inc(v2_ready, 1)

            def norm(part, n):
                i = ln_index[part, n]
                tiles = [n] if part.startswith("attn") else [2 * n, 2 * n + 1]
                w = len(tiles)
                if part == "attn0":
                    dve.wait_ge(ld_x[n], 16)
                for k, t in enumerate(tiles):
                    link(nc.vector.bn_stats(stats[:, k, :], X[:, t, :]))
                for k, t in enumerate(tiles):
                    link(nc.vector.bn_aggr(mv[:, k, :], stats[:, k, :]))
                nc.vector.tensor_scalar(vare[:, 0:w], mv[:, 0:w, 1], EPS, None, ALU.add).then_inc(var_ready, 1)
                dve.wait_ge(rstd_ready, i + 1)
                return tiles

            def normed(dst, k, t):
                return nc.vector.tensor_scalar(dst, X[:, t, :], mv[:, k, 0:1], rstd[:, k:k + 1], ALU.subtract, ALU.mult)

            def attn0(t):
                key = ("attn0", t)
                norm(*key)
                link(normed(Q[:, :], 0, t))
                if t:
                    dve.wait_ge(full["AB"], uses["AB", "attn0", t - 1, "q"] + 1)
                q = Q[:, :].rearrange("p (h d) -> p h d", d=HD0)
                rest = QR[:, :].rearrange("p (h d) -> p h d", d=HD0)

                def slot(s):
                    return QS[:, :, s * HD0:(s + 1) * HD0]
                link(nc.vector.tensor_copy(slot(0), q))
                nc.vector.tensor_copy(slot(1), slot(0))
                nc.vector.tensor_copy(slot(2), slot(0))
                link(nc.vector.tensor_tensor(rest, q, slot(0), ALU.subtract))
                link(nc.vector.tensor_copy(slot(3), rest))
                nc.vector.tensor_copy(slot(4), slot(3))
                nc.vector.tensor_tensor(slot(5), rest, slot(3), ALU.subtract).then_inc(qs_ready, 1)
                filled(dve, "AB", *key, "k")
                for half in range(2):
                    rows = slice(half * S, (half + 1) * S)
                    last = nc.vector.tensor_copy(K2[rows, :, :, half, :],
                                                 ABb[rows, 0:1024].rearrange("p (k b t) -> p k b t", k=NKV0, b=2))
                    if half == 0:
                        link(last)
                last.then_inc(free["AB"], 1)
                for c in range(2):
                    filled(dve, "AB", *key, f"s{c}")
                    nc.vector.tensor_reduce(MN[:, 16 * c:16 * c + 16], AB[:, :].rearrange("p (h t) -> p h t", t=S),
                                            AX.X, ALU.max, negate=True).then_inc(free["AB"], 1)
                read_out(dve, "AB", *key, "s1")
                m = MN[:, :].rearrange("p (k g h) -> p g h k", g=2, h=2)
                rest = MR[:, :].rearrange("p (g h k) -> p g h k", g=2, h=2)
                link(nc.vector.tensor_copy(MS[:, :, 0, :, :], m))
                link(nc.vector.tensor_tensor(rest, m, MS[:, :, 0, :, :], ALU.subtract))
                link(nc.vector.tensor_copy(MS[:, :, 1, :, :], rest))
                nc.vector.tensor_tensor(MS[:, :, 2, :, :], rest, MS[:, :, 1, :, :], ALU.subtract).then_inc(ms_ready, 1)
                filled(dve, "TB", *key, "n")
                N = TB[:, :].rearrange("p (h x) -> p h x", x=16)
                link(nc.vector.reciprocal(rec0[:, :], N[:, :, HD0]))
                link(nc.vector.tensor_tensor(O0[:, :].rearrange("p (h d) -> p h d", d=HD0), N[:, :, 0:HD0],
                                             rec0[:, :].unsqueeze(2).to_broadcast([P, NH0, HD0]), ALU.mult))
                for half in range(2):
                    xh = X[:, t, half * P:(half + 1) * P].rearrange("p (k g r) -> p g k r", k=4, g=2)
                    oh_ = O0[:, half * P:(half + 1) * P].rearrange("p (g k r) -> p g k r", k=4, g=2)
                    last = nc.vector.tensor_tensor(xh, xh, oh_, ALU.add)
                    if half == 0:
                        link(last)
                last.then_inc(free["TB"], 1)
                read_out(dve, "TB", *key, "n")

            def softmax_small(g, e, which):
                link(nc.vector.tensor_reduce(lmax[:, :], lg[:, :, 0:e], AX.X, ALU.max))
                nc.vector.tensor_tensor(lg[:, :, 0:e], lg[:, :, 0:e], lmax[:, :].unsqueeze(2).to_broadcast([P, 2, e]),
                                        ALU.subtract).then_inc(z_ready, 1)
                dve.wait_ge(e_ready, 2 * g + which)
                link(nc.vector.tensor_reduce(lsum[:, :], pr[:, :, 0:e], AX.X, ALU.add))
                link(nc.vector.reciprocal(lsum[:, :], lsum[:, :]))
                link(nc.vector.tensor_tensor(pr[:, :, 0:e], pr[:, :, 0:e], lsum[:, :].unsqueeze(2).to_broadcast([P, 2, e]),
                                             ALU.mult))

            def ffn0(g):
                key = ("ffn0", g)
                tiles = norm(*key)
                if g:
                    dve.wait_ge(full["PX"], uses["PX", "ffn1", g - 1, "x"] + 1)
                for k, t in enumerate(tiles):
                    normed(XN[:, k, :], k, t).then_inc(xn_ready, 1)
                filled(dve, "PX", *key, "r")
                nc.vector.tensor_copy(lg[:, :, 0:E0], PX[:, 0:2 * E0].rearrange("p (t e) -> p t e", e=E0)
                                      ).then_inc(free["PX"], 1)
                read_out(dve, "PX", *key, "r")
                softmax_small(g, E0, 1)
                nc.vector.tensor_tensor(G0[:, :, 0], pr[:, :, 0], pr[:, :, 1], ALU.is_ge)
                link(nc.vector.tensor_tensor(G0[:, :, 1], pr[:, :, 1], pr[:, :, 0], ALU.is_gt))
                link(nc.vector.tensor_tensor(G0[:, :, :], G0[:, :, :], pr[:, :, 0:E0], ALU.mult))
                for i in range(BLOCKS0):
                    n = g * BLOCKS0 + i
                    dve.wait_ge(half_ready, n + 1)
                    if n >= 2:
                        dve.wait_ge(a0_ready, n - 1)
                    u = uses["H", "ffn0", g, i]
                    nc.vector.tensor_tensor(R0[:, n % 2, :], H[u % 2][:, :], HH[:, n % 2, :], ALU.max
                                            ).then_inc(free["H"], 1)
                for k, t in enumerate(tiles):
                    u = filled(dve, "Y", *key, k)
                    link(nc.vector.scalar_tensor_tensor(X[:, t, :], Y[u % 2][:, 0:D], G0[:, k, 0:1], X[:, t, :],
                                                        ALU.mult, ALU.add))
                    nc.vector.scalar_tensor_tensor(X[:, t, :], Y[u % 2][:, D:2 * D], G0[:, k, 1:2], X[:, t, :],
                                                   ALU.mult, ALU.add).then_inc(free["Y"], 1)
                    read_out(dve, "Y", *key, k)

            def attn1(t):
                key = ("attn1", t)
                norm(*key)
                if t:
                    dve.wait_ge(full["TB"], uses["TB", "attn1", t - 1, "x"] + 1)
                normed(XA[:, :], 0, t).then_inc(xa_ready, 1)
                read_out(dve, "TB", *key, "w")
                if t:
                    dve.wait_ge(full["AB"], uses["AB", "attn1", t - 1, "q"] + 1)
                q = Q1[:, :].rearrange("p (h d) -> p h d", d=HD1)
                rest = QR1[:, :].rearrange("p (h d) -> p h d", d=HD1)
                link(nc.vector.tensor_copy(QS1[:, :, 0, :], q))
                nc.vector.tensor_copy(QS1[:, :, 1, :], QS1[:, :, 0, :])
                nc.vector.tensor_copy(QS1[:, :, 2, :], QS1[:, :, 0, :])
                link(nc.vector.tensor_tensor(rest, q, QS1[:, :, 0, :], ALU.subtract))
                link(nc.vector.tensor_copy(QS1[:, :, 3, :], rest))
                nc.vector.tensor_copy(QS1[:, :, 4, :], QS1[:, :, 3, :])
                nc.vector.tensor_tensor(QS1[:, :, 5, :], rest, QS1[:, :, 3, :], ALU.subtract).then_inc(qs1_ready, 1)
                filled(dve, "AB", *key, "s")
                nc.vector.tensor_reduce(MN1[:, :], AB[:, :].rearrange("p (h t) -> p h t", t=S), AX.X, ALU.max,
                                        negate=True).then_inc(free["AB"], 1)
                read_out(dve, "AB", *key, "s")
                link(nc.vector.tensor_copy(MS1[:, 0, :], MN1[:, :]))
                link(nc.vector.tensor_tensor(MR1[:, :], MN1[:, :], MS1[:, 0, :], ALU.subtract))
                link(nc.vector.tensor_copy(MS1[:, 1, :], MR1[:, :]))
                nc.vector.tensor_tensor(MS1[:, 2, :], MR1[:, :], MS1[:, 1, :], ALU.subtract).then_inc(ms1_ready, 1)
                filled(dve, "TB", *key, "n")
                N = TB[:, :].rearrange("p (h x) -> p h x", x=32)
                link(nc.vector.reciprocal(rec1[:, :], N[:, :, HD1]))
                nc.vector.tensor_tensor(O1[:, :].rearrange("p (h d) -> p h d", d=HD1), N[:, :, 0:HD1],
                                        rec1[:, :].unsqueeze(2).to_broadcast([P, NH1, HD1]), ALU.mult
                                        ).then_inc(free["TB"], 1)
                filled(dve, "TB", *key, "r")
                nc.vector.tensor_tensor(X[:, t, :], TB[:, 0:D], X[:, t, :], ALU.add).then_inc(free["TB"], 1)
                read_out(dve, "TB", *key, "r")

            def ffn1(g):
                key = ("ffn1", g)
                tiles = norm(*key)
                dve.wait_ge(full["PX"], uses["PX", "ffn0", g, "x"] + 1)
                for k, t in enumerate(tiles):
                    normed(XN[:, k, :], k, t).then_inc(xn_ready, 1)
                if g == 0:
                    dve.wait_ge(ld_d, 16 * N_SMALL)
                    link(nc.vector.tensor_tensor(rbias[:, :], RR[:, 0, :], RR[:, 1, :], ALU.subtract))
                    link(nc.vector.tensor_tensor(obias[:, :], BR[:, 0, :], BR[:, 1, :], ALU.add))
                filled(dve, "PX", *key, "r")
                nc.vector.tensor_tensor(lg[:, :, :], PX[:, 0:2 * E1].rearrange("p (t e) -> p t e", e=E1),
                                        rbias[:, :].unsqueeze(1).to_broadcast([P, 2, E1]), ALU.add
                                        ).then_inc(free["PX"], 1)
                read_out(dve, "PX", *key, "r")
                softmax_small(g, E1, 2)
                dve.wait_ge(pool_const, 1)
                for k in range(2):
                    link(nc.vector.max(top[:, k, :], pr[:, k, :]))
                for k in range(2):
                    link(nc.vector.max_index(topi[:, k, :], top[:, k, :], pr[:, k, :]))
                nc.vector.tensor_tensor(dlt[:, :], top[:, :, 1], top[:, :, 0], ALU.subtract).then_inc(dlt_ready, 1)
                link(nc.vector.tensor_copy(topf[:, :, :], topi[:, :, :]))
                dve.wait_ge(ge_ready, g + 1)
                link(nc.vector.tensor_scalar(dlt[:, :], ge[:, :], 1.0, None, ALU.add))
                link(nc.vector.reciprocal(gk[:, :, 0], dlt[:, :]))
                link(nc.vector.tensor_tensor(gk[:, :, 1], gk[:, :, 0], ge[:, :], ALU.mult))
                for k in range(2):
                    link(nc.vector.tensor_scalar(oh[:, k, :], iota8[:, :], topf[:, k, 0:1], gk[:, k, 0:1],
                                                 ALU.is_equal, ALU.mult))
                    link(nc.vector.tensor_scalar(gate[:, k, :], iota8[:, :], topf[:, k, 1:2], gk[:, k, 1:2],
                                                 ALU.is_equal, ALU.mult))
                link(nc.vector.tensor_tensor(gate[:, :, :], gate[:, :, :], oh[:, :, :], ALU.add))
                link(nc.vector.tensor_copy(GS[:, :, 0, :], gate[:, :, :]))
                link(nc.vector.tensor_tensor(GR[:, :, :], gate[:, :, :], GS[:, :, 0, :], ALU.subtract))
                link(nc.vector.tensor_copy(GS[:, :, 1, :], GR[:, :, :]))
                nc.vector.tensor_tensor(GS[:, :, 2, :], GR[:, :, :], GS[:, :, 1, :], ALU.subtract).then_inc(gs_ready, 1)
                if g == 0:
                    dve.wait_ge(y0_full, 1)
                    link(nc.vector.tensor_reduce(Cb[:, :], Y[1][:, 0:E1], AX.X, ALU.add))
                    link(nc.vector.tensor_reduce(lsum[:, 0:1], B2[:, 0:E1], AX.X, ALU.add))
                    link(nc.vector.tensor_tensor(Cb[:, :], Cb[:, :], lsum[:, 0:1], ALU.add))
                    nc.vector.scalar_tensor_tensor(Cb[:, :], B2[:, E1:E1 + 1], 0.1, Cb[:, :], ALU.mult, ALU.add
                                                   ).then_inc(y0_ready, 1)
                    nc.vector.tensor_scalar(Y0n[:, :], Y[1][:, 0:E1], -1.0, None, ALU.mult).then_inc(y0_ready, 1)
                read_out(dve, "Y", *key, 0)
                for e in range(E1):
                    at = expert_at(e)
                    dve.wait_ge(ys_ready, g * E1 + e + 1)
                    u = uses["Y", "ffn1", g, at]
                    nc.vector.tensor_tensor(YG[:, :], YS[:, at % 2, :], Y[u % 2][:, GT:2 * GT], ALU.mult
                                            ).then_inc(free["Y"], 1)
                    read_out(dve, "Y", *key, at)
                    if e < E1 - 1:
                        link(nc.vector.tensor_tensor(ACC[:, :], ACC[:, :], YG[:, :], ALU.add))
                    else:
                        nc.vector.tensor_tensor(ACC[:, :], ACC[:, :], YG[:, :], ALU.add).then_inc(acc_ready, 1)
                for k, t in enumerate(tiles):
                    link(nc.vector.tensor_tensor(X[:, t, :], X[:, t, :], obias[:, :], ALU.add))
                for k, t in enumerate(tiles):
                    u = filled(dve, "Y", *key, f"u{k}")
                    nc.vector.tensor_tensor(X[:, t, :], Y[u % 2][:, 0:D], X[:, t, :], ALU.add).then_inc(free["Y"], 1)
                    read_out(dve, "Y", *key, f"u{k}")

            for part, n in order:
                {"attn0": attn0, "ffn0": ffn0, "attn1": attn1, "ffn1": ffn1}[part](n)

        @block.tensor
        def _(pe):
            pe.wait_ge(pool_const, 1)

            def attn0(t):
                key = ("attn0", t)
                claim(pe, "AB", *key, "q")
                pe.wait_ge(qs_ready, t + 1)
                for pair in range(NH0 // 2):
                    last = nc.tensor.transpose(ABb[:, pair * P:(pair + 1) * P],
                                               QS[:, 2 * pair:2 * pair + 2, :].rearrange("p a b -> p (a b)"), identb[:, :])
                last.then_inc(full["AB"], 1)
                claim(pe, "AB", *key, "k")
                pe.wait_ge(ks_ready, t + 1)
                for kv in range(NKV0):
                    for half in range(2):
                        last = nc.tensor.transpose(ABb[half * S:(half + 1) * S, kv * P:(kv + 1) * P], KS[:, kv, :],
                                                   identb[:, :])
                last.then_inc(full["AB"], 1)
                for c in range(2):
                    claim(pe, "AB", *key, f"s{c}")
                    for i in range(8):
                        pair = 8 * c + i
                        for b in range(2):
                            last = nc.tensor.matmul(AB[b * S:(b + 1) * S, i * P:(i + 1) * P], QT[:, pair, b * S:(b + 1) * S],
                                                    K2[:, pair // 2, b, :, :].rearrange("p a b -> p (a b)"),
                                                    start=True, stop=True)
                    last.then_inc(full["AB"], 1)
                claim(pe, "TB", *key, "m")
                pe.wait_ge(ms_ready, t + 1)
                for gp in range(2):
                    last = nc.tensor.transpose(TBb[0:64, gp * P:(gp + 1) * P],
                                               MS[:, gp, :, :, :].rearrange("p a b c -> p (a b c)"), identb[:, :])
                last.then_inc(full["TB"], 1)
                read_out(pe, "TB", *key, "m")
                for c in range(2):
                    claim(pe, "AB", *key, f"p{c}")
                    for i in range(4):
                        kv = 4 * c + i
                        for b in range(2):
                            o = AB[:, (2 * i + b) * P:(2 * i + b + 1) * P]
                            nc.tensor.matmul(o, sel0[:, kv, :, :].rearrange("p a b -> p (a b)"),
                                             MT[:, :, b * S:(b + 1) * S], start=True, stop=False)
                            last = nc.tensor.matmul(o, K2[:, kv, b, :, :].rearrange("p a b -> p (a b)"),
                                                    QT[:, 2 * kv:2 * kv + 2, b * S:(b + 1) * S], start=False, stop=True)
                    last.then_inc(full["AB"], 1)
                claim(pe, "TB", *key, "o")
                if t == 0:
                    pe.wait_ge(v2_ready, 2)
                read_out(pe, "AB", *key, "p1")
                o = TB[:, :].rearrange("p (h g b s) -> p h g b s", h=2, g=2, b=2)
                for kh in range(2):
                    for b in range(2):
                        for k4 in range(4):
                            kv = 4 * kh + k4
                            last = nc.tensor.matmul(o[32 * k4:32 * k4 + 32, kh, :, b, :],
                                                    V2[:, 2 * t + b, kv, :, :].rearrange("p a b -> p (a b)"),
                                                    PT[:, kv, b, :], start=True, stop=True)
                last.then_inc(full["TB"], 1)
                claim(pe, "TB", *key, "n")
                for i in range(4):
                    last = nc.tensor.transpose(TB[:, i * P:(i + 1) * P], OT[:, i, :], identf[:, :])
                last.then_inc(full["TB"], 1)

            def turn(g, which):
                part = ("ffn0", "ffn1")[which]
                claim(pe, "PX", part, g, "x")
                for k in range(2):
                    pe.wait_ge(xn_ready, 4 * g + 2 * which + k + 1)
                    for dc in range(DC):
                        last = nc.tensor.transpose(PX[:, dc * GT + k * P:dc * GT + (k + 1) * P],
                                                   XN[:, k, dc * P:(dc + 1) * P], identf[:, :])
                last.then_inc(full["PX"], 1)

            def route(g, part, w, e):
                claim(pe, "PX", part, g, "r")
                for k in range(2):
                    for dc in range(DC):
                        last = nc.tensor.matmul(PX[:, k * e:(k + 1) * e], XT[:, dc, k * P:(k + 1) * P], w[:, dc, :],
                                                start=(dc == 0), stop=(dc == DC - 1))
                last.then_inc(full["PX"], 1)

            def ffn0(g):
                key = ("ffn0", g)
                turn(g, 0)
                read_out(pe, "PX", *key, "x")
                if g == 0:
                    pe.wait_ge(ld_f0, 16 * 3)
                route(g, "ffn0", WR0, E0)
                NB = E0 * K0 // 2

                def up(i):
                    u = claim(pe, "H", *key, i)
                    e, c0 = divmod(2 * i, K0)
                    for c in range(2):
                        for dc in range(DC):
                            last = nc.tensor.matmul(H[u % 2][:, c * GT:(c + 1) * GT],
                                                    WF0[:, e, dc, (c0 + c) * P:(c0 + c + 1) * P], XT[:, dc, :],
                                                    start=(dc == 0), stop=(dc == DC - 1))
                    last.then_inc(full["H"], 1)

                def down(i):
                    n = g * NB + i
                    e, c0 = divmod(2 * i, K0)
                    pe.wait_ge(a0_ready, n + 1)
                    for k in range(2):
                        for c in range(2):
                            yb = Y[uses["Y", "ffn0", g, k] % 2]
                            last = nc.tensor.matmul(yb[:, e * D:(e + 1) * D], A0[:, n % 2, c, k * P:(k + 1) * P],
                                                    WP0[:, e, c0 + c, :], start=(c0 + c == 0), stop=(c0 + c == K0 - 1))
                        if i == NB - 1:
                            last.then_inc(full["Y"], 1)
                    if i < NB - 1:
                        last.then_inc(a0_used, 1)

                up(0)
                up(1)
                claim(pe, "Y", *key, 0)
                claim(pe, "Y", *key, 1)
                if g == 0:
                    pe.wait_ge(ld_p0, 16 * 2)
                for i in range(NB):
                    down(i)
                    if i + 2 < NB:
                        up(i + 2)

            def attn1(t):
                key = ("attn1", t)
                claim(pe, "TB", *key, "x")
                pe.wait_ge(xa_ready, t + 1)
                for dc in range(DC):
                    last = nc.tensor.transpose(TB[:, dc * P:(dc + 1) * P], XA[:, dc * P:(dc + 1) * P], identf[:, :])
                last.then_inc(full["TB"], 1)
                claim(pe, "TB", *key, "w")
                if t == 0:
                    pe.wait_ge(ld_a1, 16 * 3)
                    pe.wait_ge(ld_ct, 16)
                for dc in range(DC):
                    last = nc.tensor.matmul(TB[:, 0:D], XAT[:, dc, :], WQ1[:, dc, :], start=(dc == 0), stop=(dc == DC - 1))
                last.then_inc(full["TB"], 1)
                claim(pe, "TB", *key, "kv")
                nc.tensor.matmul(TB[:, :], CT[:, t * P:(t + 1) * P], WKV1[:, :], start=True, stop=True
                                 ).then_inc(full["TB"], 1)
                for which, src, ready in (("q", QS1, qs1_ready), ("k", KS1, ks1_ready)):
                    claim(pe, "AB", *key, which)
                    pe.wait_ge(ready, t + 1)
                    for h in range(NH1):
                        last = nc.tensor.transpose(ABb[0:96, h * P:(h + 1) * P],
                                                   src[:, h, :, :].rearrange("p a b -> p (a b)"), identb[:, :])
                    last.then_inc(full["AB"], 1)
                claim(pe, "AB", *key, "s")
                for half in range(2):
                    nc.tensor.matmul(AB[:, half * 512:(half + 1) * 512], identb[:, :],
                                     maskS[:, :].unsqueeze(1).to_broadcast([P, 8, S]), start=True, stop=False,
                                     skip_group_check=True)
                    for h in range(8 * half, 8 * half + 8):
                        for b in range(2):
                            rows = slice(b * S, (b + 1) * S)
                            last = nc.tensor.matmul(AB[rows, h * S:(h + 1) * S], QT1[:, h, rows], KT1[:, h, rows],
                                                    start=False, stop=True, skip_group_check=True)
                last.then_inc(full["AB"], 1)
                claim(pe, "TB", *key, "m")
                pe.wait_ge(ms1_ready, t + 1)
                nc.tensor.transpose(TBb[0:64, 0:P], MS1[:, :, :].rearrange("p a b -> p (a b)"), identb[:, :]
                                    ).then_inc(full["TB"], 1)
                read_out(pe, "TB", *key, "m")
                claim(pe, "AB", *key, "p")
                for half in range(2):
                    nc.tensor.matmul(AB[:, half * 512:(half + 1) * 512], identb[:, :],
                                     maskT[:, :].unsqueeze(1).to_broadcast([P, 8, S]), start=True, stop=False,
                                     skip_group_check=True)
                    for h in range(8 * half, 8 * half + 8):
                        for b in range(2):
                            rows = slice(b * S, (b + 1) * S)
                            nc.tensor.matmul(AB[rows, h * S:(h + 1) * S], sel1[:, h, :], MT1[:, rows],
                                             start=False, stop=True, skip_group_check=True)
                            last = nc.tensor.matmul(AB[rows, h * S:(h + 1) * S], KT1[:, h, rows], QT1[:, h, rows],
                                                    start=False, stop=True, skip_group_check=True)
                last.then_inc(full["AB"], 1)
                claim(pe, "AB", *key, "o")
                read_out(pe, "TB", *key, "kv")
                for hq in range(4):
                    for h4 in range(4):
                        h = 4 * hq + h4
                        for b in range(2):
                            rows = slice(b * S, (b + 1) * S)
                            last = nc.tensor.matmul(AB[32 * h4:32 * h4 + 32, b * 512 + hq * S:b * 512 + (hq + 1) * S],
                                                    V1[rows, h, :], PT1[rows, h, :], start=True, stop=True)
                last.then_inc(full["AB"], 1)
                read_out(pe, "AB", *key, "o")
                claim(pe, "TB", *key, "n")
                for i in range(4):
                    last = nc.tensor.transpose(TB[:, i * P:(i + 1) * P], OT1[:, i, :], identf[:, :])
                last.then_inc(full["TB"], 1)
                claim(pe, "TB", *key, "a")
                for dc in range(DC):
                    last = nc.tensor.transpose(TB[:, dc * P:(dc + 1) * P], O1[:, dc * P:(dc + 1) * P], identf[:, :])
                last.then_inc(full["TB"], 1)
                claim(pe, "TB", *key, "r")
                for dc in range(DC):
                    last = nc.tensor.matmul(TB[:, 0:D], O1T[:, dc, :], WO1[:, dc, :], start=(dc == 0), stop=(dc == DC - 1))
                last.then_inc(full["TB"], 1)

            def ffn1(g):
                key = ("ffn1", g)
                turn(g, 1)
                read_out(pe, "PX", *key, "x")
                if g == 0:
                    pe.wait_ge(ld_d, 16 * N_SMALL)
                route(g, "ffn1", RW, E1)
                claim(pe, "PX", *key, "g")
                pe.wait_ge(gs_ready, g + 1)
                for k in range(2):
                    last = nc.tensor.transpose(PXb[0:32, k * P:(k + 1) * P], GS[:, k, :, :].rearrange("p a b -> p (a b)"),
                                               identb[:, :])
                last.then_inc(full["PX"], 1)
                claim(pe, "PX", *key, "d")
                for dc in range(DC):
                    last = nc.tensor.matmul(PX[:, 0:GT], DW[:, dc, :], XT[:, dc, :], start=(dc == 0), stop=(dc == DC - 1))
                last.then_inc(full["PX"], 1)
                read_out(pe, "PX", *key, "d")
                if g == 0:
                    pe.wait_ge(ld_w1, 16)
                    pe.wait_ge(ld_w2, 16)
                    pe.wait_ge(gb1_ready, 1)
                    read_out(pe, "Y", "ffn0", 0, 1)
                    for e in range(E1):
                        for c in range(CH1[e]):
                            ch = FIRST1[e] + c
                            last = nc.tensor.matmul(Y[1][:, e:e + 1], W2[:, ch, :], GB1[:, ch:ch + 1], start=(c == 0),
                                                    stop=(c == CH1[e] - 1))
                    last.then_inc(y0_full, 1)
                    pe.wait_ge(y0_ready, 2)
                def up(i):
                    e, c = WORK[i]
                    u = claim(pe, "H", *key, i)
                    nc.tensor.matmul(H[u % 2][:, 0:GT], W1[:, FIRST1[e] + c, :], GH[:, :], start=True, stop=True
                                     ).then_inc(full["H"], 1)

                def down(i):
                    e, c = WORK[i]
                    at = expert_at(e)
                    read_out(pe, "H", *key, i)
                    if c == 0:
                        u = claim(pe, "Y", *key, at)
                        if e < E1:
                            nc.tensor.matmul(Y[u % 2][:, GT:2 * GT], selG[:, e, :], GTT[:, :], start=True, stop=True)
                    u = uses["Y", "ffn1", g, at]
                    last_c = c == CH1[e] - 1
                    mm = nc.tensor.matmul(Y[u % 2][:, 0:GT], W2[:, FIRST1[e] + c, :], A1[:, (g * NCH1 + i) % 2, :],
                                          start=(c == 0), stop=last_c)
                    mm.then_inc(full["Y"] if last_c else a1_used, 1)

                up(0)
                up(1)
                for i in range(NCH1):
                    down(i)
                    if i + 2 < NCH1:
                        up(i + 2)
                for k in range(2):
                    u = claim(pe, "Y", *key, f"u{k}")
                    o = Y[u % 2][:, 0:D]
                    if k == 0:
                        pe.wait_ge(gx_ready, g + 1)
                    for dc in range(DC):
                        nc.tensor.matmul(o, GX[:, dc, k * P:(k + 1) * P], CW[:, dc, :], start=(dc == 0), stop=False)
                    if k == 0:
                        pe.wait_ge(acc_ready, g + 1)
                    nc.tensor.matmul(o, ACC[:, k * P:(k + 1) * P], UW[:, :], start=False, stop=True
                                     ).then_inc(full["Y"], 1)

            for part, n in order:
                {"attn0": attn0, "ffn0": ffn0, "attn1": attn1, "ffn1": ffn1}[part](n)


COST_LAMBDA = 1e-07


def kernel(**inputs):
    import numpy as np
    import concourse.bacc as bacc
    from concourse.bass_utils import run_bass_kernel_spmd as run

    a = {n: np.asarray(v) for n, v in inputs.items()}

    def chunks(w):
        return w.reshape(-1, P, w.shape[1]).transpose(1, 0, 2)

    f = "L1_ffn_"
    names = [f"{f}e{e}_" for e in range(E1)] + [f + "shared_"]
    cost = np.array([2 * L * h for h in HIDS], np.float32) * np.float32(COST_LAMBDA)
    arrays = {
        "x": a["x"].reshape(B * S, D),
        "ctx_in": a["ctx_512"].reshape(B * S, CTX),
        "ctxT": a["ctx_512"].reshape(B * S, CTX).T,
        "wr0": chunks(a["L0_ffn_w_router"].T),
        "wf0": a["L0_ffn_w_fc"].reshape(E0, HID0, DC, P).transpose(3, 0, 2, 1),
        "wp0": a["L0_ffn_w_proj"].reshape(E0, D, K0, P).transpose(3, 0, 2, 1),
        "wq1": chunks(a["L1_xattn_Wq"].T),
        "wkv1": a["L1_xattn_Wkv_expand"].T,
        "wo1": chunks(a["L1_xattn_Wout"].T),
        "down_w": chunks(a[f + "down_w"]),
        "down_b": a[f + "down_b"].reshape(L, 1),
        "up_w": a[f + "up_w"],
        "bias_rows": np.broadcast_to(np.stack([a[f + "up_b"], a[f + "core_b"]]), (P, 2, D)),
        "router_w": chunks(a[f + "router_w"]),
        "router_rows": np.broadcast_to(np.stack([a[f + "router_b"], cost]), (P, 2, E1)),
        "core_w": chunks(a[f + "core_w"]),
        "w1": np.concatenate([a[n + ("w1")] for n in names], 1).reshape(L, NCH1, P),
        "b1": np.concatenate([a[n + "b1"] for n in names]).reshape(NCH1, P).T,
        "w2": chunks(np.concatenate([a[n + "w2"] for n in names], 0)),
        "b2": np.stack([a[n + "b2"] for n in names], 1),
    }
    nc = bacc.Bacc("TRN2", target_bir_lowering=False, num_devices=1)
    feed, args = {}, []
    for name, v in arrays.items():
        v = np.ascontiguousarray(v)
        feed[f"in_{name}"] = v
        args.append(nc.dram_tensor(f"in_{name}", v.shape, mybir.dt.from_np(v.dtype), kind="ExternalInput").ap())
    args.append(nc.dram_tensor("out_dram", (B * S, D), fp32, kind="ExternalOutput").ap())
    mixed_network(nc, *args)
    r = run(nc, [feed], core_ids=[0])
    return r.results[0]["out_dram"].reshape(B, S, D)
```

```python
import concourse.bass as bass
from concourse import mybir
from contextlib import ExitStack

fp32 = mybir.dt.float32
bf16 = mybir.dt.bfloat16
u32 = mybir.dt.uint32
ALU = mybir.AluOpType
ACT = mybir.ActivationFunctionType
AX = mybir.AxisListType

P = 128
B, S, D = 16, 64, 256
TILES = B * S // P
GROUPS = TILES // 2
GT = 2 * P
DC = D // P
CTX = 64
NH0, NKV0, HD0 = 32, 8, 8
NH1, HD1 = 16, 16
E0, HID0 = 2, 1024
K0 = HID0 // P
L = 128
HIDS = [128, 256, 384, 512, 128, 256, 384, 512]
E1 = len(HIDS)
CH1 = [h // P for h in HIDS] + [1]
FIRST1 = [sum(CH1[:e]) for e in range(E1 + 1)]
NCH1 = sum(CH1)
EPS = 1e-5
MASKED = -3.0e38
PARTS = 3
SLOTS = 6


def mixed_network(nc: bass.Bass, x, ctx_in, ctxT, wr0, wf0, wp0, wq1, wkv1, wo1, down_w, down_b,
                  up_w, bias_rows, router_w, router_rows, core_w, w1, b1, w2, b2, out):
    ctx = ExitStack()
    with ctx:
        def sb(name, shape, dt):
            return ctx.enter_context(nc.sbuf_tensor(name, shape, dt))

        def ps(name, shape, dt):
            return ctx.enter_context(nc.psum_tensor(name, shape, dt))

        def sem(name):
            return ctx.enter_context(nc.semaphore(name))

        X = sb("X", [P, TILES, D], fp32)
        C = sb("C", [P, TILES, CTX], fp32)
        CT = sb("CT", [CTX, B * S], fp32)
        CD = sb("CD", [P, B, CTX], fp32)
        WR0 = sb("WR0", [P, DC, E0], fp32)
        WF0 = sb("WF0", [P, E0, DC, HID0], fp32)
        WP0 = sb("WP0", [P, E0, K0, D], fp32)
        WQ1 = sb("WQ1", [P, DC, D], fp32)
        WKV1 = sb("WKV1", [CTX, 2 * D], fp32)
        WO1 = sb("WO1", [P, DC, D], fp32)
        DW = sb("DW", [P, DC, L], fp32)
        DB = sb("DB", [P, 1], fp32)
        UW = sb("UW", [P, D], fp32)
        BR = sb("BR", [P, 2, D], fp32)
        RW = sb("RW", [P, DC, E1], fp32)
        RR = sb("RR", [P, 2, E1], fp32)
        CW = sb("CW", [P, DC, D], fp32)
        W1 = sb("W1", [P, NCH1, P], fp32)
        B1 = sb("B1", [P, NCH1], fp32)
        W2 = sb("W2", [P, NCH1, L], fp32)
        B2 = sb("B2", [P, E1 + 1], fp32)

        identf = sb("identf", [P, P], fp32)
        identb = sb("identb", [P, P], bf16)
        maskS = sb("maskS", [P, S], bf16)
        maskT = sb("maskT", [P, S], bf16)
        sel0 = sb("sel0", [64, NKV0, 2, S], bf16)
        sel1 = sb("sel1", [64, NH1, S], bf16)
        selG = sb("selG", [32, E1, P], bf16)
        iota8 = sb("iota8", [P, E1], fp32)
        mhalf = sb("mhalf", [P, 2], fp32)
        rbias = sb("rbias", [P, E1], fp32)
        obias = sb("obias", [P, D], fp32)
        GB1 = sb("GB1", [P, NCH1], fp32)
        Y0n = sb("Y0n", [P, E1], fp32)
        Cb = sb("Cb", [P, 1], fp32)

        stats = sb("stats", [P, 2, 2, 6], fp32)
        mv = sb("mv", [P, 2, 2, 2], fp32)
        vare = sb("vare", [P, 2, 2], fp32)
        rstd = sb("rstd", [P, 2, 2], fp32)
        Q = sb("Q", [P, 2, D], fp32)
        QR = sb("QR", [P, 2, D], fp32)
        QS = sb("QS", [P, 2, NH0, 64], bf16)
        KR = sb("KR", [P, 2, CTX], fp32)
        KS = sb("KS", [P, 2, NKV0, 64], bf16)
        QT = sb("QT", [P, 2, NH0 // 2, P], bf16)
        K2 = sb("K2", [P, 2, NKV0, 2, 2, S], bf16)
        MN = sb("MN", [P, 2, NH0], fp32)
        MR = sb("MR", [P, 2, NH0], fp32)
        MS = sb("MS", [P, 2, 2, 4, 2, NKV0], bf16)
        MT = sb("MT", [64, 2, 2, P], bf16)
        PT = sb("PT", [P, 2, NKV0, 2, P], fp32)
        V2 = sb("V2", [P, 2, 2, NKV0, 2, 16], fp32)
        OT = sb("OT", [P, 2, 4, P], fp32)
        rec = sb("rec", [P, 2, NH0], fp32)
        O0 = sb("O0", [P, 2, D], fp32)
        XA, QR1, OT1, O1 = Q, QR, OT[:, :, :, :].rearrange("p t a (b s) -> p t a b s", b=2), O0
        QS1 = QS[:, :, 0:24, :].rearrange("p t a (c d) -> p t (a c) d", d=HD1).rearrange(
            "p t (h s) d -> p t h s d", s=SLOTS)
        QT1 = QT[0:SLOTS * HD1, :, :, :]
        PT1 = PT[:, :, 0:4, :, :].rearrange("p t a b (c s) -> p t (a b c) s", s=S)
        XAT = sb("XAT", [P, 2, DC, P], fp32)
        KR1 = sb("KR1", [P, 2, D], fp32)
        KS1 = sb("KS1", [P, 2, NH1, SLOTS, HD1], bf16)
        V1 = sb("V1", [P, 2, NH1, 32], fp32)
        KT1 = sb("KT1", [SLOTS * HD1, 2, NH1, P], bf16)
        MS1 = sb("MS1", [P, 2, 4, NH1], bf16)
        MT1 = sb("MT1", [64, 2, P], bf16)
        O1T = sb("O1T", [P, 2, DC, P], fp32)

        statsf = sb("statsf", [P, 2, 6], fp32)
        mvf = sb("mvf", [P, 2, 2], fp32)
        varef = sb("varef", [P, 2], fp32)
        rstdf = sb("rstdf", [P, 2], fp32)
        XN = sb("XN", [P, 2, D], fp32)
        XT0 = sb("XT0", [P, DC, GT], fp32)
        XT1 = sb("XT1", [P, DC, GT], fp32)
        lg = sb("lg", [P, 2, E1], fp32)
        pr = sb("pr", [P, 2, E1], fp32)
        lmax = sb("lmax", [P, 2], fp32)
        lsum = sb("lsum", [P, 2], fp32)
        G0 = sb("G0", [P, 2, E0], fp32)
        HH = sb("HH", [P, 2, 512], fp32)
        R0 = sb("R0", [P, 2, 512], fp32)
        A0 = sb("A0", [P, 2, 2, GT], fp32)
        top = sb("top", [P, 2, 8], fp32)
        topi = sb("topi", [P, 2, 8], u32)
        topf = sb("topf", [P, 2, 8], fp32)
        dlt = sb("dlt", [P, 2], fp32)
        ge = sb("ge", [P, 2], fp32)
        gk = sb("gk", [P, 2, 2], fp32)
        oh = sb("oh", [P, 2, E1], fp32)
        gate = sb("gate", [P, 2, E1], fp32)
        GR = sb("GR", [P, 2, E1], fp32)
        GS = sb("GS", [P, 2, 4, E1], bf16)
        GTT = sb("GTT", [32, GT], bf16)
        GX = sb("GX", [P, DC, GT], fp32)
        GH = sb("GH", [P, GT], fp32)
        A1 = sb("A1", [P, 2, GT], fp32)
        YS = sb("YS", [P, 2, GT], fp32)
        YG = sb("YG", [P, 2, GT], fp32)
        ACC = sb("ACC", [P, GT], fp32)

        BANKS = {"AB": 2, "TB": 1, "PX": 1, "H": 2, "Y": 2}
        bank = {n: [ps(f"{n}{i}", [P, 512], fp32) for i in range(k)] for n, k in BANKS.items()}

        BLOCKS0 = E0 * K0 // 2
        EXPERTS = [E1] + list(range(E1))
        WORK = [(e, c) for e in EXPERTS for c in range(CH1[e])]

        def stages(part, n, *names):
            out = []
            for name in names:
                name, _, times = name.partition("*")
                out += [(part, n, name, i) for i in range(int(times or 1))]
            return out

        def attn0(t):
            return stages("attn0", t, "v", "ln", "q*2", "k", "s*4", "m", "p*4", "o", "n")

        def attn1(t):
            return stages("attn1", t, "v", "kv", "ln", "x", "w", "k*2", "q*2", "s*2", "m", "p*2", "o*2", "n", "a", "r")

        def ffn0_head(g):
            return stages("ffn0", g, "v", "ln", "x", "r", "g")

        def ffn0_body(g):
            up, down = stages("ffn0", g, f"u*{BLOCKS0}"), stages("ffn0", g, f"d*{BLOCKS0}")
            return up[0:2] + sum(([down[i]] + up[i + 2:i + 3] for i in range(BLOCKS0)), []) + stages("ffn0", g, "y*2")

        def ffn1_head(g):
            return stages("ffn1", g, "v", "ln", "x", "r", "e", "t", "g", "d")

        def ffn1_body(g):
            out = stages("ffn1", g, "c*2")
            for i, (e, c) in enumerate(WORK):
                out.append(("ffn1", g, "w", i))
                if i + 2 < NCH1:
                    out.append(("ffn1", g, "c", i + 2))
                if c == CH1[e] - 1:
                    out.append(("ffn1", g, "y", EXPERTS.index(e)))
            return out + stages("ffn1", g, "o*2")

        def merge(a, b):
            out, i, j = [], 0, 0
            while i < len(a) or j < len(b):
                if j >= len(b) or (i < len(a) and i * len(b) <= j * len(a)):
                    out.append(a[i])
                    i += 1
                else:
                    out.append(b[j])
                    j += 1
            return out

        def pair(part, g):
            return merge(part(2 * g), part(2 * g + 1))

        last = GROUPS - 1
        plan = pair(attn0, 0) + ffn0_head(0) + merge(ffn0_body(0), pair(attn0, 1) + ffn0_head(1))
        plan += stages("ffn1", 0, "z")
        for g in range(GROUPS):
            light = pair(attn1, g) + ffn1_head(g)
            if g < last:
                plan += merge(ffn0_body(g + 1), light)
            beside = []
            if g + 2 <= last:
                beside = pair(attn0, g + 2) + ffn0_head(g + 2)
            if g == last - 1:
                beside = pair(attn1, last) + ffn1_head(last)
            plan += merge(ffn1_body(g), beside)
            if g == last - 1:
                plan += ffn1_body(last)
                break

        FILLS = {("attn0", s): b for s, b in zip("qkspmon", ("AB",) * 4 + ("TB",) * 3)}
        FILLS |= {("attn1", s): "AB" for s in "kqspo"}
        FILLS |= {("attn1", s): "TB" for s in ("kv", "x", "w", "m", "n", "a", "r")}
        FILLS |= {("ffn0", "x"): "PX", ("ffn0", "r"): "PX", ("ffn0", "u"): "H", ("ffn0", "y"): "Y"}
        FILLS |= {("ffn1", "x"): "PX", ("ffn1", "r"): "PX", ("ffn1", "g"): "PX", ("ffn1", "d"): "PX",
                  ("ffn1", "c"): "H", ("ffn1", "y"): "Y", ("ffn1", "o"): "Y", ("ffn1", "z"): "TB"}
        BY_ACT = {("attn0", s) for s in "qpmo"} | {("attn1", s) for s in "xqmpoa"}
        BY_ACT |= {("ffn0", "x"), ("ffn1", "x"), ("ffn1", "g"), ("ffn1", "d"), ("ffn1", "c")}
        READERS = ("act", "dve")
        full = {b: sem(f"{b}_full") for b in BANKS}
        free = {(b, r): sem(f"{b}_free_{r}") for b in BANKS for r in READERS}
        uses, order, reads = {}, {b: [] for b in BANKS}, dict.fromkeys(free, 0)
        for step in plan:
            b = FILLS.get((step[0], step[2]))
            if b:
                shared_expert = step[0] == "ffn1" and step[2] == "y" and step[3] == 0
                r = "act" if (step[0], step[2]) in BY_ACT or shared_expert else "dve"
                reads[b, r] += 1
                uses[step] = b, len(order[b]), free[b, r], reads[b, r]
                order[b].append(step)

        def at(*step):
            b, u, _, _ = uses[step]
            return bank[b][u % BANKS[b]]

        def read_out(eng, *step):
            _, _, done, n = uses[step]
            eng.wait_ge(done, n)

        def claim(eng, *step):
            b, u, _, _ = uses[step]
            if u >= BANKS[b]:
                read_out(eng, *order[b][u - BANKS[b]])
            return at(*step), full[b]

        def filled(eng, *step):
            b, u, done, _ = uses[step]
            eng.wait_ge(full[b], u + 1)
            return at(*step), done

        LN = [x for x in plan if x[2] == "v"]
        TURNS = [x for x in plan if x[0][0] == "f" and x[2] == "x"]
        ROUTES = [x for x in plan if (x[0], x[2]) in (("ffn0", "g"), ("ffn1", "e"))]
        ROUTED = {(x[0], x[1]): i + 1 for i, x in enumerate(ROUTES)}

        def block_used(eng, n):
            g, i = divmod(n, BLOCKS0)
            if i == BLOCKS0 - 1:
                filled(eng, "ffn0", g, "y", 1)
            else:
                eng.wait_ge(a0_used, g * (BLOCKS0 - 1) + i + 1)

        INNER = [k for k, (e, c) in enumerate(WORK) if c < CH1[e] - 1]

        def chunk_used(eng, n):
            g, i = divmod(n, NCH1)
            e, c = WORK[i]
            if i in INNER:
                eng.wait_ge(a1_used, g * len(INNER) + INNER.index(i) + 1)
            else:
                filled(eng, "ffn1", g, "y", EXPERTS.index(e))

        ld_x = [sem(f"ld_x{t}") for t in range(TILES)]
        ld_c = sem("ld_c")
        ld_cd = sem("ld_cd")
        ld_f0 = sem("ld_f0")
        ld_p0 = sem("ld_p0")
        ld_a1 = sem("ld_a1")
        ld_w = sem("ld_w")
        ld_small = sem("ld_small")
        pool_const = sem("pool_const")
        v2_ready = sem("v2_ready")
        var_ready = sem("var_ready")
        rstd_ready = sem("rstd_ready")
        qs_ready = sem("qs_ready")
        ks_ready = sem("ks_ready")
        ms_ready = sem("ms_ready")
        xa_ready = sem("xa_ready")
        kh_ready = sem("kh_ready")
        qs1_ready = sem("qs1_ready")
        ks1_ready = sem("ks1_ready")
        ms1_ready = sem("ms1_ready")
        xn_ready = sem("xn_ready")
        z_ready = sem("z_ready")
        e_ready = sem("e_ready")
        half_ready = sem("half_ready")
        a0_ready = sem("a0_ready")
        a0_used = sem("a0_used")
        a1_used = sem("a1_used")
        dlt_ready = sem("dlt_ready")
        ge_ready = sem("ge_ready")
        gs_ready = sem("gs_ready")
        gx_ready = sem("gx_ready")
        gb1_ready = sem("gb1_ready")
        ys_ready = sem("ys_ready")
        acc_ready = sem("acc_ready")
        stored = sem("stored")
        dve_step = sem("dve_step")
        pool_step = sem("pool_step")

        def chain(eng, step):
            done = [0]

            def link(ins):
                done[0] += 1
                ins.then_inc(step, 1)
                eng.wait_ge(step, done[0])
            return link

        def run(handlers):
            for part, n, stage, i in plan:
                f = handlers.get((part, stage))
                if f:
                    f(n, i)

        def flat(ap):
            letters = "abcdefg"[:len(ap.shape) - 1]
            return ap.rearrange(f"p {' '.join(letters)} -> p ({' '.join(letters)})") if len(letters) > 1 else ap

        block = ctx.enter_context(nc.Block())
        SMALL = 9

        @block.sync
        def _(sp):
            for t in range(TILES):
                sp.dma_start(X[:, t, :], x[t * P:(t + 1) * P, :]).then_inc(ld_x[t], 16)
                if t == 0:
                    sp.dma_start(C[:, :, :], ctx_in.rearrange("(t p) d -> p t d", p=P)).then_inc(ld_c, 16)
                if t == 1:
                    for half in range(2):
                        sp.dma_start(CD[half * S:(half + 1) * S, :, :],
                                     ctx_in.rearrange("(b s) d -> s b d", s=S)).then_inc(ld_cd, 16)
            sp.dma_start(WR0[:, :, :], wr0).then_inc(ld_f0, 16)
            for e in range(E0):
                sp.dma_start(WF0[:, e, :, :], wf0[:, e, :, :]).then_inc(ld_f0, 16)
                sp.dma_start(WP0[:, e, :, :], wp0[:, e, :, :]).then_inc(ld_p0, 16)
            sp.dma_start(CT[:, :], ctxT).then_inc(ld_a1, 16)
            sp.dma_start(WKV1[:, :], wkv1).then_inc(ld_a1, 16)
            sp.dma_start(WQ1[:, :, :], wq1).then_inc(ld_a1, 16)
            sp.dma_start(WO1[:, :, :], wo1).then_inc(ld_a1, 16)
            sp.dma_start(W1[:, :, :], w1).then_inc(ld_w, 16)
            sp.dma_start(W2[:, :, :], w2).then_inc(ld_w, 16)
            for t in range(TILES):
                read_out(sp, "ffn1", t // 2, "o", t % 2)
                sp.dma_start(out[t * P:(t + 1) * P, :], X[:, t, :]).then_inc(stored, 16)
            sp.wait_ge(stored, 16 * TILES)

        @block.scalar
        def _(act):
            for dst, src in ((DW[:, :, :], down_w), (DB[:, :], down_b), (UW[:, :], up_w), (BR[:, :, :], bias_rows),
                             (RW[:, :, :], router_w), (RR[:, :, :], router_rows), (CW[:, :, :], core_w),
                             (B1[:, :], b1), (B2[:, :], b2)):
                act.dma_start(dst, src).then_inc(ld_small, 16)

            def evacuate(part, stage, dst, src):
                def f(n, i):
                    b, done = filled(act, part, n, stage, i)
                    nc.scalar.copy(dst(n, i), src(b, i)).then_inc(done, 1)
                return {(part, stage): f}

            def heads(b, rows, k):
                return b[:, :].bitcast(bf16)[0:rows, 0:k * P].rearrange("p (n c) -> p n c", c=P)

            h = {}
            h |= evacuate("attn0", "q", lambda t, i: QT[:, t % 2, 8 * i:8 * i + 8, :], lambda b, i: heads(b, P, 8))
            h |= evacuate("attn0", "m", lambda t, i: MT[:, t % 2, :, :], lambda b, i: heads(b, 64, 2))
            h |= evacuate("attn0", "o", lambda t, i: flat(OT[:, t % 2, :, :]), lambda b, i: b[:, :])
            h |= evacuate("attn1", "x", lambda t, i: flat(XAT[:, t % 2, :, :]), lambda b, i: b[:, 0:D])
            h |= evacuate("attn1", "q", lambda t, i: QT1[:, t % 2, 8 * i:8 * i + 8, :], lambda b, i: heads(b, 96, 8))
            h |= evacuate("attn1", "m", lambda t, i: MT1[:, t % 2, :], lambda b, i: b[:, :].bitcast(bf16)[0:64, 0:P])
            h |= evacuate("attn1", "o", lambda t, i: OT1[:, t % 2, :, i, :],
                          lambda b, i: b[:, 0:256].rearrange("p (h s) -> p h s", s=S))
            h |= evacuate("attn1", "a", lambda t, i: flat(O1T[:, t % 2, :, :]), lambda b, i: b[:, 0:D])
            h |= evacuate("ffn0", "x", lambda g, i: flat(XT0[:, :, :]), lambda b, i: b[:, :])
            h |= evacuate("ffn1", "x", lambda g, i: flat(XT1[:, :, :]), lambda b, i: b[:, :])
            h |= evacuate("ffn1", "g", lambda g, i: GTT[:, :], lambda b, i: b[:, :].bitcast(bf16)[0:32, 0:GT])

            def probs0(t, c):
                b, done = filled(act, "attn0", t, "p", c)
                nc.scalar.activation(flat(PT[:, t % 2, 2 * c:2 * c + 2, :, :]), b[:, :], ACT.Exp,
                                     scale=HD0 ** -0.5).then_inc(done, 1)

            def probs1(t, c):
                b, done = filled(act, "attn1", t, "p", c)
                nc.scalar.activation(flat(PT1[:, t % 2, 8 * c:8 * c + 8, :]), b[:, :], ACT.Exp,
                                     scale=HD1 ** -0.5).then_inc(done, 1)

            def keys1(t, _):
                b, _ = filled(act, "attn1", t, "kv", 0)
                if t >= 2:
                    filled(act, "attn1", t - 2, "o", 1)
                key = b[:, 0:D].rearrange("p (h d) -> p h d", d=HD1)
                nc.scalar.copy(KS1[:, t % 2, :, 0, :], key).then_inc(kh_ready, 1)
                nc.scalar.copy(KS1[:, t % 2, :, 3, :], key).then_inc(kh_ready, 1)
                nc.scalar.copy(KS1[:, t % 2, :, 5, :], key).then_inc(kh_ready, 1)
                nc.scalar.copy(V1[:, t % 2, :, 0:HD1], b[:, D:2 * D].rearrange("p (h d) -> p h d", d=HD1)
                               ).then_inc(kh_ready, 1)

            def exps(which, e):
                def f(g, _):
                    act.wait_ge(z_ready, ROUTED[which, g])
                    nc.scalar.activation(pr[:, :, 0:e], lg[:, :, 0:e], ACT.Exp).then_inc(e_ready, 1)
                return f

            def half(g, i):
                n = g * BLOCKS0 + i
                b, _ = filled(act, "ffn0", g, "u", i)
                if n >= 2:
                    read_out(act, "ffn0", (n - 2) // BLOCKS0, "u", (n - 2) % BLOCKS0)
                nc.scalar.activation(HH[:, n % 2, :], b[:, :], ACT.Copy, scale=0.5).then_inc(half_ready, 1)

            def top_exp(g, _):
                act.wait_ge(dlt_ready, g + 1)
                nc.scalar.activation(ge[:, :], dlt[:, :], ACT.Exp).then_inc(ge_ready, 1)

            def zero_row(g, _):
                act.wait_ge(ld_small, 16 * SMALL)
                nc.scalar.activation(GB1[:, :], B1[:, :], ACT.Gelu).then_inc(gb1_ready, 1)

            def inner(g, _):
                read_out(act, "ffn1", g, "x", 0)
                if g:
                    filled(act, "ffn1", g - 1, "o", 1)
                nc.scalar.activation(flat(GX[:, :, :]), flat(XT1[:, :, :]), ACT.Gelu).then_inc(gx_ready, 1)
                b, done = filled(act, "ffn1", g, "d", 0)
                nc.scalar.activation(GH[:, :], b[:, 0:GT], ACT.Gelu, bias=DB[:, :]).then_inc(done, 1)

            def hidden(g, i):
                e, c = WORK[i]
                n = g * NCH1 + i
                b, done = filled(act, "ffn1", g, "c", i)
                if n >= 2:
                    chunk_used(act, n - 2)
                ch = FIRST1[e] + c
                nc.scalar.activation(A1[:, n % 2, :], b[:, 0:GT], ACT.Gelu, bias=B1[:, ch:ch + 1]).then_inc(done, 1)

            def expert(g, j):
                b, done = filled(act, "ffn1", g, "y", j)
                if j == 0:
                    if g:
                        filled(act, "ffn1", g - 1, "o", 1)
                    nc.scalar.activation(ACC[:, :], b[:, 0:GT], ACT.Identity, bias=Cb[:, :], scale=0.1
                                         ).then_inc(done, 1)
                    return
                if j > 2:
                    read_out(act, "ffn1", g, "y", j - 2)
                e = EXPERTS[j]
                nc.scalar.activation(YS[:, j % 2, :], b[:, 0:GT], ACT.Identity, bias=Y0n[:, e:e + 1]
                                     ).then_inc(ys_ready, 1)

            run(h | {("attn0", "p"): probs0, ("attn1", "p"): probs1, ("attn1", "kv"): keys1,
                     ("ffn0", "g"): exps("ffn0", E0), ("ffn0", "u"): half, ("ffn1", "e"): exps("ffn1", E1),
                     ("ffn1", "t"): top_exp, ("ffn1", "z"): zero_row, ("ffn1", "d"): inner,
                     ("ffn1", "c"): hidden, ("ffn1", "y"): expert})

        @block.gpsimd
        def _(pool):
            link = chain(pool, pool_step)
            nc.gpsimd.memset(mhalf[:, :], -0.5)
            for m in (KS, identf, identb, maskS, maskT, sel0, sel1):
                nc.gpsimd.memset(flat(m[tuple(slice(None) for _ in m.shape)]), 0.0)
            link(nc.gpsimd.memset(selG[:, :, :], 0.0))
            for m in (identf, identb):
                link(nc.gpsimd.affine_select(out=m[:, :], in_=m[:, :], compare_op=ALU.not_equal, fill=1.0, base=0,
                                             pattern=[[-1, P]], channel_multiplier=1))

            def norm(part):
                def f(n, _):
                    i = LN.index((part, n, "v", 0))
                    src, dst = (vare[:, n % 2, 0:1], rstd[:, n % 2, 0:1]) if part[0] == "a" else (varef[:, :], rstdf[:, :])
                    pool.wait_ge(var_ready, i + 1)
                    nc.gpsimd.tensor_tensor(dst, src, mhalf[:, 0:dst.shape[1]], ALU.pow).then_inc(rstd_ready, 1)
                return f

            def keys0(t, _):
                if t == 0:
                    pool.wait_ge(ld_c, 16)
                if t >= 2:
                    filled(pool, "attn0", t - 2, "k", 0)
                key = C[:, t, :].rearrange("p (k d) -> p k d", d=HD0)
                rest = KR[:, t % 2, :].rearrange("p (k d) -> p k d", d=HD0)

                def slot(s):
                    return KS[:, t % 2, :, s * HD0:(s + 1) * HD0]
                link(nc.gpsimd.tensor_copy(slot(0), key))
                link(nc.gpsimd.tensor_tensor(rest, key, slot(0), ALU.subtract))
                nc.gpsimd.tensor_copy(slot(3), key)
                nc.gpsimd.tensor_copy(slot(5), key)
                link(nc.gpsimd.tensor_copy(slot(1), rest))
                nc.gpsimd.tensor_copy(slot(4), rest)
                nc.gpsimd.tensor_tensor(slot(2), rest, slot(1), ALU.subtract).then_inc(ks_ready, 1)

            def keys1(t, _):
                read_out(pool, "attn1", t, "kv", 0)
                rest = KR1[:, t % 2, :].rearrange("p (h d) -> p h d", d=HD1)
                link(nc.gpsimd.tensor_scalar(KS1[:, t % 2, :, 1, :], rest, 1.0, 0.0, ALU.mult, ALU.add))
                nc.gpsimd.tensor_scalar(KS1[:, t % 2, :, 4, :], rest, 1.0, 0.0, ALU.mult, ALU.add)
                nc.gpsimd.tensor_tensor(KS1[:, t % 2, :, 2, :], rest, KS1[:, t % 2, :, 1, :], ALU.subtract
                                        ).then_inc(ks1_ready, 1)

            def square(g, i):
                n = g * BLOCKS0 + i
                read_out(pool, "ffn0", g, "u", i)
                if n >= 2:
                    block_used(pool, n - 2)
                nc.gpsimd.tensor_tensor(flat(A0[:, n % 2, :, :]), R0[:, n % 2, :], R0[:, n % 2, :], ALU.mult
                                        ).then_inc(a0_ready, 1)

            def first(t, i):
                keys0(t, i)
                norm("attn0")(t, i)
                if t:
                    return
                for part in range(PARTS):
                    link(nc.gpsimd.affine_select(out=sel0[:, :, :, :], in_=sel0[:, :, :, :], compare_op=ALU.not_equal,
                                                 fill=1.0, base=-16 * part, pattern=[[-1, NKV0], [-NKV0, 2], [0, S]],
                                                 channel_multiplier=1))
                    link(nc.gpsimd.affine_select(out=sel1[:, :, :], in_=sel1[:, :, :], compare_op=ALU.not_equal,
                                                 fill=1.0, base=-NH1 * part, pattern=[[-1, NH1], [0, S]],
                                                 channel_multiplier=1))
                    link(nc.gpsimd.affine_select(out=selG[:, :, :], in_=selG[:, :, :], compare_op=ALU.not_equal,
                                                 fill=1.0, base=-E1 * part, pattern=[[-1, E1], [0, P]],
                                                 channel_multiplier=1))
                for b in range(2):
                    rows = slice(b * S, (b + 1) * S)
                    link(nc.gpsimd.affine_select(out=maskS[rows, :], in_=maskS[rows, :], compare_op=ALU.is_ge,
                                                 fill=MASKED, base=0, pattern=[[-1, S]], channel_multiplier=1))
                    link(nc.gpsimd.affine_select(out=maskT[rows, :], in_=maskT[rows, :], compare_op=ALU.is_ge,
                                                 fill=MASKED, base=0, pattern=[[1, S]], channel_multiplier=-1))
                nc.gpsimd.iota(iota8[:, :], pattern=[[1, E1]], base=0, channel_multiplier=0,
                               allow_small_or_imprecise_dtypes=True).then_inc(pool_const, 1)

            run({("attn0", "v"): first, ("attn1", "v"): norm("attn1"), ("ffn0", "v"): norm("ffn0"),
                 ("ffn1", "v"): norm("ffn1"), ("attn1", "kv"): keys1, ("ffn0", "u"): square})

        @block.vector
        def _(dve):
            link = chain(dve, dve_step)

            def setup():
                for m in (QS, MS, MS1, K2, GS):
                    whole = flat(m[tuple(slice(None) for _ in m.shape)])
                    link(nc.vector.memset(whole.bitcast(u32), 0))
                nc.vector.memset(V1[:, :, :, HD1 + 1:32], 0.0)
                link(nc.vector.memset(V1[:, :, :, HD1:HD1 + 1], 1.0))
                link(nc.vector.memset(flat(V2[:, :, :, :, :, :]), 0.0))
                for half in range(2):
                    link(nc.vector.memset(V2[half * S:(half + 1) * S, :, :, :, half, HD0:HD0 + 1].rearrange(
                        "p t b k c -> p (t b k) c"), 1.0))

            def values0(t, _):
                if t == 0:
                    dve.wait_ge(ld_cd, 32)
                if t >= 2:
                    filled(dve, "attn0", t - 2, "o", 0)
                for half in range(2):
                    rows = slice(half * S, (half + 1) * S)
                    nc.vector.tensor_copy(V2[rows, t % 2, :, :, half, 0:HD0], CD[rows, 2 * t:2 * t + 2, :].rearrange(
                        "p b (k d) -> p b k d", d=HD0)).then_inc(v2_ready, 1)

            def variance(part):
                def f(n, _):
                    one = part[0] == "a"
                    tiles = [n] if one else [2 * n, 2 * n + 1]
                    if part == "attn0":
                        dve.wait_ge(ld_x[n], 16)
                    st = [stats[:, n % 2, 0, :]] if one else [statsf[:, k, :] for k in range(2)]
                    m = [mv[:, n % 2, 0, :]] if one else [mvf[:, k, :] for k in range(2)]
                    for k, t in enumerate(tiles):
                        link(nc.vector.bn_stats(st[k], X[:, t, :]))
                    for k, t in enumerate(tiles):
                        link(nc.vector.bn_aggr(m[k], st[k]))
                    src, dst = (mv[:, n % 2, 0:1, 1], vare[:, n % 2, 0:1]) if one else (mvf[:, :, 1], varef[:, :])
                    nc.vector.tensor_scalar(dst, src, EPS, None, ALU.add).then_inc(var_ready, 1)
                return f

            def normed(part, n, k, t, dst):
                m, r = (mv[:, n % 2, 0, 0:1], rstd[:, n % 2, 0:1]) if part[0] == "a" else (mvf[:, k, 0:1], rstdf[:, k:k + 1])
                return nc.vector.tensor_scalar(dst, X[:, t, :], m, r, ALU.subtract, ALU.mult)

            def wait_rstd(part, n):
                dve.wait_ge(rstd_ready, LN.index((part, n, "v", 0)) + 1)

            def queries0(t, _):
                wait_rstd("attn0", t)
                link(normed("attn0", t, 0, t, Q[:, t % 2, :]))
                if t >= 2:
                    filled(dve, "attn0", t - 2, "q", 1)
                q = Q[:, t % 2, :].rearrange("p (h d) -> p h d", d=HD0)
                rest = QR[:, t % 2, :].rearrange("p (h d) -> p h d", d=HD0)
                s = QS[:, t % 2, :, 0:SLOTS * HD0].rearrange("p h (s d) -> p h s d", d=HD0)
                link(nc.vector.tensor_copy(s[:, :, 0:3, :], q.unsqueeze(2).to_broadcast([P, NH0, 3, HD0])))
                link(nc.vector.tensor_tensor(rest, q, s[:, :, 0, :], ALU.subtract))
                link(nc.vector.tensor_copy(s[:, :, 3:5, :], rest.unsqueeze(2).to_broadcast([P, NH0, 2, HD0])))
                nc.vector.tensor_tensor(s[:, :, 5, :], rest, s[:, :, 3, :], ALU.subtract).then_inc(qs_ready, 1)

            def blocks0(t, _):
                b, done = filled(dve, "attn0", t, "k", 0)
                for half in range(2):
                    rows = slice(half * S, (half + 1) * S)
                    ins = nc.vector.tensor_copy(K2[rows, t % 2, :, :, half, :], b[:, :].bitcast(bf16)[rows, :].rearrange(
                        "p (k b t) -> p k b t", k=NKV0, b=2))
                    if half == 0:
                        link(ins)
                ins.then_inc(done, 1)

            def largest(part, each):
                def f(t, c):
                    b, done = filled(dve, part, t, "s", c)
                    nc.vector.tensor_reduce(MN[:, t % 2, each * c:each * c + each], b[:, :].rearrange("p (h t) -> p h t", t=S),
                                            AX.X, ALU.max, negate=True).then_inc(done, 1)
                return f

            def shifts0(t, _):
                read_out(dve, "attn0", t, "s", 3)
                m = MN[:, t % 2, :].rearrange("p (k g h) -> p g h k", g=2, h=2)
                rest = MR[:, t % 2, :].rearrange("p (g h k) -> p g h k", g=2, h=2)
                s = MS[:, t % 2, :, :, :, :]
                link(nc.vector.tensor_copy(s[:, :, 0, :, :], m))
                link(nc.vector.tensor_tensor(rest, m, s[:, :, 0, :, :], ALU.subtract))
                link(nc.vector.tensor_copy(s[:, :, 1, :, :], rest))
                nc.vector.tensor_tensor(s[:, :, 2, :, :], rest, s[:, :, 1, :, :], ALU.subtract).then_inc(ms_ready, 1)

            def shifts1(t, _):
                read_out(dve, "attn1", t, "s", 1)
                m, rest, s = MN[:, t % 2, 0:NH1], MR[:, t % 2, 0:NH1], MS1[:, t % 2, :, :]
                link(nc.vector.tensor_copy(s[:, 0, :], m))
                link(nc.vector.tensor_tensor(rest, m, s[:, 0, :], ALU.subtract))
                link(nc.vector.tensor_copy(s[:, 1, :], rest))
                nc.vector.tensor_tensor(s[:, 2, :], rest, s[:, 1, :], ALU.subtract).then_inc(ms1_ready, 1)

            def result0(t, _):
                b, done = filled(dve, "attn0", t, "n", 0)
                N = b[:, :].rearrange("p (h x) -> p h x", x=16)
                link(nc.vector.reciprocal(rec[:, t % 2, :], N[:, :, HD0]))
                link(nc.vector.tensor_tensor(O0[:, t % 2, :].rearrange("p (h d) -> p h d", d=HD0), N[:, :, 0:HD0],
                                             rec[:, t % 2, :].unsqueeze(2).to_broadcast([P, NH0, HD0]), ALU.mult))
                for half in range(2):
                    xh = X[:, t, half * P:(half + 1) * P].rearrange("p (k g r) -> p g k r", k=4, g=2)
                    o = O0[:, t % 2, half * P:(half + 1) * P].rearrange("p (g k r) -> p g k r", k=4, g=2)
                    ins = nc.vector.tensor_tensor(xh, xh, o, ALU.add)
                    if half == 0:
                        link(ins)
                ins.then_inc(done, 1)
                read_out(dve, "attn0", t, "n", 0)

            def keys1(t, _):
                b, done = filled(dve, "attn1", t, "kv", 0)
                dve.wait_ge(kh_ready, 4 * t + 4)
                if t >= 2:
                    dve.wait_ge(ks1_ready, t - 1)
                nc.vector.tensor_tensor(KR1[:, t % 2, :].rearrange("p (h d) -> p h d", d=HD1),
                                        b[:, 0:D].rearrange("p (h d) -> p h d", d=HD1), KS1[:, t % 2, :, 0, :],
                                        ALU.subtract).then_inc(done, 1)

            def rows1(t, _):
                wait_rstd("attn1", t)
                if t >= 2:
                    filled(dve, "attn1", t - 2, "x", 0)
                normed("attn1", t, 0, t, XA[:, t % 2, :]).then_inc(xa_ready, 1)

            def queries1(t, _):
                b, done = filled(dve, "attn1", t, "w", 0)
                if t >= 2:
                    filled(dve, "attn1", t - 2, "q", 1)
                q = b[:, 0:D].rearrange("p (h d) -> p h d", d=HD1)
                rest = QR1[:, t % 2, :].rearrange("p (h d) -> p h d", d=HD1)
                s = QS1[:, t % 2, :, :, :]
                link(nc.vector.tensor_copy(s[:, :, 0:3, :], q.unsqueeze(2).to_broadcast([P, NH1, 3, HD1])))
                nc.vector.tensor_tensor(rest, q, s[:, :, 0, :], ALU.subtract).then_inc(done, 1)
                read_out(dve, "attn1", t, "w", 0)
                link(nc.vector.tensor_copy(s[:, :, 3:5, :], rest.unsqueeze(2).to_broadcast([P, NH1, 2, HD1])))
                nc.vector.tensor_tensor(s[:, :, 5, :], rest, s[:, :, 3, :], ALU.subtract).then_inc(qs1_ready, 1)

            def turned_keys1(t, i):
                b, done = filled(dve, "attn1", t, "k", i)
                nc.vector.tensor_copy(KT1[:, t % 2, 8 * i:8 * i + 8, :],
                                      b[:, :].bitcast(bf16)[0:96, :].rearrange("p (n c) -> p n c", c=P)).then_inc(done, 1)

            def divide1(t, _):
                b, done = filled(dve, "attn1", t, "n", 0)
                N = b[:, :].rearrange("p (h x) -> p h x", x=32)
                link(nc.vector.reciprocal(rec[:, t % 2, 0:NH1], N[:, :, HD1]))
                nc.vector.tensor_tensor(O1[:, t % 2, :].rearrange("p (h d) -> p h d", d=HD1), N[:, :, 0:HD1],
                                        rec[:, t % 2, 0:NH1].unsqueeze(2).to_broadcast([P, NH1, HD1]), ALU.mult
                                        ).then_inc(done, 1)

            def result1(t, _):
                b, done = filled(dve, "attn1", t, "r", 0)
                nc.vector.tensor_tensor(X[:, t, :], b[:, 0:D], X[:, t, :], ALU.add).then_inc(done, 1)
                read_out(dve, "attn1", t, "r", 0)

            def rows(part):
                def f(g, _):
                    wait_rstd(part, g)
                    i = TURNS.index((part, g, "x", 0))
                    if i:
                        filled(dve, *TURNS[i - 1])
                    for k, t in enumerate((2 * g, 2 * g + 1)):
                        normed(part, g, k, t, XN[:, k, :]).then_inc(xn_ready, 1)
                return f

            def less_max(e):
                link(nc.vector.tensor_reduce(lmax[:, :], lg[:, :, 0:e], AX.X, ALU.max))
                nc.vector.tensor_tensor(lg[:, :, 0:e], lg[:, :, 0:e], lmax[:, :].unsqueeze(2).to_broadcast([P, 2, e]),
                                        ALU.subtract).then_inc(z_ready, 1)

            def softmax(which, g, e):
                dve.wait_ge(e_ready, ROUTED[which, g])
                link(nc.vector.tensor_reduce(lsum[:, :], pr[:, :, 0:e], AX.X, ALU.add))
                link(nc.vector.reciprocal(lsum[:, :], lsum[:, :]))
                link(nc.vector.tensor_tensor(pr[:, :, 0:e], pr[:, :, 0:e], lsum[:, :].unsqueeze(2).to_broadcast([P, 2, e]),
                                             ALU.mult))

            def logits0(g, _):
                b, done = filled(dve, "ffn0", g, "r", 0)
                nc.vector.tensor_copy(lg[:, :, 0:E0], b[:, 0:2 * E0].rearrange("p (t e) -> p t e", e=E0)).then_inc(done, 1)
                read_out(dve, "ffn0", g, "r", 0)
                less_max(E0)

            def gates0(g, _):
                softmax("ffn0", g, E0)
                nc.vector.tensor_tensor(G0[:, :, 0], pr[:, :, 0], pr[:, :, 1], ALU.is_ge)
                link(nc.vector.tensor_tensor(G0[:, :, 1], pr[:, :, 1], pr[:, :, 0], ALU.is_gt))
                link(nc.vector.tensor_tensor(G0[:, :, :], G0[:, :, :], pr[:, :, 0:E0], ALU.mult))

            def leaky(g, i):
                n = g * BLOCKS0 + i
                dve.wait_ge(half_ready, n + 1)
                if n >= 2:
                    dve.wait_ge(a0_ready, n - 1)
                b, done = at("ffn0", g, "u", i), free["H", "dve"]
                nc.vector.tensor_tensor(R0[:, n % 2, :], b[:, :], HH[:, n % 2, :], ALU.max).then_inc(done, 1)

            def result_ffn0(g, k):
                t = 2 * g + k
                b, done = filled(dve, "ffn0", g, "y", k)
                link(nc.vector.scalar_tensor_tensor(X[:, t, :], b[:, 0:D], G0[:, k, 0:1], X[:, t, :], ALU.mult, ALU.add))
                nc.vector.scalar_tensor_tensor(X[:, t, :], b[:, D:2 * D], G0[:, k, 1:2], X[:, t, :], ALU.mult, ALU.add
                                               ).then_inc(done, 1)
                read_out(dve, "ffn0", g, "y", k)

            def logits1(g, _):
                if g == 0:
                    dve.wait_ge(ld_small, 16 * SMALL)
                    link(nc.vector.tensor_tensor(rbias[:, :], RR[:, 0, :], RR[:, 1, :], ALU.subtract))
                    link(nc.vector.tensor_tensor(obias[:, :], BR[:, 0, :], BR[:, 1, :], ALU.add))
                b, done = filled(dve, "ffn1", g, "r", 0)
                nc.vector.tensor_tensor(lg[:, :, :], b[:, 0:2 * E1].rearrange("p (t e) -> p t e", e=E1),
                                        rbias[:, :].unsqueeze(1).to_broadcast([P, 2, E1]), ALU.add).then_inc(done, 1)
                read_out(dve, "ffn1", g, "r", 0)
                less_max(E1)

            def two_largest(g, _):
                softmax("ffn1", g, E1)
                if g == 0:
                    dve.wait_ge(pool_const, 1)
                for k in range(2):
                    link(nc.vector.max(top[:, k, :], pr[:, k, :]))
                nc.vector.tensor_tensor(dlt[:, :], top[:, :, 1], top[:, :, 0], ALU.subtract).then_inc(dlt_ready, 1)
                for k in range(2):
                    link(nc.vector.max_index(topi[:, k, :], top[:, k, :], pr[:, k, :]))
                link(nc.vector.tensor_copy(topf[:, :, :], topi[:, :, :]))

            def gates1(g, _):
                dve.wait_ge(ge_ready, g + 1)
                link(nc.vector.tensor_scalar(lsum[:, :], ge[:, :], 1.0, None, ALU.add))
                link(nc.vector.reciprocal(gk[:, :, 0], lsum[:, :]))
                link(nc.vector.tensor_tensor(gk[:, :, 1], gk[:, :, 0], ge[:, :], ALU.mult))
                for k in range(2):
                    nc.vector.tensor_scalar(oh[:, k, :], iota8[:, :], topf[:, k, 0:1], gk[:, k, 0:1],
                                            ALU.is_equal, ALU.mult)
                    link(nc.vector.tensor_scalar(gate[:, k, :], iota8[:, :], topf[:, k, 1:2], gk[:, k, 1:2],
                                                 ALU.is_equal, ALU.mult))
                link(nc.vector.tensor_tensor(gate[:, :, :], gate[:, :, :], oh[:, :, :], ALU.add))
                link(nc.vector.tensor_copy(GS[:, :, 0, :], gate[:, :, :]))
                link(nc.vector.tensor_tensor(GR[:, :, :], gate[:, :, :], GS[:, :, 0, :], ALU.subtract))
                link(nc.vector.tensor_copy(GS[:, :, 1, :], GR[:, :, :]))
                nc.vector.tensor_tensor(GS[:, :, 2, :], GR[:, :, :], GS[:, :, 1, :], ALU.subtract).then_inc(gs_ready, 1)

            def zero_row(g, _):
                b, done = filled(dve, "ffn1", g, "z", 0)
                link(nc.vector.tensor_reduce(Cb[:, :], b[:, 0:E1], AX.X, ALU.add))
                link(nc.vector.tensor_reduce(lsum[:, 0:1], B2[:, 0:E1], AX.X, ALU.add))
                link(nc.vector.tensor_tensor(Cb[:, :], Cb[:, :], lsum[:, 0:1], ALU.add))
                link(nc.vector.scalar_tensor_tensor(Cb[:, :], B2[:, E1:E1 + 1], 0.1, Cb[:, :], ALU.mult, ALU.add))
                nc.vector.tensor_scalar(Y0n[:, :], b[:, 0:E1], -1.0, None, ALU.mult).then_inc(done, 1)

            def expert(g, j):
                if j == 0:
                    read_out(dve, "ffn1", g, "y", 0)
                    return
                n = g * E1 + j
                dve.wait_ge(ys_ready, n)
                b = at("ffn1", g, "y", j)
                nc.vector.tensor_tensor(YG[:, j % 2, :], YS[:, j % 2, :], b[:, GT:2 * GT], ALU.mult
                                        ).then_inc(free["Y", "dve"], 1)
                read_out(dve, "ffn1", g, "y", j)
                add = nc.vector.tensor_tensor(ACC[:, :], ACC[:, :], YG[:, j % 2, :], ALU.add)
                if j < E1:
                    link(add)
                else:
                    add.then_inc(acc_ready, 1)

            def result_ffn1(g, k):
                if k == 0:
                    for t in (2 * g, 2 * g + 1):
                        link(nc.vector.tensor_tensor(X[:, t, :], X[:, t, :], obias[:, :], ALU.add))
                t = 2 * g + k
                b, done = filled(dve, "ffn1", g, "o", k)
                nc.vector.tensor_tensor(X[:, t, :], b[:, 0:D], X[:, t, :], ALU.add).then_inc(done, 1)

            var0 = variance("attn0")

            def first(t, i):
                var0(t, i)
                if t == 0:
                    setup()

            def late(t, i):
                if i == 0:
                    values0(t, i)
                largest("attn0", 8)(t, i)

            run({("attn0", "v"): first, ("attn0", "ln"): queries0, ("attn0", "k"): blocks0,
                 ("attn0", "s"): late, ("attn0", "m"): shifts0, ("attn0", "n"): result0,
                 ("attn1", "v"): variance("attn1"), ("attn1", "kv"): keys1, ("attn1", "ln"): rows1,
                 ("attn1", "w"): queries1, ("attn1", "k"): turned_keys1, ("attn1", "s"): largest("attn1", 8),
                 ("attn1", "m"): shifts1, ("attn1", "n"): divide1, ("attn1", "r"): result1,
                 ("ffn0", "v"): variance("ffn0"), ("ffn0", "ln"): rows("ffn0"), ("ffn0", "r"): logits0,
                 ("ffn0", "g"): gates0, ("ffn0", "u"): leaky, ("ffn0", "y"): result_ffn0,
                 ("ffn1", "v"): variance("ffn1"), ("ffn1", "ln"): rows("ffn1"), ("ffn1", "r"): logits1,
                 ("ffn1", "e"): two_largest, ("ffn1", "t"): gates1, ("ffn1", "z"): zero_row,
                 ("ffn1", "y"): expert, ("ffn1", "o"): result_ffn1})

        @block.tensor
        def _(pe):
            def mm(o, a, b, start=True, stop=True, shared=False):
                return nc.tensor.matmul(o, a, b, start=start, stop=stop, skip_group_check=shared)

            def turn_queries0(t, i):
                b, done = claim(pe, "attn0", t, "q", i)
                if i == 0:
                    pe.wait_ge(qs_ready, t + 1)
                for p in range(8):
                    pair_ = 8 * i + p
                    ins = nc.tensor.transpose(b[:, :].bitcast(bf16)[:, p * P:(p + 1) * P],
                                              flat(QS[:, t % 2, 2 * pair_:2 * pair_ + 2, :]), identb[:, :])
                ins.then_inc(done, 1)

            def turn_keys0(t, _):
                b, done = claim(pe, "attn0", t, "k", 0)
                pe.wait_ge(ks_ready, t + 1)
                for kv in range(NKV0):
                    for half in range(2):
                        ins = nc.tensor.transpose(b[:, :].bitcast(bf16)[half * S:(half + 1) * S, kv * P:(kv + 1) * P],
                                                  KS[:, t % 2, kv, :], identb[:, :])
                ins.then_inc(done, 1)

            def scores0(t, c):
                b, done = claim(pe, "attn0", t, "s", c)
                if c == 0:
                    read_out(pe, "attn0", t, "k", 0)
                read_out(pe, "attn0", t, "q", c // 2)
                for i in range(4):
                    pair_ = 4 * c + i
                    for bt in range(2):
                        ins = mm(b[bt * S:(bt + 1) * S, i * P:(i + 1) * P], QT[:, t % 2, pair_, bt * S:(bt + 1) * S],
                                 flat(K2[:, t % 2, pair_ // 2, bt, :, :]))
                ins.then_inc(done, 1)

            def turn_shifts0(t, _):
                b, done = claim(pe, "attn0", t, "m", 0)
                pe.wait_ge(ms_ready, t + 1)
                for gp in range(2):
                    ins = nc.tensor.transpose(b[:, :].bitcast(bf16)[0:64, gp * P:(gp + 1) * P],
                                              flat(MS[:, t % 2, gp, :, :, :]), identb[:, :])
                ins.then_inc(done, 1)

            def probs0(t, c):
                if t == 0 and c == 0:
                    pe.wait_ge(pool_const, 1)
                b, done = claim(pe, "attn0", t, "p", c)
                if c == 0:
                    read_out(pe, "attn0", t, "m", 0)
                for i in range(2):
                    kv = 2 * c + i
                    for bt in range(2):
                        cols = slice(bt * S, (bt + 1) * S)
                        o = b[:, (2 * i + bt) * P:(2 * i + bt + 1) * P]
                        mm(o, flat(sel0[:, kv, :, :]), MT[:, t % 2, :, cols], stop=False)
                        ins = mm(o, flat(K2[:, t % 2, kv, bt, :, :]), QT[:, t % 2, 2 * kv:2 * kv + 2, cols], start=False)
                ins.then_inc(done, 1)

            def values0(t, _):
                b, done = claim(pe, "attn0", t, "o", 0)
                pe.wait_ge(v2_ready, 2 * t + 2)
                read_out(pe, "attn0", t, "p", 3)
                o = b[:, :].rearrange("p (h g b s) -> p h g b s", h=2, g=2, b=2)
                for kh in range(2):
                    for bt in range(2):
                        for k4 in range(4):
                            kv = 4 * kh + k4
                            ins = mm(o[32 * k4:32 * k4 + 32, kh, :, bt, :], flat(V2[:, t % 2, bt, kv, :, :]),
                                     PT[:, t % 2, kv, bt, :])
                ins.then_inc(done, 1)

            def turn_back(part, src):
                def f(t, _):
                    b, done = claim(pe, part, t, "n", 0)
                    read_out(pe, part, t, "o", 0 if part == "attn0" else 1)
                    for i in range(4):
                        o = src[:, t % 2, i]
                        o = o if len(o.shape) == 2 else flat(o)
                        ins = nc.tensor.transpose(b[:, i * P:(i + 1) * P], o, identf[:, :])
                    ins.then_inc(done, 1)
                return f

            def turn_two(stage, src, wait):
                def f(t, _):
                    b, done = claim(pe, "attn1", t, stage, 0)
                    wait(t)
                    for dc in range(DC):
                        ins = nc.tensor.transpose(b[:, dc * P:(dc + 1) * P], src[:, t % 2, dc * P:(dc + 1) * P], identf[:, :])
                    ins.then_inc(done, 1)
                return f

            def project(stage, src, w, before):
                def f(t, _):
                    b, done = claim(pe, "attn1", t, stage, 0)
                    read_out(pe, "attn1", t, before, 0)
                    if t == 0:
                        pe.wait_ge(ld_a1, 16 * 4)
                    for dc in range(DC):
                        ins = mm(b[:, 0:D], src[:, t % 2, dc, :], w[:, dc, :], start=(dc == 0), stop=(dc == DC - 1))
                    ins.then_inc(done, 1)
                return f

            def keys_values1(t, _):
                b, done = claim(pe, "attn1", t, "kv", 0)
                if t == 0:
                    pe.wait_ge(ld_a1, 16 * 4)
                mm(b[:, :], CT[:, t * P:(t + 1) * P], WKV1[:, :]).then_inc(done, 1)

            def turn_heads1(stage, src, ready):
                def f(t, i):
                    b, done = claim(pe, "attn1", t, stage, i)
                    if i == 0:
                        pe.wait_ge(ready, t + 1)
                    for h in range(8):
                        ins = nc.tensor.transpose(b[:, :].bitcast(bf16)[0:96, h * P:(h + 1) * P],
                                                  flat(src[:, t % 2, 8 * i + h, :, :]), identb[:, :])
                    ins.then_inc(done, 1)
                return f

            def scores1(t, c):
                b, done = claim(pe, "attn1", t, "s", c)
                read_out(pe, "attn1", t, "k", c)
                read_out(pe, "attn1", t, "q", c)
                mm(b[:, :], identb[:, :], maskS[:, :].unsqueeze(1).to_broadcast([P, 8, S]), stop=False, shared=True)
                for h in range(8):
                    for bt in range(2):
                        rows = slice(bt * S, (bt + 1) * S)
                        ins = mm(b[rows, h * S:(h + 1) * S], QT1[:, t % 2, 8 * c + h, rows], KT1[:, t % 2, 8 * c + h, rows],
                                 start=False, shared=True)
                ins.then_inc(done, 1)

            def turn_shifts1(t, _):
                b, done = claim(pe, "attn1", t, "m", 0)
                pe.wait_ge(ms1_ready, t + 1)
                nc.tensor.transpose(b[:, :].bitcast(bf16)[0:64, 0:P], flat(MS1[:, t % 2, :, :]), identb[:, :]
                                    ).then_inc(done, 1)

            def probs1(t, c):
                b, done = claim(pe, "attn1", t, "p", c)
                if c == 0:
                    read_out(pe, "attn1", t, "m", 0)
                mm(b[:, :], identb[:, :], maskT[:, :].unsqueeze(1).to_broadcast([P, 8, S]), stop=False, shared=True)
                for h in range(8):
                    for bt in range(2):
                        rows = slice(bt * S, (bt + 1) * S)
                        o = b[rows, h * S:(h + 1) * S]
                        mm(o, sel1[:, 8 * c + h, :], MT1[:, t % 2, rows], start=False, shared=True)
                        ins = mm(o, KT1[:, t % 2, 8 * c + h, rows], QT1[:, t % 2, 8 * c + h, rows], start=False, shared=True)
                ins.then_inc(done, 1)

            def values1(t, bt):
                b, done = claim(pe, "attn1", t, "o", bt)
                if bt == 0:
                    read_out(pe, "attn1", t, "p", 1)
                rows = slice(bt * S, (bt + 1) * S)
                for hq in range(4):
                    for h4 in range(4):
                        h = 4 * hq + h4
                        ins = mm(b[32 * h4:32 * h4 + 32, hq * S:(hq + 1) * S], V1[rows, t % 2, h, :], PT1[rows, t % 2, h, :])
                ins.then_inc(done, 1)

            def turn_rows(part):
                def f(g, _):
                    b, done = claim(pe, part, g, "x", 0)
                    i = TURNS.index((part, g, "x", 0))
                    for k in range(2):
                        pe.wait_ge(xn_ready, 2 * i + k + 1)
                        for dc in range(DC):
                            ins = nc.tensor.transpose(b[:, dc * GT + k * P:dc * GT + (k + 1) * P],
                                                      XN[:, k, dc * P:(dc + 1) * P], identf[:, :])
                    ins.then_inc(done, 1)
                return f

            def route(part, xt, w, e):
                def f(g, _):
                    b, done = claim(pe, part, g, "r", 0)
                    read_out(pe, part, g, "x", 0)
                    if g == 0:
                        pe.wait_ge(*((ld_f0, 16 * 3) if part == "ffn0" else (ld_small, 16 * SMALL)))
                    for k in range(2):
                        for dc in range(DC):
                            ins = mm(b[:, k * e:(k + 1) * e], xt[:, dc, k * P:(k + 1) * P], w[:, dc, :],
                                     start=(dc == 0), stop=(dc == DC - 1))
                    ins.then_inc(done, 1)
                return f

            def up0(g, i):
                b, done = claim(pe, "ffn0", g, "u", i)
                e, c0 = divmod(2 * i, K0)
                for c in range(2):
                    for dc in range(DC):
                        ins = mm(b[:, c * GT:(c + 1) * GT], WF0[:, e, dc, (c0 + c) * P:(c0 + c + 1) * P], XT0[:, dc, :],
                                 start=(dc == 0), stop=(dc == DC - 1))
                ins.then_inc(done, 1)

            def down0(g, i):
                n = g * BLOCKS0 + i
                e, c0 = divmod(2 * i, K0)
                if i == 0:
                    for k in range(2):
                        claim(pe, "ffn0", g, "y", k)
                    if g == 0:
                        pe.wait_ge(ld_p0, 16 * 2)
                pe.wait_ge(a0_ready, n + 1)
                for k in range(2):
                    for c in range(2):
                        ins = mm(at("ffn0", g, "y", k)[:, e * D:(e + 1) * D], A0[:, n % 2, c, k * P:(k + 1) * P],
                                 WP0[:, e, c0 + c, :], start=(c0 + c == 0), stop=(c0 + c == K0 - 1))
                    if i == BLOCKS0 - 1:
                        ins.then_inc(full["Y"], 1)
                if i < BLOCKS0 - 1:
                    ins.then_inc(a0_used, 1)

            def turn_gates(g, _):
                b, done = claim(pe, "ffn1", g, "g", 0)
                pe.wait_ge(gs_ready, g + 1)
                for k in range(2):
                    ins = nc.tensor.transpose(b[:, :].bitcast(bf16)[0:32, k * P:(k + 1) * P], flat(GS[:, k, :, :]),
                                              identb[:, :])
                ins.then_inc(done, 1)

            def narrow(g, _):
                b, done = claim(pe, "ffn1", g, "d", 0)
                for dc in range(DC):
                    ins = mm(b[:, 0:GT], DW[:, dc, :], XT1[:, dc, :], start=(dc == 0), stop=(dc == DC - 1))
                ins.then_inc(done, 1)

            def zero_row(g, _):
                b, done = claim(pe, "ffn1", g, "z", 0)
                pe.wait_ge(ld_w, 32)
                pe.wait_ge(gb1_ready, 1)
                for e in range(E1):
                    for c in range(CH1[e]):
                        ch = FIRST1[e] + c
                        ins = mm(b[:, e:e + 1], W2[:, ch, :], GB1[:, ch:ch + 1], start=(c == 0), stop=(c == CH1[e] - 1))
                ins.then_inc(done, 1)

            def up1(g, i):
                e, c = WORK[i]
                b, done = claim(pe, "ffn1", g, "c", i)
                if i == 0:
                    read_out(pe, "ffn1", g, "d", 0)
                mm(b[:, 0:GT], W1[:, FIRST1[e] + c, :], GH[:, :]).then_inc(done, 1)

            def down1(g, i):
                e, c = WORK[i]
                y = ("ffn1", g, "y", EXPERTS.index(e))
                read_out(pe, "ffn1", g, "c", i)
                if c == 0:
                    b, _ = claim(pe, *y)
                    if e < E1:
                        mm(b[:, GT:2 * GT], selG[:, e, :], GTT[:, :])
                last_c = c == CH1[e] - 1
                ins = mm(at(*y)[:, 0:GT], W2[:, FIRST1[e] + c, :], A1[:, (g * NCH1 + i) % 2, :], start=(c == 0), stop=last_c)
                ins.then_inc(full["Y"] if last_c else a1_used, 1)

            def widen(g, k):
                b, done = claim(pe, "ffn1", g, "o", k)
                if k == 0:
                    pe.wait_ge(gx_ready, g + 1)
                for dc in range(DC):
                    mm(b[:, 0:D], GX[:, dc, k * P:(k + 1) * P], CW[:, dc, :], start=(dc == 0), stop=False)
                if k == 0:
                    pe.wait_ge(acc_ready, g + 1)
                mm(b[:, 0:D], ACC[:, k * P:(k + 1) * P], UW[:, :], start=False).then_inc(done, 1)

            pe.wait_ge(pool_step, 3)
            run({("attn0", "q"): turn_queries0, ("attn0", "k"): turn_keys0, ("attn0", "s"): scores0,
                 ("attn0", "m"): turn_shifts0, ("attn0", "p"): probs0, ("attn0", "o"): values0,
                 ("attn0", "n"): turn_back("attn0", OT),
                 ("attn1", "kv"): keys_values1, ("attn1", "x"): turn_two("x", XA, lambda t: pe.wait_ge(xa_ready, t + 1)),
                 ("attn1", "w"): project("w", XAT, WQ1, "x"), ("attn1", "q"): turn_heads1("q", QS1, qs1_ready),
                 ("attn1", "k"): turn_heads1("k", KS1, ks1_ready), ("attn1", "s"): scores1,
                 ("attn1", "m"): turn_shifts1, ("attn1", "p"): probs1, ("attn1", "o"): values1,
                 ("attn1", "n"): turn_back("attn1", OT1),
                 ("attn1", "a"): turn_two("a", O1, lambda t: read_out(pe, "attn1", t, "n", 0)),
                 ("attn1", "r"): project("r", O1T, WO1, "a"),
                 ("ffn0", "x"): turn_rows("ffn0"), ("ffn0", "r"): route("ffn0", XT0, WR0, E0), ("ffn0", "u"): up0,
                 ("ffn0", "d"): down0, ("ffn1", "x"): turn_rows("ffn1"), ("ffn1", "r"): route("ffn1", XT1, RW, E1),
                 ("ffn1", "g"): turn_gates, ("ffn1", "d"): narrow, ("ffn1", "z"): zero_row, ("ffn1", "c"): up1,
                 ("ffn1", "w"): down1, ("ffn1", "o"): widen})


COST_LAMBDA = 1e-07


def kernel(**inputs):
    import numpy as np
    import concourse.bacc as bacc
    from concourse.bass_utils import run_bass_kernel_spmd as run

    a = {n: np.asarray(v) for n, v in inputs.items()}

    def chunks(w):
        return w.reshape(-1, P, w.shape[1]).transpose(1, 0, 2)

    f = "L1_ffn_"
    names = [f"{f}e{e}_" for e in range(E1)] + [f + "shared_"]
    cost = np.array([2 * L * h for h in HIDS], np.float32) * np.float32(COST_LAMBDA)
    arrays = {
        "x": a["x"].reshape(B * S, D),
        "ctx_in": a["ctx_512"].reshape(B * S, CTX),
        "ctxT": a["ctx_512"].reshape(B * S, CTX).T,
        "wr0": chunks(a["L0_ffn_w_router"].T),
        "wf0": a["L0_ffn_w_fc"].reshape(E0, HID0, DC, P).transpose(3, 0, 2, 1),
        "wp0": a["L0_ffn_w_proj"].reshape(E0, D, K0, P).transpose(3, 0, 2, 1),
        "wq1": chunks(a["L1_xattn_Wq"].T),
        "wkv1": a["L1_xattn_Wkv_expand"].T,
        "wo1": chunks(a["L1_xattn_Wout"].T),
        "down_w": chunks(a[f + "down_w"]),
        "down_b": a[f + "down_b"].reshape(L, 1),
        "up_w": a[f + "up_w"],
        "bias_rows": np.broadcast_to(np.stack([a[f + "up_b"], a[f + "core_b"]]), (P, 2, D)),
        "router_w": chunks(a[f + "router_w"]),
        "router_rows": np.broadcast_to(np.stack([a[f + "router_b"], cost]), (P, 2, E1)),
        "core_w": chunks(a[f + "core_w"]),
        "w1": np.concatenate([a[n + ("w1")] for n in names], 1).reshape(L, NCH1, P),
        "b1": np.concatenate([a[n + "b1"] for n in names]).reshape(NCH1, P).T,
        "w2": chunks(np.concatenate([a[n + "w2"] for n in names], 0)),
        "b2": np.stack([a[n + "b2"] for n in names], 1),
    }
    nc = bacc.Bacc("TRN2", target_bir_lowering=False, num_devices=1)
    feed, args = {}, []
    for name, v in arrays.items():
        v = np.ascontiguousarray(v)
        feed[f"in_{name}"] = v
        args.append(nc.dram_tensor(f"in_{name}", v.shape, mybir.dt.from_np(v.dtype), kind="ExternalInput").ap())
    args.append(nc.dram_tensor("out_dram", (B * S, D), fp32, kind="ExternalOutput").ap())
    mixed_network(nc, *args)
    r = run(nc, [feed], core_ids=[0])
    return r.results[0]["out_dram"].reshape(B, S, D)
```

```python
import concourse.bass as bass
from concourse import mybir
from contextlib import ExitStack

fp32 = mybir.dt.float32
bf16 = mybir.dt.bfloat16
u32 = mybir.dt.uint32
ALU = mybir.AluOpType
ACT = mybir.ActivationFunctionType
AX = mybir.AxisListType

P = 128
B, S, D = 16, 64, 256
TILES = B * S // P
GROUPS = TILES // 2
GT = 2 * P
DC = D // P
CTX = 64
NH0, NKV0, HD0 = 32, 8, 8
NH1, HD1 = 16, 16
E0, HID0 = 2, 1024
K0 = HID0 // P
L = 128
HIDS = [128, 256, 384, 512, 128, 256, 384, 512]
E1 = len(HIDS)
CH1 = [h // P for h in HIDS] + [1]
FIRST1 = [sum(CH1[:e]) for e in range(E1 + 1)]
NCH1 = sum(CH1)
EPS = 1e-5
MASKED = -3.0e38
PARTS = 3
SLOTS = 6


BLOCKS0 = E0 * K0 // 2
EXPERTS = [E1] + list(range(E1))
WORK = [(e, c) for e in EXPERTS for c in range(CH1[e])]


def stages(part, n, *names):
    out = []
    for name in names:
        name, _, times = name.partition("*")
        out += [(part, n, name, i) for i in range(int(times or 1))]
    return out


def queries_part(t):
    return stages("attn0", t, "v", "ln")


def scores_part(t):
    e, p = stages("attn0", t, "e*4"), stages("attn0", t, "p*4")
    return stages("attn0", t, "q*2", "k", "s*4") + [e[0], e[1], p[0], e[2], p[1], e[3], p[2], p[3]]


def values_part(t):
    return stages("attn0", t, "o", "n")


def keys_part(t):
    return stages("attn1", t, "kv", "k*2")


def attn1(t):
    return stages("attn1", t, "v", "ln", "x", "w", "q*2", "s*2", "m", "p*2", "o*2", "n", "a", "r")


def ffn0_head(g):
    return stages("ffn0", g, "v", "ln", "x", "r")


def ffn0_up(g):
    return stages("ffn0", g, f"u*{BLOCKS0}")


def ffn0_down(g):
    return stages("ffn0", g, f"d*{BLOCKS0}", "y*2")


def ffn0_gates(g):
    return stages("ffn0", g, "g")


def ffn1_head(g):
    return stages("ffn1", g, "v", "ln", "x", "r", "e", "t", "d")


def zero_rows(g):
    return stages("ffn1", g, "b", f"z*{E1 // 2}")


def ffn1_up(g):
    return stages("ffn1", g, f"c*{NCH1}")


def ffn1_down(g):
    out = []
    for i, (e, c) in enumerate(WORK):
        out.append(("ffn1", g, "w", i))
        if i == 0:
            out.append(("ffn1", g, "g", 0))
        if c == CH1[e] - 1:
            out.append(("ffn1", g, "y", EXPERTS.index(e)))
    return out + stages("ffn1", g, "o*2")


BANKS = {"S": 4, "H": 2, "Y": 2}
FILLS = {(part, s): "S" for part, names in (("attn0", "q k s p o n"), ("attn1", "kv k q s p o x w m n a r"),
                                            ("ffn0", "x r"), ("ffn1", "x r g d z")) for s in names.split()}
FILLS |= {("ffn0", "u"): "H", ("ffn0", "y"): "Y", ("ffn1", "c"): "H", ("ffn1", "y"): "Y", ("ffn1", "o"): "Y"}

COST = {
    "attn0": dict(v="dve .14 pool .86", ln="dve 3.58", q="pe .42 act .52", k="pe .47 dve 1.7",
                 s="pe .45 dve 2.61", e="act .56", p="pe .5 act .43", o="pe .84 act .54", n="pe .55 dve 2.99"),
    "attn1": dict(kv="pe .3 act .59 dve .37 pool 1.3", k="pe .43 dve .4", v="dve 1.2 pool .67", ln="dve .34",
                 x="pe .16 act .42", w="pe 1.51 dve 1.6", q="pe .71 act .65", s="pe .54 dve .64",
                 m="dve .31 pe .17 act .3", p="pe 1 act .54", o="pe .65 act .55", n="pe .31 dve .53",
                 a="pe .27 act 1.39", r="pe .85 dve .51"),
    "ffn0": dict(v="dve .58 pool .97", ln="dve 3.14", x="pe .06 act .36", r="pe .61 dve .41",
                g="act .24 dve .6", u="pe 1.7 act .41 dve .6 pool 1.06", d="pe .85", y="dve .59"),
    "ffn1": dict(v="dve 1.28 pool .62", ln="dve .72", x="pe .19 act .34", r="pe .51 dve .92",
                e="act .11 dve 1.59", t="act .18 dve 7.59", d="pe .59 act 1.18", g="pe 1.43 act .24",
                c="pe .43 act .33", w="pe .41", y="act .45 dve 1.1", o="pe 2.59 dve .09", b="act .1",
                z="pe 2.57 dve .32")}
COST = {part: {s: [(e, float(d)) for e, d in zip(text.split()[::2], text.split()[1::2])] for s, text in costs.items()}
        for part, costs in COST.items()}
LOADED = {("ffn0", "u"): 0, ("attn1", "kv"): 8.0, ("ffn1", "z"): 28.9, ("ffn1", "b"): 10.3}
HANDOFF = 0.188
SLACK = 0.137
URGENCY = {"attn0": 0.0, "attn1": 0.0, "ffn0": 0.0, "ffn0_body": 0.0, "ffn1": 22.1, "ffn1_body": -0.7}
BODY = {("ffn0", "u"), ("ffn0", "d"), ("ffn0", "y"), ("ffn1", "c"), ("ffn1", "w"), ("ffn1", "y"), ("ffn1", "o")}
EXPS = {("attn0", "e"), ("attn1", "p"), ("ffn0", "g"), ("ffn1", "e"), ("ffn1", "t")}


def chains_and_orders():
    chains, after = [], {}

    def order(first, second):
        after.setdefault(second, []).append(first)

    for t in range(TILES):
        chains += [queries_part(t) + scores_part(t) + values_part(t), keys_part(t), attn1(t)]
        order(("attn1", t, "k", 1), ("attn1", t, "w", 0))
        if t:
            for part, names in (("attn0", ("v", "ln", "o")), ("attn1", ("kv", "ln", "w", "m"))):
                for name in names:
                    order((part, t - 1, name, 0), (part, t, name, 0))
            order(("attn0", t - 1, "e", 3), ("attn0", t, "e", 3))
        if t >= 2:
            for part, first, second in (("attn0", ("n", 0), ("q", 0)), ("attn0", ("k", 0), ("v", 0)),
                                        ("attn1", ("r", 0), ("kv", 0)),
                                        ("attn1", ("r", 0), ("ln", 0)), ("attn1", ("ln", 0), ("v", 0))):
                order((part, t - 2) + first, (part, t) + second)
    chains.append(zero_rows(0))
    order(("ffn1", 0, "z", E1 // 2 - 1), ("ffn1", 0, "c", 0))
    for g in range(GROUPS):
        chains += [ffn0_head(g), ffn0_gates(g), ffn0_up(g), ffn0_down(g), ffn1_head(g), ffn1_up(g), ffn1_down(g)]
        for t in (2 * g, 2 * g + 1):
            order(("attn0", t, "n", 0), ("ffn0", g, "v", 0))
            order(("ffn0", g, "y", 1), ("attn1", t, "v", 0))
            order(("attn1", t, "r", 0), ("ffn1", g, "v", 0))
        order(("ffn0", g, "r", 0), ("ffn0", g, "g", 0))
        order(("ffn0", g, "r", 0), ("ffn0", g, "u", 0))
        order(("ffn0", g, "g", 0), ("ffn0", g, "y", 0))
        order(("ffn1", g, "d", 0), ("ffn1", g, "c", 0))
        for part, n, first, second in (("ffn0", BLOCKS0, "u", "d"), ("ffn1", NCH1, "c", "w")):
            for i in range(n):
                order((part, g, first, i), (part, g, second, i))
                if i >= 2:
                    order((part, g, second, i - 2), (part, g, first, i))
        if g:
            order(("ffn0", g - 1, "u", BLOCKS0 - 1), ("ffn0", g, "x", 0))
            order(("ffn0", g - 1, "g", 0), ("ffn0", g, "r", 0))
            order(("ffn0", g - 1, "y", 1), ("ffn0", g, "g", 0))
            order(("ffn1", g - 1, "g", 0), ("ffn1", g, "t", 0))
            order(("ffn1", g - 1, "o", 1), ("ffn1", g, "d", 0))
    bodies = [("ffn0", 0)] + [x for g in range(GROUPS - 1) for x in (("ffn0", g + 1), ("ffn1", g))] + [("ffn1", GROUPS - 1)]
    ends = {"ffn0": (("u", 0), ("y", 1)), "ffn1": (("c", 0), ("o", 1))}
    for a, b in zip(bodies, bodies[1:]):
        order(a + ends[a[0]][1], b + ends[b[0]][0])
    return chains, after


def make_plan():
    chains, before = chains_and_orders()
    for c in chains:
        for a, b in zip(c, c[1:]):
            before.setdefault(b, []).append(a)
    follow = {}
    for s, firsts in before.items():
        for f in firsts:
            follow.setdefault(f, []).append(s)
    way = {}

    def way_to_end(s):
        if s not in way:
            cost = COST[s[0]][s[2]]
            way[s] = max([way_to_end(f) + (cost[0][1] if f[:3] == s[:3] else sum(d for _, d in cost))
                          for f in follow.get(s, [])], default=0.0)
        return way[s]

    def urgency(s):
        return way_to_end(s) + URGENCY[s[0] + "_body" * ((s[0], s[2]) in BODY)]

    free = dict.fromkeys(("pe", "act", "dve", "pool"), 0.0)
    rings = {b: [0.0] * n for b, n in BANKS.items()}
    finish, plan = {}, []

    def tried(s):
        now = dict(free)
        ready = max([finish[f] for f in before.get(s, []) if f[:3] != s[:3]] + [LOADED.get((s[0], s[2]), 0.0)])
        ring = FILLS.get((s[0], s[2]))
        start = None
        for eng, d in COST[s[0]][s[2]]:
            begin = max(now[eng], ready)
            if eng == "pe" and ring:
                begin = max(begin, rings[ring][-BANKS[ring]])
            if start is None or eng == "pe":
                start = begin
            now[eng] = begin + d
            ready = begin + d + HANDOFF
        return start, ready, now

    taken = {c[0]: 0 for c in chains}
    total = sum(len(c) for c in chains)
    head = None
    while len(plan) < total:
        gelus = [g for g in range(GROUPS) if ("ffn1", g, "c", 0) in finish and ("ffn1", g, "y", E1) not in finish]
        choices = []
        for c in chains:
            if taken[c[0]] == len(c):
                continue
            s = c[taken[c[0]]]
            if any(f not in finish for f in before.get(s, [])):
                continue
            if head and s[0][0] == "f" and s[2] == "v":
                continue
            if gelus and (s[0], s[2]) in EXPS and gelus[0] < GROUPS - 2:
                continue
            choices.append((s, c) + tried(s))
        now = max(free["pe"], min(x[2] for x in choices)) + SLACK
        s, c, _, ready, free = max((x for x in choices if x[2] <= now), key=lambda x: urgency(x[0]))
        plan.append(s)
        finish[s] = ready
        taken[c[0]] += 1
        if FILLS.get((s[0], s[2])):
            rings[FILLS[s[0], s[2]]].append(ready)
        if s[0][0] == "f" and s[2] in "vx":
            head = s if s[2] == "v" else None
    return plan


def mixed_network(nc: bass.Bass, x, ctx_in, ctxT, wr0, wf0, wp0, wq1, wkv1, wo1, down_w, down_b,
                  up_w, bias_rows, router_w, router_rows, core_w, w1, b1, w2, b2, out):
    ctx = ExitStack()
    with ctx:
        def sb(name, shape, dt):
            return ctx.enter_context(nc.sbuf_tensor(name, shape, dt))

        def ps(name, shape, dt):
            return ctx.enter_context(nc.psum_tensor(name, shape, dt))

        def sem(name):
            return ctx.enter_context(nc.semaphore(name))

        X = sb("X", [P, TILES, D], fp32)
        C = sb("C", [P, TILES, CTX], fp32)
        CT = sb("CT", [CTX, B * S], fp32)
        CD = sb("CD", [P, B, CTX], fp32)
        WR0 = sb("WR0", [P, DC, E0], fp32)
        WF0 = sb("WF0", [P, E0, DC, HID0], fp32)
        WP0 = sb("WP0", [P, E0, K0, D], fp32)
        WQ1 = sb("WQ1", [P, DC, D], fp32)
        WKV1 = sb("WKV1", [CTX, 2 * D], fp32)
        WO1 = sb("WO1", [P, DC, D], fp32)
        DW = sb("DW", [P, DC, L], fp32)
        DB = sb("DB", [P, 1], fp32)
        UW = sb("UW", [P, D], fp32)
        BR = sb("BR", [P, 2, D], fp32)
        RW = sb("RW", [P, DC, E1], fp32)
        RR = sb("RR", [P, 2, E1], fp32)
        CW = sb("CW", [P, DC, D], fp32)
        W1 = sb("W1", [P, NCH1, P], fp32)
        B1 = sb("B1", [P, NCH1], fp32)
        W2 = sb("W2", [P, NCH1, L], fp32)
        B2 = sb("B2", [P, E1 + 1], fp32)

        identf = sb("identf", [P, P], fp32)
        identb = sb("identb", [P, P], bf16)
        maskS = sb("maskS", [P, S], bf16)
        maskT = sb("maskT", [P, S], bf16)
        sel = sb("sel", [32, NH1, S], bf16)
        selG = sb("selG", [32, E1, P], bf16)
        iota8 = sb("iota8", [P, E1], fp32)
        mhalf = sb("mhalf", [P, 2], fp32)
        rbias = sb("rbias", [P, E1], fp32)
        GB1 = sb("GB1", [P, NCH1], fp32)
        Y0s = sb("Y0s", [P, E1], fp32)
        Y0n = sb("Y0n", [P, E1], fp32)
        Cb = sb("Cb", [P, 1], fp32)

        stats = sb("stats", [P, 4, 6], fp32)
        mv = sb("mv", [P, 4, 2], fp32)
        vare = sb("vare", [P, 4], fp32)
        rstd = sb("rstd", [P, 4], fp32)
        MN = sb("MN", [P, 4, NH0], fp32)
        rec = sb("rec", [P, 4, NH0], fp32)
        Q = sb("Q", [P, 2, D], fp32)
        QR = sb("QR", [P, 2, D], fp32)
        QS = sb("QS", [P, 2, NH0, 64], bf16)
        KR = sb("KR", [P, 2, CTX], fp32)
        KS = sb("KS", [P, 2, NKV0, 64], bf16)
        QT = sb("QT", [P, 2, NH0 // 2, P], bf16)
        K2 = sb("K2", [P, 2, NKV0, 2, 2, S], bf16)
        PT = sb("PT", [P, 2, NH0 // 2, P], fp32)
        V2 = sb("V2", [P, 2, 2, NKV0, 2, 16], fp32)
        OT = QT[:, :, 0:8, :].bitcast(fp32).rearrange("p t (a b) s -> p t a (b s)", b=2)
        O0 = QR
        XA = sb("XA", [P, 2, D], fp32)
        XAT = sb("XAT", [P, 2, DC, P], fp32)
        R1 = sb("R1", [P, 2, D], fp32)
        KQS = sb("KQS", [P, 2, NH1, SLOTS, HD1], bf16)
        V1 = sb("V1", [P, 2, NH1, 32], fp32)
        QT1_OT1 = sb("QT1_OT1", [P, 2, NH1, P], bf16)
        KT1 = sb("KT1", [SLOTS * HD1, 2, NH1, P], bf16)
        MS1 = sb("MS1", [P, 2, 2, NH1], bf16)
        MT1 = sb("MT1", [32, 2, P], bf16)
        PT1 = sb("PT1", [P, 2, NH1, S], fp32)
        QT1 = QT1_OT1[0:SLOTS * HD1, :, :, :]
        OT1 = QT1_OT1[:, :, 0:8, :].bitcast(fp32).rearrange("p t (a b) s -> p t a b s", b=2)
        O1 = XA
        O1T = R1[:, :, :].rearrange("p t (c r) -> p t c r", r=P)

        statsf = sb("statsf", [P, 2, 6], fp32)
        mvf = sb("mvf", [P, 2, 2], fp32)
        varef = sb("varef", [P, 2], fp32)
        rstdf = sb("rstdf", [P, 2], fp32)
        XN = sb("XN", [P, 2, D], fp32)
        XT0 = sb("XT0", [P, DC, GT], fp32)
        XT1 = sb("XT1", [P, DC, GT], fp32)
        lg = {part: sb(f"lg_{part}", [P, 2, E1], fp32) for part in ("ffn0", "ffn1")}
        pr = {part: sb(f"pr_{part}", [P, 2, E1], fp32) for part in ("ffn0", "ffn1")}
        lmax = {part: sb(f"lmax_{part}", [P, 2], fp32) for part in ("ffn0", "ffn1")}
        lsum = {part: sb(f"lsum_{part}", [P, 2], fp32) for part in ("ffn0", "ffn1")}
        G0 = sb("G0", [P, 2, E0], fp32)
        HH = sb("HH", [P, 2, 512], fp32)
        R0 = sb("R0", [P, 2, 512], fp32)
        A0 = sb("A0", [P, 2, 2, GT], fp32)
        top = sb("top", [P, 2, 8], fp32)
        topi = sb("topi", [P, 2, 8], u32)
        topf = sb("topf", [P, 2, 8], fp32)
        dlt = sb("dlt", [P, 2], fp32)
        ge = sb("ge", [P, 2], fp32)
        gk = sb("gk", [P, 2, 2], fp32)
        oh = sb("oh", [P, 2, E1], fp32)
        gate = sb("gate", [P, 2, E1], fp32)
        GR = sb("GR", [P, 2, E1], fp32)
        GS = sb("GS", [P, 2, 4, E1], bf16)
        GTT = sb("GTT", [32, GT], bf16)
        GX = sb("GX", [P, DC, GT], fp32)
        GH = sb("GH", [P, GT], fp32)
        A1, YS, YG = A0[:, :, 0, :], HH[:, :, 0:GT], R0[:, :, 0:GT]
        ACC = sb("ACC", [P, GT], fp32)

        bank = {n: [ps(f"{n}{i}", [P, 512], fp32) for i in range(k)] for n, k in BANKS.items()}

        plan = make_plan()

        BY_ACT = {("attn0", s) for s in "qpo"} | {("attn1", s) for s in "xqmpoa"}
        BY_ACT |= {("ffn0", "x"), ("ffn1", "x"), ("ffn1", "g"), ("ffn1", "d"), ("ffn1", "c")}
        READERS = ("act", "dve")
        full = {b: sem(f"{b}_full") for b in BANKS}
        free = {(b, r): sem(f"{b}_free_{r}") for b in BANKS for r in READERS}
        uses, order, reads = {}, {b: [] for b in BANKS}, dict.fromkeys(free, 0)
        for step in plan:
            b = FILLS.get((step[0], step[2]))
            if b:
                shared_expert = step[0] == "ffn1" and step[2] == "y" and step[3] == 0
                r = "act" if (step[0], step[2]) in BY_ACT or shared_expert else "dve"
                reads[b, r] += 1
                uses[step] = b, len(order[b]), free[b, r], reads[b, r]
                order[b].append(step)

        def at(*step):
            b, u, _, _ = uses[step]
            return bank[b][u % BANKS[b]]

        def read_out(eng, *step):
            _, _, done, n = uses[step]
            eng.wait_ge(done, n)

        def claim(eng, *step):
            b, u, _, _ = uses[step]
            if u >= BANKS[b]:
                read_out(eng, *order[b][u - BANKS[b]])
            return at(*step), full[b]

        def filled(eng, *step):
            b, u, done, _ = uses[step]
            eng.wait_ge(full[b], u + 1)
            return at(*step), done

        EXP0 = [x for x in plan if x[0] == "attn0" and x[2] == "e"]
        LN = [x for x in plan if x[2] == "v"]
        TURNS = [x for x in plan if x[0][0] == "f" and x[2] == "x"]
        LOGITS = [x for x in plan if x[0][0] == "f" and x[2] == "r"]
        ROUTES = [x for x in plan if (x[0], x[2]) in (("ffn0", "g"), ("ffn1", "e"))]
        ROUTED = {(x[0], x[1]): i + 1 for i, x in enumerate(ROUTES)}

        def block_used(eng, n):
            g, i = divmod(n, BLOCKS0)
            if i == BLOCKS0 - 1:
                filled(eng, "ffn0", g, "y", 1)
            else:
                eng.wait_ge(a0_used, g * (BLOCKS0 - 1) + i + 1)

        INNER = [k for k, (e, c) in enumerate(WORK) if c < CH1[e] - 1]

        def chunk_used(eng, n):
            g, i = divmod(n, NCH1)
            e, c = WORK[i]
            if i in INNER:
                eng.wait_ge(a1_used, g * len(INNER) + INNER.index(i) + 1)
            else:
                filled(eng, "ffn1", g, "y", EXPERTS.index(e))

        ld_x = [sem(f"ld_x{t}") for t in range(TILES)]
        ld_c = sem("ld_c")
        ld_cd = sem("ld_cd")
        ld_f0 = sem("ld_f0")
        ld_p0 = sem("ld_p0")
        ld_kv = sem("ld_kv")
        ld_qo = sem("ld_qo")
        ld_w1 = sem("ld_w1")
        ld_w2 = sem("ld_w2")
        ld_small = sem("ld_small")
        pool_const = sem("pool_const")
        v2_filled = sem("v2_filled")
        v2_ready = sem("v2_ready")
        var_ready = sem("var_ready")
        rstd_ready = sem("rstd_ready")
        qs_ready = sem("qs_ready")
        ks_ready = sem("ks_ready")
        exp_ready = sem("exp_ready")
        xa_ready = sem("xa_ready")
        kh_ready = sem("kh_ready")
        qs1_ready = sem("qs1_ready")
        ks1_ready = sem("ks1_ready")
        ms1_ready = sem("ms1_ready")
        xn_ready = sem("xn_ready")
        z_ready = sem("z_ready")
        e_ready = sem("e_ready")
        half_ready = sem("half_ready")
        a0_ready = sem("a0_ready")
        a0_used = sem("a0_used")
        a1_used = sem("a1_used")
        dlt_ready = sem("dlt_ready")
        ge_ready = sem("ge_ready")
        gs_ready = sem("gs_ready")
        gx_ready = sem("gx_ready")
        gb1_ready = sem("gb1_ready")
        ys_ready = sem("ys_ready")
        acc_ready = sem("acc_ready")
        stored = sem("stored")
        biased = sem("biased")
        dve_step = sem("dve_step")
        pool_step = sem("pool_step")

        def slot(part, t):
            return 2 * (part == "attn1") + t % 2

        def chain(eng, step):
            done = [0]

            def link(ins):
                done[0] += 1
                ins.then_inc(step, 1)
                eng.wait_ge(step, done[0])
            return link

        def run(handlers):
            for part, n, stage, i in plan:
                f = handlers.get((part, stage))
                if f:
                    f(n, i)

        def flat(ap):
            letters = "abcdefg"[:len(ap.shape) - 1]
            return ap.rearrange(f"p {' '.join(letters)} -> p ({' '.join(letters)})") if len(letters) > 1 else ap

        block = ctx.enter_context(nc.Block())
        SMALL = 9

        @block.sync
        def _(sp):
            def rows(t):
                sp.dma_start(X[:, t, :], x[t * P:(t + 1) * P, :]).then_inc(ld_x[t], 16)

            rows(0)
            sp.dma_start(C[:, :, :], ctx_in.rearrange("(t p) d -> p t d", p=P)).then_inc(ld_c, 16)
            rows(1)
            sp.dma_start(CT[:, :], ctxT).then_inc(ld_kv, 16)
            sp.dma_start(WKV1[:, :], wkv1).then_inc(ld_kv, 16)
            for half in range(2):
                sp.dma_start(CD[half * S:(half + 1) * S, :, :], ctx_in.rearrange("(b s) d -> s b d", s=S)
                             ).then_inc(ld_cd, 16)
            sp.dma_start(W2[:, :, :], w2).then_inc(ld_w2, 16)
            rows(2)
            rows(3)
            sp.dma_start(WR0[:, :, :], wr0).then_inc(ld_f0, 16)
            for e in range(E0):
                sp.dma_start(WF0[:, e, :, :], wf0[:, e, :, :]).then_inc(ld_f0, 16)
                sp.dma_start(WP0[:, e, :, :], wp0[:, e, :, :]).then_inc(ld_p0, 16)
            for t in range(4, TILES):
                rows(t)
            sp.dma_start(WQ1[:, :, :], wq1).then_inc(ld_qo, 16)
            sp.dma_start(WO1[:, :, :], wo1).then_inc(ld_qo, 16)
            sp.dma_start(W1[:, :, :], w1).then_inc(ld_w1, 16)
            for t in range(TILES):
                read_out(sp, "ffn1", t // 2, "o", t % 2)
                sp.dma_start(out[t * P:(t + 1) * P, :], X[:, t, :]).then_inc(stored, 16)
            sp.wait_ge(stored, 16 * TILES)

        @block.scalar
        def _(act):
            for dst, src in ((DW[:, :, :], down_w), (DB[:, :], down_b), (UW[:, :], up_w), (BR[:, :, :], bias_rows),
                             (RW[:, :, :], router_w), (RR[:, :, :], router_rows), (CW[:, :, :], core_w),
                             (B1[:, :], b1), (B2[:, :], b2)):
                act.dma_start(dst, src).then_inc(ld_small, 16)

            def evacuate(part, stage, dst, src):
                def f(n, i):
                    b, done = filled(act, part, n, stage, i)
                    nc.scalar.copy(dst(n, i), src(b, i)).then_inc(done, 1)
                return {(part, stage): f}

            def heads(b, rows, k):
                return b[:, :].bitcast(bf16)[0:rows, 0:k * P].rearrange("p (n c) -> p n c", c=P)

            h = {}
            h |= evacuate("attn0", "q", lambda t, i: QT[:, t % 2, 8 * i:8 * i + 8, :], lambda b, i: heads(b, P, 8))
            h |= evacuate("attn0", "p", lambda t, i: flat(PT[:, t % 2, 4 * i:4 * i + 4, :]), lambda b, i: b[:, :])
            h |= evacuate("attn0", "o", lambda t, i: flat(OT[:, t % 2, :, :]), lambda b, i: b[:, :])
            h |= evacuate("attn1", "x", lambda t, i: flat(XAT[:, t % 2, :, :]), lambda b, i: b[:, 0:D])
            h |= evacuate("attn1", "q", lambda t, i: QT1[:, t % 2, 8 * i:8 * i + 8, :], lambda b, i: heads(b, 96, 8))
            h |= evacuate("attn1", "m", lambda t, i: MT1[:, t % 2, :], lambda b, i: b[:, :].bitcast(bf16)[0:32, 0:P])
            h |= evacuate("attn1", "o", lambda t, i: OT1[:, t % 2, :, i, :],
                          lambda b, i: b[:, 0:256].rearrange("p (h s) -> p h s", s=S))
            h |= evacuate("attn1", "a", lambda t, i: flat(O1T[:, t % 2, :, :]), lambda b, i: b[:, 0:D])
            h |= evacuate("ffn0", "x", lambda g, i: flat(XT0[:, :, :]), lambda b, i: b[:, :])
            h |= evacuate("ffn1", "x", lambda g, i: flat(XT1[:, :, :]), lambda b, i: b[:, :])
            h |= evacuate("ffn1", "g", lambda g, i: GTT[:, :], lambda b, i: b[:, :].bitcast(bf16)[0:32, 0:GT])

            def values0(t):
                if t == 0:
                    act.wait_ge(ld_cd, 32)
                    act.wait_ge(v2_filled, 2)
                if t >= 2:
                    filled(act, "attn0", t - 2, "o", 0)
                for half in range(2):
                    rows = slice(half * S, (half + 1) * S)
                    nc.scalar.copy(V2[rows, t % 2, :, :, half, 0:HD0], CD[rows, 2 * t:2 * t + 2, :].rearrange(
                        "p b (k d) -> p b k d", d=HD0)).then_inc(v2_ready, 1)

            def exps0(t, c):
                read_out(act, "attn0", t, "s", c)
                e = flat(PT[:, t % 2, 4 * c:4 * c + 4, :])
                nc.scalar.activation(e, e, ACT.Exp, scale=HD0 ** -0.5).then_inc(exp_ready, 1)
                if c == 3:
                    values0(t)

            def probs1(t, c):
                b, done = filled(act, "attn1", t, "p", c)
                nc.scalar.activation(flat(PT1[:, t % 2, 8 * c:8 * c + 8, :]), b[:, :], ACT.Exp,
                                     scale=HD1 ** -0.5).then_inc(done, 1)

            def keys1(t, _):
                b, _ = filled(act, "attn1", t, "kv", 0)
                if t >= 2:
                    filled(act, "attn1", t - 2, "o", 1)
                key = b[:, 0:D].rearrange("p (h d) -> p h d", d=HD1)
                nc.scalar.copy(KQS[:, t % 2, :, 0, :], key).then_inc(kh_ready, 1)
                nc.scalar.copy(KQS[:, t % 2, :, 3, :], key).then_inc(kh_ready, 1)
                nc.scalar.copy(KQS[:, t % 2, :, 5, :], key).then_inc(kh_ready, 1)
                nc.scalar.copy(V1[:, t % 2, :, 0:HD1], b[:, D:2 * D].rearrange("p (h d) -> p h d", d=HD1)
                               ).then_inc(kh_ready, 1)

            def exps(which, e):
                def f(g, _):
                    act.wait_ge(z_ready, LOGITS.index((which, g, "r", 0)) + 1)
                    nc.scalar.activation(pr[which][:, :, 0:e], lg[which][:, :, 0:e], ACT.Exp).then_inc(e_ready, 1)
                return f

            def half(g, i):
                n = g * BLOCKS0 + i
                b, _ = filled(act, "ffn0", g, "u", i)
                if n >= 2:
                    read_out(act, "ffn0", (n - 2) // BLOCKS0, "u", (n - 2) % BLOCKS0)
                nc.scalar.activation(HH[:, n % 2, :], b[:, :], ACT.Copy, scale=0.5).then_inc(half_ready, 1)

            def top_exp(g, _):
                act.wait_ge(dlt_ready, g + 1)
                nc.scalar.activation(ge[:, :], dlt[:, :], ACT.Exp).then_inc(ge_ready, 1)

            def gelu_biases(g, _):
                act.wait_ge(ld_small, 16 * SMALL)
                nc.scalar.activation(GB1[:, :], B1[:, :], ACT.Gelu).then_inc(gb1_ready, 1)

            def inner(g, _):
                read_out(act, "ffn1", g, "x", 0)
                if g:
                    filled(act, "ffn1", g - 1, "o", 1)
                nc.scalar.activation(flat(GX[:, :, :]), flat(XT1[:, :, :]), ACT.Gelu).then_inc(gx_ready, 1)
                b, done = filled(act, "ffn1", g, "d", 0)
                nc.scalar.activation(GH[:, :], b[:, 0:GT], ACT.Gelu, bias=DB[:, :]).then_inc(done, 1)

            def hidden(g, i):
                e, c = WORK[i]
                n = g * NCH1 + i
                b, done = filled(act, "ffn1", g, "c", i)
                if n >= 2:
                    chunk_used(act, n - 2)
                ch = FIRST1[e] + c
                nc.scalar.activation(A1[:, n % 2, :], b[:, 0:GT], ACT.Gelu, bias=B1[:, ch:ch + 1]).then_inc(done, 1)

            def expert(g, j):
                b, done = filled(act, "ffn1", g, "y", j)
                if j == 0:
                    if g:
                        filled(act, "ffn1", g - 1, "o", 1)
                    nc.scalar.activation(ACC[:, :], b[:, 0:GT], ACT.Identity, bias=Cb[:, :], scale=0.1
                                         ).then_inc(done, 1)
                    return
                if j > 2:
                    read_out(act, "ffn1", g, "y", j - 2)
                e = EXPERTS[j]
                nc.scalar.activation(YS[:, j % 2, :], b[:, 0:GT], ACT.Identity, bias=Y0n[:, e:e + 1]
                                     ).then_inc(ys_ready, 1)

            run(h | {("attn0", "e"): exps0, ("attn1", "p"): probs1, ("attn1", "kv"): keys1,
                     ("ffn0", "g"): exps("ffn0", E0), ("ffn0", "u"): half, ("ffn1", "e"): exps("ffn1", E1),
                     ("ffn1", "t"): top_exp, ("ffn1", "b"): gelu_biases, ("ffn1", "d"): inner,
                     ("ffn1", "c"): hidden, ("ffn1", "y"): expert})

        @block.gpsimd
        def _(pool):
            link = chain(pool, pool_step)
            nc.gpsimd.memset(mhalf[:, :], -0.5)
            nc.gpsimd.memset(flat(KS[:, :, :, :]), 0.0)

            def identity(m):
                link(nc.gpsimd.memset(m[:, :], 0.0))
                return nc.gpsimd.affine_select(out=m[:, :], in_=m[:, :], compare_op=ALU.not_equal, fill=1.0, base=0,
                                               pattern=[[-1, P]], channel_multiplier=1)
            link(identity(identb))

            def norm(part):
                def f(n, _):
                    i = LN.index((part, n, "v", 0))
                    k = slot(part, n)
                    src, dst = (vare[:, k:k + 1], rstd[:, k:k + 1]) if part[0] == "a" else (varef[:, :], rstdf[:, :])
                    pool.wait_ge(var_ready, i + 1)
                    nc.gpsimd.tensor_tensor(dst, src, mhalf[:, 0:dst.shape[1]], ALU.pow).then_inc(rstd_ready, 1)
                return f

            def keys0(t, _):
                if t == 0:
                    pool.wait_ge(ld_c, 16)
                if t >= 2:
                    filled(pool, "attn0", t - 2, "k", 0)
                key = C[:, t, :].rearrange("p (k d) -> p k d", d=HD0)
                rest = KR[:, t % 2, :].rearrange("p (k d) -> p k d", d=HD0)

                def column(s):
                    return KS[:, t % 2, :, s * HD0:(s + 1) * HD0]
                link(nc.gpsimd.tensor_copy(column(0), key))
                link(nc.gpsimd.tensor_tensor(rest, key, column(0), ALU.subtract))
                nc.gpsimd.tensor_copy(column(3), key)
                nc.gpsimd.tensor_copy(column(5), key)
                link(nc.gpsimd.tensor_copy(column(1), rest))
                nc.gpsimd.tensor_copy(column(4), rest)
                nc.gpsimd.tensor_tensor(column(2), rest, column(1), ALU.subtract).then_inc(ks_ready, 1)

            def keys1(t, _):
                read_out(pool, "attn1", t, "kv", 0)
                rest = R1[:, t % 2, :].rearrange("p (h d) -> p h d", d=HD1)
                link(nc.gpsimd.tensor_scalar(KQS[:, t % 2, :, 1, :], rest, 1.0, 0.0, ALU.mult, ALU.add))
                nc.gpsimd.tensor_scalar(KQS[:, t % 2, :, 4, :], rest, 1.0, 0.0, ALU.mult, ALU.add)
                nc.gpsimd.tensor_tensor(KQS[:, t % 2, :, 2, :], rest, KQS[:, t % 2, :, 1, :], ALU.subtract
                                        ).then_inc(ks1_ready, 1)

            def biases(g, _):
                if g == 0:
                    pool.wait_ge(ld_small, 16 * SMALL)
                    link(nc.gpsimd.tensor_tensor(BR[:, 0, :], BR[:, 0, :], BR[:, 1, :], ALU.add))
                pool.wait_ge(xn_ready, 2 * TURNS.index(("ffn1", g, "x", 0)) + 2)
                for t in (2 * g, 2 * g + 1):
                    nc.gpsimd.tensor_tensor(X[:, t, :], X[:, t, :], BR[:, 0, :], ALU.add).then_inc(biased, 1)

            def square(g, i):
                n = g * BLOCKS0 + i
                read_out(pool, "ffn0", g, "u", i)
                if n >= 2:
                    block_used(pool, n - 2)
                nc.gpsimd.tensor_tensor(flat(A0[:, n % 2, :, :]), R0[:, n % 2, :], R0[:, n % 2, :], ALU.mult
                                        ).then_inc(a0_ready, 1)

            def first(t, i):
                norm("attn0")(t, i)
                keys0(t, i)
                if t != 1:
                    return
                link(nc.gpsimd.memset(flat(V2[:, :, :, :, :, :]), 0.0))
                for half in range(2):
                    ones = nc.gpsimd.memset(V2[half * S:(half + 1) * S, :, :, :, half, HD0:HD0 + 1].rearrange(
                        "p t b k c -> p (t b k) c"), 1.0)
                    ones.then_inc(v2_filled, 1)
                    pool.wait_ge(v2_filled, half + 1)
                link(identity(identf))
                for m in (maskS, maskT, sel):
                    nc.gpsimd.memset(flat(m[tuple(slice(None) for _ in m.shape)]), 0.0)
                link(nc.gpsimd.memset(selG[:, :, :], 0.0))
                for part in range(PARTS):
                    if part < 2:
                        link(nc.gpsimd.affine_select(out=sel[:, :, :], in_=sel[:, :, :], compare_op=ALU.not_equal,
                                                     fill=1.0, base=-NH1 * part, pattern=[[-1, NH1], [0, S]],
                                                     channel_multiplier=1))
                    link(nc.gpsimd.affine_select(out=selG[:, :, :], in_=selG[:, :, :], compare_op=ALU.not_equal,
                                                 fill=1.0, base=-E1 * part, pattern=[[-1, E1], [0, P]],
                                                 channel_multiplier=1))
                for b in range(2):
                    rows = slice(b * S, (b + 1) * S)
                    link(nc.gpsimd.affine_select(out=maskS[rows, :], in_=maskS[rows, :], compare_op=ALU.is_ge,
                                                 fill=MASKED, base=0, pattern=[[-1, S]], channel_multiplier=1))
                    link(nc.gpsimd.affine_select(out=maskT[rows, :], in_=maskT[rows, :], compare_op=ALU.is_ge,
                                                 fill=MASKED, base=0, pattern=[[1, S]], channel_multiplier=-1))
                nc.gpsimd.iota(iota8[:, :], pattern=[[1, E1]], base=0, channel_multiplier=0,
                               allow_small_or_imprecise_dtypes=True).then_inc(pool_const, 1)

            run({("attn0", "v"): first, ("attn1", "v"): norm("attn1"), ("ffn0", "v"): norm("ffn0"),
                 ("ffn1", "v"): norm("ffn1"), ("attn1", "kv"): keys1, ("ffn1", "d"): biases, ("ffn0", "u"): square})

        @block.vector
        def _(dve):
            link = chain(dve, dve_step)

            def setup():
                nc.vector.memset(V1[:, :, :, HD1 + 1:32], 0.0)
                nc.vector.memset(V1[:, :, :, HD1:HD1 + 1], 1.0)
                link(nc.vector.memset(GS[:, :, 3, :].bitcast(u32), 0))

            def variance(part):
                def f(n, _):
                    one = part[0] == "a"
                    tiles = [n] if one else [2 * n, 2 * n + 1]
                    if part == "attn0":
                        dve.wait_ge(ld_x[n], 16)
                    j = slot(part, n)
                    st = [stats[:, j, :]] if one else [statsf[:, k, :] for k in range(2)]
                    m = [mv[:, j, :]] if one else [mvf[:, k, :] for k in range(2)]
                    for k, t in enumerate(tiles):
                        link(nc.vector.bn_stats(st[k], X[:, t, :]))
                    for k, t in enumerate(tiles):
                        link(nc.vector.bn_aggr(m[k], st[k]))
                    src, dst = (mv[:, j:j + 1, 1], vare[:, j:j + 1]) if one else (mvf[:, :, 1], varef[:, :])
                    nc.vector.tensor_scalar(dst, src, EPS, None, ALU.add).then_inc(var_ready, 1)
                return f

            def normed(part, n, k, t, dst):
                j = slot(part, n)
                m, r = (mv[:, j, 0:1], rstd[:, j:j + 1]) if part[0] == "a" else (mvf[:, k, 0:1], rstdf[:, k:k + 1])
                return nc.vector.tensor_scalar(dst, X[:, t, :], m, r, ALU.subtract, ALU.mult)

            def wait_rstd(part, n):
                dve.wait_ge(rstd_ready, LN.index((part, n, "v", 0)) + 1)

            def queries0(t, _):
                wait_rstd("attn0", t)
                link(normed("attn0", t, 0, t, Q[:, t % 2, :]))
                if t >= 2:
                    filled(dve, "attn0", t - 2, "q", 1)
                q = Q[:, t % 2, :].rearrange("p (h d) -> p h d", d=HD0)
                rest = QR[:, t % 2, :].rearrange("p (h d) -> p h d", d=HD0)
                s = QS[:, t % 2, :, 0:SLOTS * HD0].rearrange("p h (s d) -> p h s d", d=HD0)
                link(nc.vector.tensor_copy(s[:, :, 0:3, :], q.unsqueeze(2).to_broadcast([P, NH0, 3, HD0])))
                link(nc.vector.tensor_tensor(rest, q, s[:, :, 0, :], ALU.subtract))
                link(nc.vector.tensor_copy(s[:, :, 3:5, :], rest.unsqueeze(2).to_broadcast([P, NH0, 2, HD0])))
                nc.vector.tensor_tensor(s[:, :, 5, :], rest, s[:, :, 3, :], ALU.subtract).then_inc(qs_ready, 1)

            def blocks0(t, _):
                b, done = filled(dve, "attn0", t, "k", 0)
                for half in range(2):
                    rows = slice(half * S, (half + 1) * S)
                    ins = nc.vector.tensor_copy(K2[rows, t % 2, :, :, half, :], b[:, :].bitcast(bf16)[rows, :].rearrange(
                        "p (k b t) -> p k b t", k=NKV0, b=2))
                    if half == 0:
                        link(ins)
                ins.then_inc(done, 1)

            def scores_less_max0(t, c):
                b, done = filled(dve, "attn0", t, "s", c)
                if t >= 2 and c == 0:
                    filled(dve, "attn0", t - 2, "o", 0)
                scores = b[:, :].rearrange("p (h t) -> p h t", t=S)
                least = MN[:, slot("attn0", t), 8 * c:8 * c + 8]
                link(nc.vector.tensor_reduce(least, scores, AX.X, ALU.max, negate=True))
                nc.vector.tensor_tensor(flat(PT[:, t % 2, 4 * c:4 * c + 4, :]).rearrange("p (h t) -> p h t", t=S), scores,
                                        least.unsqueeze(2).to_broadcast([P, 8, S]), ALU.add).then_inc(done, 1)

            def largest1(t, c):
                b, done = filled(dve, "attn1", t, "s", c)
                nc.vector.tensor_reduce(MN[:, slot("attn1", t), 8 * c:8 * c + 8],
                                        b[:, :].rearrange("p (h t) -> p h t", t=S), AX.X, ALU.max, negate=True
                                        ).then_inc(done, 1)

            def shifts1(t, _):
                read_out(dve, "attn1", t, "s", 1)
                m, s = MN[:, slot("attn1", t), 0:NH1], MS1[:, t % 2, :, :]
                link(nc.vector.tensor_copy(s[:, 0, :], m))
                nc.vector.tensor_tensor(s[:, 1, :], m, s[:, 0, :], ALU.subtract).then_inc(ms1_ready, 1)

            def result0(t, _):
                b, done = filled(dve, "attn0", t, "n", 0)
                N = b[:, :].rearrange("p (h x) -> p h x", x=16)
                link(nc.vector.reciprocal(rec[:, slot("attn0", t), :], N[:, :, HD0]))
                link(nc.vector.tensor_tensor(O0[:, t % 2, :].rearrange("p (h d) -> p h d", d=HD0), N[:, :, 0:HD0],
                                             rec[:, slot("attn0", t), :].unsqueeze(2).to_broadcast([P, NH0, HD0]), ALU.mult))
                for half in range(2):
                    xh = X[:, t, half * P:(half + 1) * P].rearrange("p (k g r) -> p g k r", k=4, g=2)
                    o = O0[:, t % 2, half * P:(half + 1) * P].rearrange("p (g k r) -> p g k r", k=4, g=2)
                    ins = nc.vector.tensor_tensor(xh, xh, o, ALU.add)
                    if half == 0:
                        link(ins)
                ins.then_inc(done, 1)
                read_out(dve, "attn0", t, "n", 0)

            def keys1(t, _):
                b, done = filled(dve, "attn1", t, "kv", 0)
                dve.wait_ge(kh_ready, 4 * t + 4)
                if t >= 2:
                    dve.wait_ge(ks1_ready, t - 1)
                nc.vector.tensor_tensor(R1[:, t % 2, :].rearrange("p (h d) -> p h d", d=HD1),
                                        b[:, 0:D].rearrange("p (h d) -> p h d", d=HD1), KQS[:, t % 2, :, 0, :],
                                        ALU.subtract).then_inc(done, 1)

            def rows1(t, _):
                wait_rstd("attn1", t)
                if t >= 2:
                    filled(dve, "attn1", t - 2, "x", 0)
                normed("attn1", t, 0, t, XA[:, t % 2, :]).then_inc(xa_ready, 1)

            def queries1(t, _):
                b, done = filled(dve, "attn1", t, "w", 0)
                filled(dve, "attn1", t, "k", 1)
                q = b[:, 0:D].rearrange("p (h d) -> p h d", d=HD1)
                rest = R1[:, t % 2, :].rearrange("p (h d) -> p h d", d=HD1)
                s = KQS[:, t % 2, :, :, :]
                link(nc.vector.tensor_copy(s[:, :, 0:3, :], q.unsqueeze(2).to_broadcast([P, NH1, 3, HD1])))
                nc.vector.tensor_tensor(rest, q, s[:, :, 0, :], ALU.subtract).then_inc(done, 1)
                read_out(dve, "attn1", t, "w", 0)
                link(nc.vector.tensor_copy(s[:, :, 3:5, :], rest.unsqueeze(2).to_broadcast([P, NH1, 2, HD1])))
                nc.vector.tensor_tensor(s[:, :, 5, :], rest, s[:, :, 3, :], ALU.subtract).then_inc(qs1_ready, 1)

            def turned_keys1(t, i):
                b, done = filled(dve, "attn1", t, "k", i)
                nc.vector.tensor_copy(KT1[:, t % 2, 8 * i:8 * i + 8, :],
                                      b[:, :].bitcast(bf16)[0:96, :].rearrange("p (n c) -> p n c", c=P)).then_inc(done, 1)

            def divide1(t, _):
                b, done = filled(dve, "attn1", t, "n", 0)
                N = b[:, :].rearrange("p (h x) -> p h x", x=32)
                link(nc.vector.reciprocal(rec[:, slot("attn1", t), 0:NH1], N[:, :, HD1]))
                nc.vector.tensor_tensor(O1[:, t % 2, :].rearrange("p (h d) -> p h d", d=HD1), N[:, :, 0:HD1],
                                        rec[:, slot("attn1", t), 0:NH1].unsqueeze(2).to_broadcast([P, NH1, HD1]), ALU.mult
                                        ).then_inc(done, 1)

            def result1(t, _):
                b, done = filled(dve, "attn1", t, "r", 0)
                nc.vector.tensor_tensor(X[:, t, :], b[:, 0:D], X[:, t, :], ALU.add).then_inc(done, 1)
                read_out(dve, "attn1", t, "r", 0)

            def rows(part):
                def f(g, _):
                    wait_rstd(part, g)
                    i = TURNS.index((part, g, "x", 0))
                    if i:
                        filled(dve, *TURNS[i - 1])
                    for k, t in enumerate((2 * g, 2 * g + 1)):
                        normed(part, g, k, t, XN[:, k, :]).then_inc(xn_ready, 1)
                return f

            def less_max(which, e):
                link(nc.vector.tensor_reduce(lmax[which][:, :], lg[which][:, :, 0:e], AX.X, ALU.max))
                nc.vector.tensor_tensor(lg[which][:, :, 0:e], lg[which][:, :, 0:e], lmax[which][:, :].unsqueeze(2).to_broadcast([P, 2, e]),
                                        ALU.subtract).then_inc(z_ready, 1)

            def softmax(which, g, e):
                dve.wait_ge(e_ready, ROUTED[which, g])
                link(nc.vector.tensor_reduce(lsum[which][:, :], pr[which][:, :, 0:e], AX.X, ALU.add))
                link(nc.vector.reciprocal(lsum[which][:, :], lsum[which][:, :]))
                link(nc.vector.tensor_tensor(pr[which][:, :, 0:e], pr[which][:, :, 0:e], lsum[which][:, :].unsqueeze(2).to_broadcast([P, 2, e]),
                                             ALU.mult))

            def logits0(g, _):
                b, done = filled(dve, "ffn0", g, "r", 0)
                nc.vector.tensor_copy(lg["ffn0"][:, :, 0:E0], b[:, 0:2 * E0].rearrange("p (t e) -> p t e", e=E0)).then_inc(done, 1)
                read_out(dve, "ffn0", g, "r", 0)
                less_max("ffn0", E0)

            def gates0(g, _):
                softmax("ffn0", g, E0)
                nc.vector.tensor_tensor(G0[:, :, 0], pr["ffn0"][:, :, 0], pr["ffn0"][:, :, 1], ALU.is_ge)
                link(nc.vector.tensor_tensor(G0[:, :, 1], pr["ffn0"][:, :, 1], pr["ffn0"][:, :, 0], ALU.is_gt))
                link(nc.vector.tensor_tensor(G0[:, :, :], G0[:, :, :], pr["ffn0"][:, :, 0:E0], ALU.mult))

            def leaky(g, i):
                n = g * BLOCKS0 + i
                dve.wait_ge(half_ready, n + 1)
                if n >= 2:
                    dve.wait_ge(a0_ready, n - 1)
                b, done = at("ffn0", g, "u", i), free["H", "dve"]
                nc.vector.tensor_tensor(R0[:, n % 2, :], b[:, :], HH[:, n % 2, :], ALU.max).then_inc(done, 1)

            def result_ffn0(g, k):
                t = 2 * g + k
                b, done = filled(dve, "ffn0", g, "y", k)
                link(nc.vector.scalar_tensor_tensor(X[:, t, :], b[:, 0:D], G0[:, k, 0:1], X[:, t, :], ALU.mult, ALU.add))
                nc.vector.scalar_tensor_tensor(X[:, t, :], b[:, D:2 * D], G0[:, k, 1:2], X[:, t, :], ALU.mult, ALU.add
                                               ).then_inc(done, 1)
                read_out(dve, "ffn0", g, "y", k)

            def logits1(g, _):
                if g == 0:
                    dve.wait_ge(ld_small, 16 * SMALL)
                    link(nc.vector.tensor_tensor(rbias[:, :], RR[:, 0, :], RR[:, 1, :], ALU.subtract))
                b, done = filled(dve, "ffn1", g, "r", 0)
                nc.vector.tensor_tensor(lg["ffn1"][:, :, :], b[:, 0:2 * E1].rearrange("p (t e) -> p t e", e=E1),
                                        rbias[:, :].unsqueeze(1).to_broadcast([P, 2, E1]), ALU.add).then_inc(done, 1)
                read_out(dve, "ffn1", g, "r", 0)
                less_max("ffn1", E1)

            def two_largest(g, _):
                softmax("ffn1", g, E1)
                if g == 0:
                    dve.wait_ge(pool_const, 1)
                for k in range(2):
                    link(nc.vector.max(top[:, k, :], pr["ffn1"][:, k, :]))
                nc.vector.tensor_tensor(dlt[:, :], top[:, :, 1], top[:, :, 0], ALU.subtract).then_inc(dlt_ready, 1)
                for k in range(2):
                    link(nc.vector.max_index(topi[:, k, :], top[:, k, :], pr["ffn1"][:, k, :]))
                link(nc.vector.tensor_copy(topf[:, :, :], topi[:, :, :]))

            def gates1(g, _):
                dve.wait_ge(ge_ready, g + 1)
                link(nc.vector.tensor_scalar(lsum["ffn1"][:, :], ge[:, :], 1.0, None, ALU.add))
                link(nc.vector.reciprocal(gk[:, :, 0], lsum["ffn1"][:, :]))
                link(nc.vector.tensor_tensor(gk[:, :, 1], gk[:, :, 0], ge[:, :], ALU.mult))
                for k in range(2):
                    nc.vector.tensor_scalar(oh[:, k, :], iota8[:, :], topf[:, k, 0:1], gk[:, k, 0:1],
                                            ALU.is_equal, ALU.mult)
                    second = nc.vector.tensor_scalar(gate[:, k, :], iota8[:, :], topf[:, k, 1:2], gk[:, k, 1:2],
                                                     ALU.is_equal, ALU.mult)
                link(second)
                link(nc.vector.tensor_tensor(gate[:, :, :], gate[:, :, :], oh[:, :, :], ALU.add))
                link(nc.vector.tensor_copy(GS[:, :, 0, :], gate[:, :, :]))
                link(nc.vector.tensor_tensor(GR[:, :, :], gate[:, :, :], GS[:, :, 0, :], ALU.subtract))
                link(nc.vector.tensor_copy(GS[:, :, 1, :], GR[:, :, :]))
                nc.vector.tensor_tensor(GS[:, :, 2, :], GR[:, :, :], GS[:, :, 1, :], ALU.subtract).then_inc(gs_ready, 1)

            def zero_row(g, i):
                b, done = filled(dve, "ffn1", g, "z", i)
                nc.vector.tensor_scalar(Y0n[:, 2 * i:2 * i + 2], b[:, 0:2], -1.0, None, ALU.mult).then_inc(done, 1)
                if i == E1 // 2 - 1:
                    total = lsum["ffn1"][:, 0:1]
                    read_out(dve, "ffn1", g, "z", i)
                    dve.wait_ge(ld_small, 16 * SMALL)
                    link(nc.vector.tensor_tensor(Y0s[:, :], B2[:, 0:E1], Y0n[:, :], ALU.subtract))
                    link(nc.vector.tensor_reduce(total, Y0s[:, :], AX.X, ALU.add))
                    link(nc.vector.scalar_tensor_tensor(Cb[:, :], B2[:, E1:E1 + 1], 0.1, total, ALU.mult, ALU.add))

            def expert(g, j):
                if j == 0:
                    read_out(dve, "ffn1", g, "y", 0)
                    return
                n = g * E1 + j
                dve.wait_ge(ys_ready, n)
                b = at("ffn1", g, "y", j)
                nc.vector.tensor_tensor(YG[:, j % 2, :], YS[:, j % 2, :], b[:, GT:2 * GT], ALU.mult
                                        ).then_inc(free["Y", "dve"], 1)
                read_out(dve, "ffn1", g, "y", j)
                add = nc.vector.tensor_tensor(ACC[:, :], ACC[:, :], YG[:, j % 2, :], ALU.add)
                if j < E1:
                    link(add)
                else:
                    add.then_inc(acc_ready, 1)

            def result_ffn1(g, k):
                dve.wait_ge(biased, 2 * g + k + 1)
                t = 2 * g + k
                b, done = filled(dve, "ffn1", g, "o", k)
                nc.vector.tensor_tensor(X[:, t, :], b[:, 0:D], X[:, t, :], ALU.add).then_inc(done, 1)

            var0 = variance("attn0")

            def first(t, i):
                if t == 0:
                    nc.vector.memset(QS[:, :, :, SLOTS * HD0:64], 0.0)
                    for half in range(2):
                        link(nc.vector.memset(K2[half * S:(half + 1) * S, :, :, :, 1 - half, :], 0.0))
                var0(t, i)

            def first_queries(t, i):
                queries0(t, i)
                if t == 1:
                    setup()

            run({("attn0", "v"): first, ("attn0", "ln"): first_queries, ("attn0", "k"): blocks0,
                 ("attn0", "s"): scores_less_max0, ("attn0", "n"): result0,
                 ("attn1", "v"): variance("attn1"), ("attn1", "kv"): keys1, ("attn1", "ln"): rows1,
                 ("attn1", "w"): queries1, ("attn1", "k"): turned_keys1, ("attn1", "s"): largest1,
                 ("attn1", "m"): shifts1, ("attn1", "n"): divide1, ("attn1", "r"): result1,
                 ("ffn0", "v"): variance("ffn0"), ("ffn0", "ln"): rows("ffn0"), ("ffn0", "r"): logits0,
                 ("ffn0", "g"): gates0, ("ffn0", "u"): leaky, ("ffn0", "y"): result_ffn0,
                 ("ffn1", "v"): variance("ffn1"), ("ffn1", "ln"): rows("ffn1"), ("ffn1", "r"): logits1,
                 ("ffn1", "e"): two_largest, ("ffn1", "t"): gates1, ("ffn1", "z"): zero_row,
                 ("ffn1", "y"): expert, ("ffn1", "o"): result_ffn1})

        @block.tensor
        def _(pe):
            def mm(o, a, b, start=True, stop=True, shared=False):
                return nc.tensor.matmul(o, a, b, start=start, stop=stop, skip_group_check=shared)

            def turn_queries0(t, i):
                b, done = claim(pe, "attn0", t, "q", i)
                if i == 0:
                    pe.wait_ge(qs_ready, t + 1)
                for p in range(8):
                    pair_ = 8 * i + p
                    ins = nc.tensor.transpose(b[:, :].bitcast(bf16)[:, p * P:(p + 1) * P],
                                              flat(QS[:, t % 2, 2 * pair_:2 * pair_ + 2, :]), identb[:, :])
                ins.then_inc(done, 1)

            def turn_keys0(t, _):
                b, done = claim(pe, "attn0", t, "k", 0)
                pe.wait_ge(ks_ready, t + 1)
                for kv in range(NKV0):
                    for half in range(2):
                        ins = nc.tensor.transpose(b[:, :].bitcast(bf16)[half * S:(half + 1) * S, kv * P:(kv + 1) * P],
                                                  KS[:, t % 2, kv, :], identb[:, :])
                ins.then_inc(done, 1)

            def scores0(t, c):
                b, done = claim(pe, "attn0", t, "s", c)
                if c == 0:
                    read_out(pe, "attn0", t, "k", 0)
                read_out(pe, "attn0", t, "q", c // 2)
                for i in range(4):
                    pair_ = 4 * c + i
                    for bt in range(2):
                        ins = mm(b[bt * S:(bt + 1) * S, i * P:(i + 1) * P], QT[:, t % 2, pair_, bt * S:(bt + 1) * S],
                                 flat(K2[:, t % 2, pair_ // 2, bt, :, :]))
                ins.then_inc(done, 1)

            def turn_probs0(t, c):
                b, done = claim(pe, "attn0", t, "p", c)
                pe.wait_ge(exp_ready, EXP0.index(("attn0", t, "e", c)) + 1)
                if t == 0 and c == 0:
                    pe.wait_ge(pool_const, 1)
                for i in range(4):
                    ins = nc.tensor.transpose(b[:, i * P:(i + 1) * P], PT[:, t % 2, 4 * c + i, :], identf[:, :])
                ins.then_inc(done, 1)

            def values0(t, _):
                b, done = claim(pe, "attn0", t, "o", 0)
                pe.wait_ge(v2_ready, 2 * t + 2)
                read_out(pe, "attn0", t, "p", 3)
                o = b[:, :].rearrange("p (h g b s) -> p h g b s", h=2, g=2, b=2)
                for kh in range(2):
                    for bt in range(2):
                        for k4 in range(4):
                            kv = 4 * kh + k4
                            ins = mm(o[32 * k4:32 * k4 + 32, kh, :, bt, :], flat(V2[:, t % 2, bt, kv, :, :]),
                                     PT[:, t % 2, 2 * kv:2 * kv + 2, bt * S:(bt + 1) * S])
                ins.then_inc(done, 1)

            def turn_back(part, src):
                def f(t, _):
                    b, done = claim(pe, part, t, "n", 0)
                    read_out(pe, part, t, "o", 0 if part == "attn0" else 1)
                    for i in range(4):
                        o = src[:, t % 2, i]
                        o = o if len(o.shape) == 2 else flat(o)
                        ins = nc.tensor.transpose(b[:, i * P:(i + 1) * P], o, identf[:, :])
                    ins.then_inc(done, 1)
                return f

            def turn_two(stage, src, wait):
                def f(t, _):
                    b, done = claim(pe, "attn1", t, stage, 0)
                    wait(t)
                    for dc in range(DC):
                        ins = nc.tensor.transpose(b[:, dc * P:(dc + 1) * P], src[:, t % 2, dc * P:(dc + 1) * P], identf[:, :])
                    ins.then_inc(done, 1)
                return f

            def project(stage, src, w, before):
                def f(t, _):
                    b, done = claim(pe, "attn1", t, stage, 0)
                    read_out(pe, "attn1", t, before, 0)
                    if t == 0:
                        pe.wait_ge(ld_qo, 16 * 2)
                    for dc in range(DC):
                        ins = mm(b[:, 0:D], src[:, t % 2, dc, :], w[:, dc, :], start=(dc == 0), stop=(dc == DC - 1))
                    ins.then_inc(done, 1)
                return f

            def keys_values1(t, _):
                b, done = claim(pe, "attn1", t, "kv", 0)
                if t == 0:
                    pe.wait_ge(ld_kv, 16 * 2)
                mm(b[:, :], CT[:, t * P:(t + 1) * P], WKV1[:, :]).then_inc(done, 1)

            def turn_heads1(stage, src, ready):
                def f(t, i):
                    b, done = claim(pe, "attn1", t, stage, i)
                    if i == 0:
                        pe.wait_ge(ready, t + 1)
                    for h in range(8):
                        ins = nc.tensor.transpose(b[:, :].bitcast(bf16)[0:96, h * P:(h + 1) * P],
                                                  flat(src[:, t % 2, 8 * i + h, :, :]), identb[:, :])
                    ins.then_inc(done, 1)
                return f

            def scores1(t, c):
                b, done = claim(pe, "attn1", t, "s", c)
                read_out(pe, "attn1", t, "k", c)
                read_out(pe, "attn1", t, "q", c)
                mm(b[:, :], identb[:, :], maskS[:, :].unsqueeze(1).to_broadcast([P, 8, S]), stop=False, shared=True)
                for h in range(8):
                    for bt in range(2):
                        rows = slice(bt * S, (bt + 1) * S)
                        ins = mm(b[rows, h * S:(h + 1) * S], QT1[:, t % 2, 8 * c + h, rows], KT1[:, t % 2, 8 * c + h, rows],
                                 start=False, shared=True)
                ins.then_inc(done, 1)

            def turn_shifts1(t, _):
                b, done = claim(pe, "attn1", t, "m", 0)
                pe.wait_ge(ms1_ready, t + 1)
                nc.tensor.transpose(b[:, :].bitcast(bf16)[0:32, 0:P], flat(MS1[:, t % 2, :, :]), identb[:, :]
                                    ).then_inc(done, 1)

            def probs1(t, c):
                b, done = claim(pe, "attn1", t, "p", c)
                if c == 0:
                    read_out(pe, "attn1", t, "m", 0)
                mm(b[:, :], identb[:, :], maskT[:, :].unsqueeze(1).to_broadcast([P, 8, S]), stop=False, shared=True)
                for h in range(8):
                    for bt in range(2):
                        rows = slice(bt * S, (bt + 1) * S)
                        o = b[rows, h * S:(h + 1) * S]
                        mm(o, sel[:, 8 * c + h, :], MT1[:, t % 2, rows], start=False, shared=True)
                        ins = mm(o, KT1[:, t % 2, 8 * c + h, rows], QT1[:, t % 2, 8 * c + h, rows], start=False, shared=True)
                ins.then_inc(done, 1)

            def values1(t, bt):
                b, done = claim(pe, "attn1", t, "o", bt)
                if bt == 0:
                    read_out(pe, "attn1", t, "p", 1)
                rows = slice(bt * S, (bt + 1) * S)
                for hq in range(4):
                    for h4 in range(4):
                        h = 4 * hq + h4
                        ins = mm(b[32 * h4:32 * h4 + 32, hq * S:(hq + 1) * S], V1[rows, t % 2, h, :], PT1[rows, t % 2, h, :])
                ins.then_inc(done, 1)

            def turn_rows(part):
                def f(g, _):
                    b, done = claim(pe, part, g, "x", 0)
                    i = TURNS.index((part, g, "x", 0))
                    for k in range(2):
                        pe.wait_ge(xn_ready, 2 * i + k + 1)
                        for dc in range(DC):
                            ins = nc.tensor.transpose(b[:, dc * GT + k * P:dc * GT + (k + 1) * P],
                                                      XN[:, k, dc * P:(dc + 1) * P], identf[:, :])
                    ins.then_inc(done, 1)
                return f

            def route(part, xt, w, e):
                def f(g, _):
                    b, done = claim(pe, part, g, "r", 0)
                    read_out(pe, part, g, "x", 0)
                    if g == 0:
                        pe.wait_ge(*((ld_f0, 16 * 3) if part == "ffn0" else (ld_small, 16 * SMALL)))
                    for k in range(2):
                        for dc in range(DC):
                            ins = mm(b[:, k * e:(k + 1) * e], xt[:, dc, k * P:(k + 1) * P], w[:, dc, :],
                                     start=(dc == 0), stop=(dc == DC - 1))
                    ins.then_inc(done, 1)
                return f

            def up0(g, i):
                b, done = claim(pe, "ffn0", g, "u", i)
                e, c0 = divmod(2 * i, K0)
                for c in range(2):
                    for dc in range(DC):
                        ins = mm(b[:, c * GT:(c + 1) * GT], WF0[:, e, dc, (c0 + c) * P:(c0 + c + 1) * P], XT0[:, dc, :],
                                 start=(dc == 0), stop=(dc == DC - 1))
                ins.then_inc(done, 1)

            def down0(g, i):
                n = g * BLOCKS0 + i
                e, c0 = divmod(2 * i, K0)
                if i == 0:
                    for k in range(2):
                        claim(pe, "ffn0", g, "y", k)
                    if g == 0:
                        pe.wait_ge(ld_p0, 16 * 2)
                pe.wait_ge(a0_ready, n + 1)
                for k in range(2):
                    for c in range(2):
                        ins = mm(at("ffn0", g, "y", k)[:, e * D:(e + 1) * D], A0[:, n % 2, c, k * P:(k + 1) * P],
                                 WP0[:, e, c0 + c, :], start=(c0 + c == 0), stop=(c0 + c == K0 - 1))
                    if i == BLOCKS0 - 1:
                        ins.then_inc(full["Y"], 1)
                if i < BLOCKS0 - 1:
                    ins.then_inc(a0_used, 1)

            def turn_gates(g, _):
                b, done = claim(pe, "ffn1", g, "g", 0)
                pe.wait_ge(gs_ready, g + 1)
                for k in range(2):
                    ins = nc.tensor.transpose(b[:, :].bitcast(bf16)[0:32, k * P:(k + 1) * P], flat(GS[:, k, :, :]),
                                              identb[:, :])
                ins.then_inc(done, 1)

            def narrow(g, _):
                b, done = claim(pe, "ffn1", g, "d", 0)
                for dc in range(DC):
                    ins = mm(b[:, 0:GT], DW[:, dc, :], XT1[:, dc, :], start=(dc == 0), stop=(dc == DC - 1))
                ins.then_inc(done, 1)

            def zero_row(g, i):
                b, done = claim(pe, "ffn1", g, "z", i)
                if i == 0:
                    pe.wait_ge(ld_w2, 16)
                    pe.wait_ge(gb1_ready, 1)
                for e in (2 * i, 2 * i + 1):
                    for c in range(CH1[e]):
                        ch = FIRST1[e] + c
                        ins = mm(b[:, e % 2:e % 2 + 1], W2[:, ch, :], GB1[:, ch:ch + 1], start=(c == 0), stop=(c == CH1[e] - 1))
                ins.then_inc(done, 1)

            def up1(g, i):
                e, c = WORK[i]
                b, done = claim(pe, "ffn1", g, "c", i)
                if i == 0:
                    read_out(pe, "ffn1", g, "d", 0)
                    if g == 0:
                        pe.wait_ge(ld_w1, 16)
                mm(b[:, 0:GT], W1[:, FIRST1[e] + c, :], GH[:, :]).then_inc(done, 1)

            def down1(g, i):
                e, c = WORK[i]
                y = ("ffn1", g, "y", EXPERTS.index(e))
                read_out(pe, "ffn1", g, "c", i)
                if c == 0:
                    b, _ = claim(pe, *y)
                    if e == EXPERTS[1]:
                        read_out(pe, "ffn1", g, "g", 0)
                    if e < E1:
                        mm(b[:, GT:2 * GT], selG[:, e, :], GTT[:, :])
                last_c = c == CH1[e] - 1
                ins = mm(at(*y)[:, 0:GT], W2[:, FIRST1[e] + c, :], A1[:, (g * NCH1 + i) % 2, :], start=(c == 0), stop=last_c)
                ins.then_inc(full["Y"] if last_c else a1_used, 1)

            def widen(g, k):
                b, done = claim(pe, "ffn1", g, "o", k)
                if k == 0:
                    pe.wait_ge(gx_ready, g + 1)
                for dc in range(DC):
                    mm(b[:, 0:D], GX[:, dc, k * P:(k + 1) * P], CW[:, dc, :], start=(dc == 0), stop=False)
                if k == 0:
                    pe.wait_ge(acc_ready, g + 1)
                mm(b[:, 0:D], ACC[:, k * P:(k + 1) * P], UW[:, :], start=False).then_inc(done, 1)

            pe.wait_ge(pool_step, 2)
            run({("attn0", "q"): turn_queries0, ("attn0", "k"): turn_keys0, ("attn0", "s"): scores0,
                 ("attn0", "p"): turn_probs0, ("attn0", "o"): values0,
                 ("attn0", "n"): turn_back("attn0", OT),
                 ("attn1", "kv"): keys_values1, ("attn1", "x"): turn_two("x", XA, lambda t: pe.wait_ge(xa_ready, t + 1)),
                 ("attn1", "w"): project("w", XAT, WQ1, "x"), ("attn1", "q"): turn_heads1("q", KQS, qs1_ready),
                 ("attn1", "k"): turn_heads1("k", KQS, ks1_ready), ("attn1", "s"): scores1,
                 ("attn1", "m"): turn_shifts1, ("attn1", "p"): probs1, ("attn1", "o"): values1,
                 ("attn1", "n"): turn_back("attn1", OT1),
                 ("attn1", "a"): turn_two("a", O1, lambda t: read_out(pe, "attn1", t, "n", 0)),
                 ("attn1", "r"): project("r", O1T, WO1, "a"),
                 ("ffn0", "x"): turn_rows("ffn0"), ("ffn0", "r"): route("ffn0", XT0, WR0, E0), ("ffn0", "u"): up0,
                 ("ffn0", "d"): down0, ("ffn1", "x"): turn_rows("ffn1"), ("ffn1", "r"): route("ffn1", XT1, RW, E1),
                 ("ffn1", "g"): turn_gates, ("ffn1", "d"): narrow, ("ffn1", "z"): zero_row, ("ffn1", "c"): up1,
                 ("ffn1", "w"): down1, ("ffn1", "o"): widen})


COST_LAMBDA = 1e-07


def kernel(**inputs):
    import numpy as np
    import concourse.bacc as bacc
    from concourse.bass_utils import run_bass_kernel_spmd as run

    a = {n: np.asarray(v) for n, v in inputs.items()}

    def chunks(w):
        return w.reshape(-1, P, w.shape[1]).transpose(1, 0, 2)

    f = "L1_ffn_"
    names = [f"{f}e{e}_" for e in range(E1)] + [f + "shared_"]
    cost = np.array([2 * L * h for h in HIDS], np.float32) * np.float32(COST_LAMBDA)
    arrays = {
        "x": a["x"].reshape(B * S, D),
        "ctx_in": a["ctx_512"].reshape(B * S, CTX),
        "ctxT": a["ctx_512"].reshape(B * S, CTX).T,
        "wr0": chunks(a["L0_ffn_w_router"].T),
        "wf0": a["L0_ffn_w_fc"].reshape(E0, HID0, DC, P).transpose(3, 0, 2, 1),
        "wp0": a["L0_ffn_w_proj"].reshape(E0, D, K0, P).transpose(3, 0, 2, 1),
        "wq1": chunks(a["L1_xattn_Wq"].T),
        "wkv1": a["L1_xattn_Wkv_expand"].T,
        "wo1": chunks(a["L1_xattn_Wout"].T),
        "down_w": chunks(a[f + "down_w"]),
        "down_b": a[f + "down_b"].reshape(L, 1),
        "up_w": a[f + "up_w"],
        "bias_rows": np.broadcast_to(np.stack([a[f + "up_b"], a[f + "core_b"]]), (P, 2, D)),
        "router_w": chunks(a[f + "router_w"]),
        "router_rows": np.broadcast_to(np.stack([a[f + "router_b"], cost]), (P, 2, E1)),
        "core_w": chunks(a[f + "core_w"]),
        "w1": np.concatenate([a[n + ("w1")] for n in names], 1).reshape(L, NCH1, P),
        "b1": np.concatenate([a[n + "b1"] for n in names]).reshape(NCH1, P).T,
        "w2": chunks(np.concatenate([a[n + "w2"] for n in names], 0)),
        "b2": np.stack([a[n + "b2"] for n in names], 1),
    }
    nc = bacc.Bacc("TRN2", target_bir_lowering=False, num_devices=1)
    feed, args = {}, []
    for name, v in arrays.items():
        v = np.ascontiguousarray(v)
        feed[f"in_{name}"] = v
        args.append(nc.dram_tensor(f"in_{name}", v.shape, mybir.dt.from_np(v.dtype), kind="ExternalInput").ap())
    args.append(nc.dram_tensor("out_dram", (B * S, D), fp32, kind="ExternalOutput").ap())
    mixed_network(nc, *args)
    r = run(nc, [feed], core_ids=[0])
    return r.results[0]["out_dram"].reshape(B, S, D)
```
